# Optimizing a Trainium2 kernel written in Bass

```python
import numpy as np
import jax
import jax.numpy as jnp

def _softmax(x, axis=-1):
    return jax.nn.softmax(x, axis=axis)

def _gelu(x):
    return jax.nn.gelu(x, approximate=True)

def _silu(x):
    return jax.nn.silu(x)

def _sigmoid(x):
    return jax.nn.sigmoid(x)

def _layernorm(x, axis=-1, eps=1e-05):
    m = jnp.mean(x, axis=axis, keepdims=True)
    v = jnp.var(x, axis=axis, keepdims=True)
    return (x - m) / jnp.sqrt(v + eps)

def _scatter_add(tgt, idx, src, axis=0):
    return tgt.at[idx].add(src)

def _segment_sum(src, seg, n):
    return jax.ops.segment_sum(src, seg, n)
kernel_name = 'mk_gnn_resnorm_d2_gnn_r8_b25b8c'

def setup_inputs(seed: int=0):
    np.random.seed(seed)
    _w = jnp.asarray

    def _rec_inputs():
        import jax
        import jax.numpy as jnp
        _gk = jax.random.key(seed)
        x = -0.000202 + 1 * jax.random.normal(jax.random.fold_in(_gk, 1), (6250, 128), jnp.float32)
        _s = jax.random.randint(jax.random.fold_in(_gk, 2), (100000,), 0, 6250, jnp.int32)
        _d = jax.random.randint(jax.random.fold_in(_gk, 3), (100000,), 0, 6250, jnp.int32)
        _loop = jnp.arange(6250, dtype=jnp.int32)
        src = jnp.concatenate([_s, _d, _loop])
        dst = jnp.concatenate([_d, _s, _loop])
        _o = jnp.argsort(dst, stable=True)
        src = src[_o]
        dst = dst[_o]
        edge_attr_64 = 0.000155561 + 1.00019 * jax.random.normal(jax.random.fold_in(_gk, 11), (206250, 64), jnp.float32)
        edge_weight = jax.random.uniform(jax.random.fold_in(_gk, 13), (206250,), jnp.float32, 0.0, 0.999998)
        return (x, src, dst, edge_attr_64, edge_weight)
    x, src, dst, edge_attr_64, edge_weight = _rec_inputs()

    def _L0_gnn_setup():
        import jax, jax.numpy as jnp
        import numpy as np
        N = 6250
        E = 75000
        D = 128
        L = 3
        BN_EPS = 1e-05

        def _bn(x, g, b):
            m = jnp.mean(x, axis=0)
            v = jnp.var(x, axis=0)
            return (x - m) * jax.lax.rsqrt(v + BN_EPS) * g + b
        key = jax.random.key(seed)
        ks = jax.random.split(key, 5)
        h = jax.random.normal(ks[0], (N, D), jnp.float32)
        edges = jax.random.randint(ks[1], (2, E), 0, N, dtype=jnp.int32)
        w = jax.random.uniform(ks[2], (E,), jnp.float32)
        scale = 1.0 / np.sqrt(D)
        W0s = jax.random.normal(ks[3], (L, D, D), jnp.float32) * scale
        W1s = jax.random.normal(ks[4], (L, D, D), jnp.float32) * scale
        ones = jnp.ones((L, D), jnp.float32)
        zeros = jnp.zeros((L, D), jnp.float32)
        return dict(h=h, edges=edges, w=w, W0s=W0s, W1s=W1s, bn1_g=ones, bn1_b=zeros, bn2_g=ones, bn2_b=zeros, bn3_g=ones, bn3_b=zeros)
    _L0_gnn_all = _L0_gnn_setup()
    _L0_gnn_in = {k: v for k, v in _L0_gnn_all.items() if k in ('W0s', 'W1s', 'bn1_g', 'bn1_b', 'bn2_g', 'bn2_b', 'bn3_g', 'bn3_b')}
    del _L0_gnn_all

    def _L1_gnn_setup():
        import jax, jax.numpy as jnp
        import numpy as np
        N_NODES, N_EDGES = (6250, 75000)
        NODE_DIM, EDGE_DIM = (128, 64)
        H, HD = (4, 32)
        key = jax.random.key(seed)
        k = jax.random.split(key, 6)
        node_features = jax.random.normal(k[0], (N_NODES, NODE_DIM), jnp.float32)
        edge_indices = jax.random.randint(k[1], (2, N_EDGES), 0, N_NODES, jnp.int32)
        edge_features = jax.random.normal(k[2], (N_EDGES, EDGE_DIM), jnp.float32)
        W_node = jax.random.normal(k[3], (H * HD, NODE_DIM), jnp.float32) / np.sqrt(NODE_DIM).astype(np.float32)
        W_edge = jax.random.normal(k[4], (H * HD, EDGE_DIM), jnp.float32) / np.sqrt(EDGE_DIM).astype(np.float32)
        a = jax.random.normal(k[5], (H, 3 * HD), jnp.float32)
        return {'node_features': node_features, 'edge_indices': edge_indices, 'edge_features': edge_features, 'W_node': W_node, 'W_edge': W_edge, 'a': a}
    _L1_gnn_all = _L1_gnn_setup()
    _L1_gnn_in = {k: v for k, v in _L1_gnn_all.items() if k in ('W_node', 'W_edge', 'a')}
    del _L1_gnn_all
    return {'x': x, 'src': src, 'dst': dst, 'edge_attr_64': edge_attr_64, 'edge_weight': edge_weight, 'L0_gnn_W0s': _L0_gnn_in['W0s'], 'L0_gnn_W1s': _L0_gnn_in['W1s'], 'L0_gnn_bn1_g': _L0_gnn_in['bn1_g'], 'L0_gnn_bn1_b': _L0_gnn_in['bn1_b'], 'L0_gnn_bn2_g': _L0_gnn_in['bn2_g'], 'L0_gnn_bn2_b': _L0_gnn_in['bn2_b'], 'L0_gnn_bn3_g': _L0_gnn_in['bn3_g'], 'L0_gnn_bn3_b': _L0_gnn_in['bn3_b'], 'L1_gnn_W_node': _L1_gnn_in['W_node'], 'L1_gnn_W_edge': _L1_gnn_in['W_edge'], 'L1_gnn_a': _L1_gnn_in['a']}

def reference(x, src, dst, edge_attr_64, edge_weight, L0_gnn_W0s, L0_gnn_W1s, L0_gnn_bn1_g, L0_gnn_bn1_b, L0_gnn_bn2_g, L0_gnn_bn2_b, L0_gnn_bn3_g, L0_gnn_bn3_b, L1_gnn_W_node, L1_gnn_W_edge, L1_gnn_a):
    import jax
    import jax.numpy as jnp

    def _L0_gnn_ref(h, edges, w, W0s, W1s, bn1_g, bn1_b, bn2_g, bn2_b, bn3_g, bn3_b):
        import jax, jax.numpy as jnp
        import numpy as np
        N = 6250
        E = 75000
        D = 128
        L = 3
        BN_EPS = 1e-05

        def _bn(x, g, b):
            m = jnp.mean(x, axis=0)
            v = jnp.var(x, axis=0)
            return (x - m) * jax.lax.rsqrt(v + BN_EPS) * g + b
        src, dst = (edges[0], edges[1])
        for i in range(L):
            agg = jax.ops.segment_sum(h[src] * w[:, None], dst, num_segments=N)
            x = h + agg
            x = jax.nn.relu(_bn(x @ W0s[i], bn1_g[i], bn1_b[i]))
            x = x @ W1s[i]
            x = jax.nn.relu(_bn(x, bn2_g[i], bn2_b[i]))
            h = _bn(x, bn3_g[i], bn3_b[i])
            if i != L - 1:
                h = jax.nn.relu(h)
        return h

    def _L1_gnn_ref(node_features, edge_indices, edge_features, W_node, W_edge, a):
        import jax, jax.numpy as jnp
        import numpy as np
        N_NODES, N_EDGES = (6250, 75000)
        NODE_DIM, EDGE_DIM = (128, 64)
        H, HD = (4, 32)
        num_nodes = node_features.shape[0]
        num_edges = edge_indices.shape[1]
        h = (node_features @ W_node.T).reshape(num_nodes, H, HD)
        e = (edge_features @ W_edge.T).reshape(num_edges, H, HD)
        src, tgt = (edge_indices[0], edge_indices[1])
        h_src = h[src]
        h_tgt = h[tgt]
        att_in = jnp.concatenate([h_src, h_tgt, e], axis=-1)
        att = jnp.sum(att_in * a, axis=-1)
        att = jnp.where(att > 0, att, 0.2 * att)
        m = jnp.maximum(jax.ops.segment_max(att, tgt, num_segments=num_nodes), 0.0)
        ex = jnp.exp(att - m[tgt])
        ones = jnp.ones((num_edges,), node_features.dtype)
        deg = jax.ops.segment_sum(ones, tgt, num_segments=num_nodes)
        denom = jax.ops.segment_sum(ex, tgt, num_segments=num_nodes) + (num_edges - deg)[:, None] * jnp.exp(-m)
        w = ex / denom[tgt]
        h_prime = jax.ops.segment_sum(w[:, :, None] * h_src, tgt, num_segments=num_nodes)
        return h_prime.reshape(num_nodes, H * HD)
    edge_index = jnp.stack([src, dst])
    x = _layernorm(x + _L0_gnn_ref(x, edge_index, edge_weight, L0_gnn_W0s, L0_gnn_W1s, L0_gnn_bn1_g, L0_gnn_bn1_b, L0_gnn_bn2_g, L0_gnn_bn2_b, L0_gnn_bn3_g, L0_gnn_bn3_b), axis=-1)
    x = _layernorm(x + _L1_gnn_ref(x, edge_index, edge_attr_64, L1_gnn_W_node, L1_gnn_W_edge, L1_gnn_a), axis=-1)
    return x

_drawn_inputs = setup_inputs


def setup_inputs(seed=0):
    import zlib

    import numpy as np

    out = dict(_drawn_inputs(seed))
    spreads = {'L0_gnn_bn1_g': (1.0, 0.2),
     'L0_gnn_bn1_b': (0.0, 0.1),
     'L0_gnn_bn2_g': (1.0, 0.6),
     'L0_gnn_bn2_b': (0.0, 0.1),
     'L0_gnn_bn3_g': (1.0, 0.2),
     'L0_gnn_bn3_b': (0.0, 0.1)}
    factors = {}
    for name, (base, spread) in spreads.items():
        noise = np.random.default_rng([zlib.crc32(name.encode()), seed]).standard_normal(out[name].shape)
        drawn = base * np.exp(spread * noise) if base else spread * noise
        out[name] = jnp.asarray(drawn.astype(out[name].dtype))
    for name, factor in factors.items():
        out[name] = (out[name] * factor).astype(out[name].dtype)
    return out
```

```python
from contextlib import ExitStack, contextmanager

import numpy as np

import concourse.bass as bass
from concourse import mybir
from concourse.alu_op_type import AluOpType as ALU

F32, BF16 = mybir.dt.float32, mybir.dt.bfloat16
I32, I16 = mybir.dt.int32, mybir.dt.int16
ACT = mybir.ActivationFunctionType
AX = mybir.AxisListType.X

P = 128
J = 4
CHUNK = P * J
WIN = 32
HEADS, HD = 4, 32
ROW = P + HEADS
SLOTS = 8
TILE = 125
BLK = 2 * TILE
BS = 5
BN_EPS = 1e-5
FAR = float(1 << 20)
MASK = 2.0**100


def gnn_program(nc, x, src, dst, edge_attr, edge_weight, W0s, W1s, bns, W_node, W_edge, a, out):
    N, E = x.shape[0], src.shape[0]
    LAYERS, FE = W0s.shape[0], edge_attr.shape[1]
    CHR = -(-E // CHUNK)
    CH = -(-CHR // SLOTS) * SLOTS
    ITERS = CH // SLOTS
    GRP = -(-CH // P)
    FULL, TAIL = (CHR - 1) // P, (CHR - 1) % P
    LAST = E - (CHR - 1) * CHUNK
    NP = N + WIN
    NBLK, NT = N // BLK, N // TILE
    BITERS = NBLK // BS
    NWIN = -(-N // WIN)
    assert N % (BLK * BS) == 0 and FE * 2 == P and NP * 2 >= 4 * GRP * CHUNK

    ctx = ExitStack()
    with ctx:
        def sb(name, shape, dt=F32):
            return ctx.enter_context(nc.sbuf_tensor(name, shape, dt))

        def sem(name):
            return ctx.enter_context(nc.semaphore(name))

        def dram(name, shape, dt=F32):
            return nc.dram_tensor(name, shape, dt).ap()

        h_rows = dram("h_rows", (N, P))
        att_rows = dram("att_rows", (N, ROW))
        x1_rows = dram("x1_rows", (N, P))
        deg_row = dram("deg_row", (1, N))
        base_rows = dram("base_rows", (2 * GRP, P))

        src_col = sb("src_col", [P, CH + SLOTS, J], I16)
        dst_col = sb("dst_col", [P, CH, J], I16)
        dst_rel = sb("dst_rel", [P, CH, J])
        w_col = sb("w_col", [P, CH, J])
        edge_score = sb("edge_score", [P, CH, J * HEADS])
        acc = sb("acc", [P, 2, NP])
        mid = sb("mid", [P, NP])
        tgt_score = sb("tgt_score", [HEADS, NP])
        rows = sb("rows", [P, SLOTS, J, ROW])
        idx = sb("idx", [P, SLOTS, J], I32)
        base_int = sb("base_int", [1, GRP * P], I32)
        wide_int = sb("wide_int", [1, 1], I32)
        work = sb("work", [P, 5400])
        w0 = sb("w0", [P, LAYERS, P])
        w1 = sb("w1", [P, LAYERS, P])
        bn = sb("bn", [P, 6, LAYERS])
        proj = sb("proj", [P, ROW + HEADS])
        edge_fold = sb("edge_fold", [P, 2 * HEADS])
        ident = sb("ident", [P, P])
        ident_b = sb("ident_b", [P, P], BF16)
        ones_b = sb("ones_b", [P, P], BF16)
        ones4 = sb("ones4", [HEADS, CHUNK])
        iota_blk = sb("iota_blk", [P, BLK])
        iota_win = iota_blk[:, 0:WIN]
        head_sel = sb("head_sel", [P, HEADS])
        head_blk = sb("head_blk", [P, P])
        node_sel = sb("node_sel", [P, WIN])
        win_start = sb("win_start", [P, NWIN])
        blk_start = sb("blk_start", [P, NBLK])
        stats = sb("stats", [P, NT, 6])
        small = sb("small", [P, 16])
        onehot = sb("onehot", [P, SLOTS, J, WIN])
        onehot_b = sb("onehot_b", [P, SLOTS * J * WIN], BF16)

        bank = [ctx.enter_context(nc.psum_tensor(f"bank{i}", [P, 512], F32)) for i in range(8)]

        flat = acc[:, :, :].rearrange("p c n -> p (c n)")

        def cut(start, *shape, dt=F32, of=None):
            n = int(np.prod(shape))
            v = (work if of is None else of)[:, start:start + n]
            if dt != F32:
                v = v.bitcast(dt)
            if len(shape) == 2:
                v = v.rearrange("p (a b) -> p a b", b=shape[1])
            if len(shape) == 3:
                v = v.rearrange("p (a b c) -> p a b c", b=shape[1], c=shape[2])
            return v

        def bcast(v, axis, n):
            v = v.unsqueeze(axis)
            return v.broadcast_to([*v.shape[:axis], n, *v.shape[axis + 1:]])

        def after(eng, s, n):
            if not isinstance(n, int) or n >= 1:
                eng.wait_ge(s, n)

        def chunks(eng, stages):
            for u in range(SLOTS):
                for f, lag in stages:
                    if u >= lag:
                        f(u - lag, u - lag, 0)
            with eng.Fori(1, ITERS) as i:
                for u in range(SLOTS):
                    for f, lag in stages:
                        f(i * SLOTS + (u - lag), (u - lag) % SLOTS, i if u >= lag else i - 1)
            for u in range(max(lag for _, lag in stages)):
                for f, lag in stages:
                    if u < lag:
                        f(CH + u - lag, (u - lag) % SLOTS, ITERS - 1)

        s_load, s_pad, s_const = sem("s_load"), sem("s_pad"), sem("s_const")
        s_wload, s_dve, s_tr, s_trs = sem("s_wload"), sem("s_dve"), sem("s_tr"), sem("s_trs")
        s_act, s_base, s_baseld = sem("s_act"), sem("s_base"), sem("s_baseld")
        s_fold, s_basetr = sem("s_fold"), sem("s_basetr")

        raw_src = cut(0, GRP, CHUNK, dt=I32, of=flat)
        raw_min = cut(GRP * CHUNK, GRP, CHUNK, dt=I32, of=flat)
        raw_max = cut(2 * GRP * CHUNK, GRP, CHUNK, dt=I32, of=flat)
        raw_w = cut(3 * GRP * CHUNK, GRP, CHUNK, of=flat)
        scores_flat = edge_score[:, :, :].rearrange("p c k -> p (c k)")
        src_f = cut(0, GRP, CHUNK, of=scores_flat)
        dst_f = cut(GRP * CHUNK, GRP, CHUNK, of=scores_flat)
        iota_i = cut(0, BLK, dt=I32)
        base_bc = cut(250, GRP * P)
        base_f = cut(250 + GRP * P, 2 * GRP * P)
        bs = cut(1900, 2 * GRP)
        bs_t = cut(1920, P)
        win_i = cut(2600, NWIN, dt=I32)
        blk_i = cut(2900, NBLK, dt=I32)
        wn_nat, we_twice = cut(2200, P), cut(2360, 2, FE)
        a_col = cut(2500, 3)
        a_mask = cut(2520, 3, HEADS)
        spread = cut(2580, 8)

        by_chunk = [(raw_src, src), (raw_min, dst), (raw_max, dst), (raw_w, edge_weight)]
        n_loads = len(by_chunk) * ((FULL > 0) + (TAIL > 0) + 1)
        with nc.Block() as block:
            @block.sync
            def _(sp):
                sp.wait_ge(s_pad, 4)
                for raw, d in by_chunk:
                    if FULL:
                        sp.dma_start(raw[:, 0:FULL, :], d[0:FULL * P * CHUNK].rearrange(
                            "(g r c) -> r g c", r=P, c=CHUNK)).then_inc(s_load, 16)
                    if TAIL:
                        sp.dma_start(raw[0:TAIL, FULL, :], d[FULL * P * CHUNK:(CHR - 1) * CHUNK].rearrange(
                            "(r c) -> r c", c=CHUNK)).then_inc(s_load, 16)
                    sp.dma_start(raw[TAIL:TAIL + 1, FULL, 0:LAST],
                                 d[(CHR - 1) * CHUNK:E].rearrange("(r c) -> r c", r=1)).then_inc(s_load, 16)
                sp.wait_ge(s_basetr, 2)
                sp.dma_start(base_rows, bs_t[0:2 * GRP, :]).then_inc(s_base, 16)
                sp.wait_ge(s_base, 16)
                row = base_rows.rearrange("(o g) r -> o (g r)", o=1)
                sp.dma_start(base_f[0:1, :], row).then_inc(s_baseld, 16)
                sp.dma_start(base_bc[:, :], row[:, 0:GRP * P].broadcast_to([P, GRP * P])).then_inc(s_baseld, 16)

            @block.scalar
            def _(act):
                act.dma_start(w0[:, :, :], W0s.rearrange("l i o -> i l o")).then_inc(s_wload, 16)
                act.dma_start(w1[:, :, :], W1s.rearrange("l i o -> i l o")).then_inc(s_wload, 16)
                for k, v in enumerate(bns):
                    act.dma_start(bn[:, k, :], v.rearrange("l d -> d l"),
                                  allow_slow_non_contiguous=True).then_inc(s_wload, 16)
                act.dma_start(wn_nat, W_node).then_inc(s_wload, 16)
                for k in range(2):
                    act.dma_start(we_twice[:, k, :], W_edge).then_inc(s_wload, 16)
                for h in range(HEADS):
                    act.dma_start(a_col[h * HD:(h + 1) * HD, :], a[h, :].rearrange("(s k) -> k s", k=HD),
                                  allow_slow_non_contiguous=True).then_inc(s_wload, 16)

            @block.gpsimd
            def _(pool):
                pool.memset(raw_src[:, FULL:, :], 0).then_inc(s_pad, 1)
                pool.memset(raw_min[:, FULL:, :], int(FAR)).then_inc(s_pad, 1)
                pool.memset(raw_max[:, FULL:, :], -1).then_inc(s_pad, 1)
                pool.memset(raw_w[:, FULL:, :], 0.0).then_inc(s_pad, 1)
                pool.memset(ident[:, :], 0.0).then_inc(s_const, 1)
                pool.memset(head_sel[:, :], 1.0).then_inc(s_const, 1)
                pool.iota(blk_i, pattern=[[BLK, NBLK]], base=0, channel_multiplier=0)
                pool.iota(iota_i, pattern=[[1, BLK]], base=0, channel_multiplier=0).then_inc(s_const, 1)
                pool.iota(win_i, pattern=[[WIN, NWIN]], base=0, channel_multiplier=0).then_inc(s_const, 1)
                pool.wait_ge(s_const, 2)
                pool.affine_select(out=ident[:, :], in_=ident[:, :], compare_op=ALU.not_equal, fill=1.0,
                                   base=0, pattern=[[-1, P]], channel_multiplier=1).then_inc(s_const, 1)
                pool.affine_select(out=head_sel[:, :], in_=head_sel[:, :], compare_op=ALU.is_ge, fill=0.0,
                                   base=0, pattern=[[-HD, HEADS]], channel_multiplier=1).then_inc(s_const, 1)
                pool.wait_ge(s_const, 6)
                pool.affine_select(out=head_sel[:, :], in_=head_sel[:, :], compare_op=ALU.is_ge, fill=0.0,
                                   base=HD - 1, pattern=[[HD, HEADS]], channel_multiplier=-1).then_inc(s_const, 1)
                pool.memset(ones_b[:, :], 1.0).then_inc(s_const, 1)
                pool.memset(ones4[:, :], 1.0).then_inc(s_const, 1)
                pool.memset(tgt_score[:, :], 0.0).then_inc(s_const, 1)
                pool.memset(mid[:, :], 0.0).then_inc(s_const, 1)
                pool.memset(edge_fold[:, :], 0.0).then_inc(s_const, 1)

            @block.vector
            def _(dve):
                done = [0]

                def link(ins):
                    done[0] += 1
                    ins.then_inc(s_dve, 1)
                    dve.wait_ge(s_dve, done[0])

                dve.wait_ge(s_const, 12)
                nc.vector.tensor_copy(iota_blk[:, :], iota_i)
                nc.vector.tensor_copy(blk_start[:, :], blk_i)
                nc.vector.tensor_copy(win_start[:, :], win_i)
                nc.vector.tensor_copy(ident_b[:, :], ident[:, :])
                nc.vector.tensor_copy(head_blk[:, :].rearrange("p (h k) -> p h k", h=HEADS),
                                      bcast(head_sel[:, :], 2, HD))
                nc.vector.tensor_reduce(node_sel[:, :], ident[:, :].rearrange("p (h n) -> p n h", h=HEADS),
                                        AX, ALU.add)
                dve.wait_ge(s_load, 16 * n_loads)
                link(nc.vector.tensor_copy(src_f, raw_src))
                link(nc.vector.tensor_copy(dst_f, raw_max))
                link(nc.vector.tensor_reduce(spread[:, 0:GRP], raw_min, AX, ALU.min))
                link(nc.vector.tensor_reduce(spread[:, 4:4 + GRP], raw_max, AX, ALU.max))
                link(nc.vector.tensor_scalar(bs[:, 0:GRP], spread[:, 0:GRP], float(N - 1), None, ALU.min))
                link(nc.vector.tensor_tensor(bs[:, GRP:], spread[:, 4:4 + GRP], bs[:, 0:GRP], ALU.subtract))
                dve.wait_ge(s_wload, 16 * 15)
                link(nc.vector.tensor_tensor(a_mask, bcast(a_col, 2, HEADS), bcast(head_sel[:, :], 1, 3), ALU.mult))
                k = 0
                for g in range(GRP):
                    n = min(P, CH - g * P)
                    for what in range(3):
                        for j in range(J):
                            k += 1
                            dve.wait_ge(s_tr, k)
                            t = bank[k % 4][:, 0:n]
                            if what == 0:
                                nc.vector.tensor_copy(src_col[:, g * P:g * P + n, j], t).then_inc(s_trs, 1)
                            elif what == 1:
                                nc.vector.tensor_copy(dst_col[:, g * P:g * P + n, j], t)
                                nc.vector.tensor_copy(dst_rel[:, g * P:g * P + n, j], t).then_inc(s_trs, 1)
                            else:
                                nc.vector.tensor_copy(w_col[:, g * P:g * P + n, j], t).then_inc(s_trs, 1)
                dve.wait_ge(s_trs, k)
                nc.vector.tensor_copy(src_col[:, CH:CH + SLOTS, :], src_col[:, 0:SLOTS, :])
                dve.wait_ge(s_basetr, 1)
                nc.vector.tensor_copy(bs_t[0:2 * GRP, :], bank[4][0:2 * GRP, 0:P]).then_inc(s_basetr, 1)
                dve.wait_ge(s_baseld, 32)
                nc.vector.tensor_copy(base_int[:, :], base_f[0:1, 0:GRP * P])
                link(nc.vector.tensor_reduce(small[0:1, 0:1], base_f[0:1, GRP * P:], AX, ALU.max))
                nc.vector.tensor_scalar(wide_int[:, :], small[0:1, 0:1], float(WIN), None, ALU.is_ge)
                nc.vector.tensor_tensor(dst_rel[:, :, :], dst_rel[:, :, :],
                                        bcast(base_bc[:, 0:CH], 2, J), ALU.subtract)
                dve.wait_ge(s_fold, 1)
                nc.vector.tensor_copy(proj[:, 0:P], bank[5][:, 0:P])
                nc.vector.tensor_copy(proj[:, P:P + 2 * HEADS], bank[5][:, P:P + 2 * HEADS])
                for k in range(2):
                    nc.vector.tensor_copy(edge_fold[k * FE:(k + 1) * FE, k * HEADS:(k + 1) * HEADS],
                                          bank[6][k * FE:(k + 1) * FE, 0:HEADS])

            @block.tensor
            def _(pe):
                pe.wait_ge(s_const, 12)
                pe.wait_ge(s_load, 16 * n_loads)
                pe.wait_ge(s_dve, 2)
                k = 0
                for g in range(GRP):
                    n = min(P, CH - g * P)
                    for f in (src_f, dst_f, raw_w):
                        for j in range(J):
                            k += 1
                            if k > 4:
                                pe.wait_ge(s_trs, k - 4)
                            nc.tensor.transpose(bank[k % 4][:, 0:P], f[:, g, j::J], ident[:, :]).then_inc(s_tr, 1)
                pe.wait_ge(s_dve, 7)
                nc.tensor.transpose(bank[4][0:2 * GRP, 0:P], bs, ident[:, :]).then_inc(s_basetr, 1)
                nc.tensor.transpose(bank[5][:, 0:P], wn_nat, ident[:, :])
                for k in range(2):
                    nc.tensor.matmul(bank[5][:, P + k * HEADS:P + (k + 1) * HEADS], wn_nat, a_mask[:, k, :],
                                     start=True, stop=True)
                nc.tensor.matmul(bank[6][:, 0:HEADS], we_twice.rearrange("p k f -> p (k f)"), a_mask[:, 2, :],
                                 start=True, stop=True).then_inc(s_fold, 1)

        @contextmanager
        def phase():
            with ExitStack() as st:
                held = []

                def new(name, n=None):
                    got = [st.enter_context(nc.semaphore(name if n is None else f"{name}{k}")) for k in range(n or 1)]
                    held.extend(got)
                    return got if n else got[0]
                yield new
                nums = sorted(h.num for h in held)
                with nc.Block() as block:
                    @block.sync
                    def _(sp):
                        start = nums[0]
                        for k, num in enumerate(nums):
                            if k + 1 == len(nums) or nums[k + 1] != num + 1:
                                sp.sem_clear(range(start, num + 1))
                                start = nums[k + 1] if k + 1 < len(nums) else None

        def blocks(eng, f):
            with eng.Fori(0, BITERS) as i:
                for s in range(BS):
                    f(i * BS + s, s)

        def node_rows(table):
            return table.rearrange("(t p) d -> p t d", p=TILE)

        slot_x = cut(0, BS, 2, P)
        slot_f = cut(1280, BS, BLK)
        slot_n = cut(2560, BS, 2, ROW)
        slot_g = cut(2560, BS, BLK)
        slot_d = cut(3900, BS, BLK)

        def fblk(arr, b):
            return arr[:, bass.ds(b * BLK, BLK)]

        with phase() as new:
            x_landed, x_turned, x_saved, zeroed = new("x_landed", BS), new("x_turned"), new("x_saved"), new("zeroed")
            with nc.Block() as block:
                @block.sync
                def _(sp):
                    def load(b, s):
                        sp.wait_ge(x_turned, b + 1)
                        sp.dma_start(slot_x[0:TILE, s], node_rows(x)[:, bass.ds(2 * b, 2), :]).then_inc(x_landed[s], 16)
                    blocks(sp, load)

                @block.tensor
                def _(pe):
                    pe.sem_inc(x_turned, BS)

                    def turn(b, s, i=None):
                        pe.wait_ge(x_saved, b + 1)
                        for t in range(2):
                            ins = nc.tensor.transpose(bank[s][:, t * TILE:(t + 1) * TILE], slot_x[0:TILE, s, t, :],
                                                      ident[0:TILE, 0:TILE])
                        ins.then_inc(x_turned, 1)
                    with pe.Fori(0, BITERS) as i:
                        for s in range(BS):
                            pe.wait_ge(x_landed[s], i * 16 + 16)
                            turn(i * BS + s, s)

                @block.scalar
                def _(act):
                    act.sem_inc(x_saved, BS)

                    def save(b, s):
                        act.wait_ge(x_turned, b + BS + 1)
                        nc.scalar.copy(acc[:, 0, bass.ds(b * BLK, BLK)], bank[s][:, 0:BLK]).then_inc(x_saved, 1)
                    blocks(act, save)

                @block.vector
                def _(dve):
                    nc.vector.memset(acc[:, 0, N:NP], 0.0)
                    nc.vector.memset(acc[:, 1, :], 0.0)

        rows_landed = [sem(f"rows_landed{u}") for u in range(SLOTS)]
        idx_copied, rows_done, gather_go = sem("idx_copied"), sem("rows_done"), sem("gather_go")
        onehot_ready, acc_added = sem("onehot_ready"), sem("acc_added")
        LAND = 16 * J

        def gather_chunk(pool, u, table, width):
            for j in range(J):
                pool.indirect_dma_start(
                    out=rows[:, u, j, 0:width], out_offset=None, in_=table,
                    in_offset=bass.IndirectOffsetOnAxis(ap=idx[:, u, j:j + 1], axis=0),
                ).then_inc(rows_landed[u], 16)

        def gather(pool, table, width, run, freed, freed_base):
            with pool.Fori(0, ITERS) as i:
                for u in range(SLOTS):
                    pool.wait_ge(idx_copied, i * SLOTS + (run * CH + u + 1))
                    pool.wait_ge(freed, i * SLOTS + (freed_base + u + 1))
                    pool.sem_inc(gather_go, 1)
                    gather_chunk(pool, u, table, width)

        def copy_idx(act, run):
            def f(c, u, turn):
                act.wait_ge(rows_landed[u], turn * LAND + LAND * (run * ITERS + 1))
                nc.scalar.copy(idx[:, u, :], src_col[:, bass.ds(c + SLOTS, 1), :]
                               .rearrange("p c j -> p (c j)")).then_inc(idx_copied, 1)
            return f

        ea_slot = cut(0, SLOTS, J * FE)
        ea_turned_sb = cut(SLOTS * J * FE, 2, J * FE)
        gen_onehot = cut(2560, J, BLK)
        gen_plain = cut(3560, J, BLK // 2)
        gen_rel = cut(4100, J)
        gen_plain = gen_plain.rearrange("p j n -> p (j n)").bitcast(BF16).rearrange("p (j n) -> p j n", n=BLK)

        with nc.Block() as block:
            @block.scalar
            def _(act):
                for u in range(SLOTS):
                    nc.scalar.copy(idx[:, u, :], src_col[:, u, :]).then_inc(idx_copied, 1)

            @block.tensor
            def _(pe):
                pe.sem_inc(rows_done, SLOTS)

            @block.vector
            def _(dve):
                dve.sem_inc(acc_added, 2)

        def messages(layer):
            table = x if layer == 0 else h_rows
            plain = onehot_b[:, :].rearrange("p (u j n) -> p u j n", u=SLOTS, j=J)
            first = layer == 0
            done, comps = layer * CH, 2 if first else 1
            with phase() as new:
                if first:
                    ea_landed, ea_under, ea_turned = new("ea_landed", SLOTS), new("ea_under"), new("ea_turned")
                    eat_saved, score_done, score_saved = new("eat_saved"), new("score_done"), new("score_saved")
                gen_ready, gen_summed, gen_added = new("gen_ready"), new("gen_summed"), new("gen_added")
                gen_rel_ready, gen_idx, gen_free = new("gen_rel_ready"), new("gen_idx"), new("gen_free")

                with nc.Block() as block:
                    @block.sync
                    def _(sp):
                        if not first:
                            return
                        per_chunk = edge_attr[0:(CHR - 1) * CHUNK, :].rearrange("(c p j) f -> p c (j f)", p=P, j=J)
                        with sp.Fori(0, ITERS - 1) as i:
                            for u in range(SLOTS):
                                sp.wait_ge(ea_turned, i * SLOTS + u + 1)
                                sp.dma_start(ea_slot[:, u, :], per_chunk[:, bass.ds(i * SLOTS + u, 1), :]
                                             .rearrange("p c f -> p (c f)")).then_inc(ea_landed[u], 16)
                        for u in range(SLOTS):
                            c = CH - SLOTS + u
                            sp.wait_ge(ea_turned, c + 1)
                            if c < CHR - 1:
                                sp.dma_start(ea_slot[:, u, :], per_chunk[:, c, :]).then_inc(ea_landed[u], 16)
                                continue
                            if c > CHR - 1:
                                sp.dma_start(ea_slot[:, u, :], per_chunk[:, 0, :]).then_inc(ea_landed[u], 16)
                                continue
                            sp.dma_start(ea_slot[:, u, :], per_chunk[:, 0, :]).then_inc(ea_under, 16)
                            sp.wait_ge(ea_under, 16)
                            n, tail = 1, edge_attr[(CHR - 1) * CHUNK:E, :]
                            full, part = LAST // J, LAST % J
                            if full:
                                sp.dma_start(ea_slot[0:full, u, :], tail[0:full * J, :].rearrange(
                                    "(p j) f -> p (j f)", j=J)).then_inc(ea_under, 16)
                                n += 1
                            if part:
                                sp.dma_start(ea_slot[full:full + 1, u, 0:part * FE], tail[full * J:LAST, :]
                                             .rearrange("(p j) f -> p (j f)", p=1)).then_inc(ea_under, 16)
                                n += 1
                            sp.wait_ge(ea_under, 16 * n)
                            sp.sem_inc(ea_landed[u], 16)

                    @block.gpsimd
                    def _(pool):
                        wide = pool.value_load(wide_int[0:1, 0:1], min_val=0, max_val=1)
                        with pool.If(wide < 1):
                            gather(pool, table, P, layer, rows_done, done)
                        with pool.Else():
                            with pool.Fori(0, CH) as c:
                                pool.wait_ge(gen_idx, c + 1)
                                pool.wait_ge(gen_free, c + 1)
                                pool.sem_inc(gather_go, 1)
                                gather_chunk(pool, 0, table, P)

                    @block.vector
                    def _(dve):
                        wide = dve.value_load(wide_int[0:1, 0:1], min_val=0, max_val=1)

                        def select(c, u, turn):
                            dve.wait_ge(rows_done, c + (done + 1))
                            for j in range(J):
                                col = lambda arr: arr[:, bass.ds(c, 1), j:j + 1].rearrange("p c j -> p (c j)")
                                ins = nc.vector.tensor_scalar(onehot[:, u, j, :], iota_win[:, :], col(dst_rel),
                                                              col(w_col), ALU.is_equal, ALU.mult)
                            if first:
                                ins = nc.vector.tensor_tensor(
                                    plain[:, u], bcast(iota_win[:, :], 1, J),
                                    bcast(dst_rel[:, bass.ds(c, 1), :].rearrange("p c j -> p (c j)"), 2, WIN),
                                    ALU.is_equal)
                            ins.then_inc(onehot_ready, 1)

                        def add(c, u, turn):
                            b = dve.value_load(base_int[0:1, bass.ds(c, 1)], min_val=0, max_val=N - 1)
                            dve.wait_ge(rows_done, c + (SLOTS + done + 1))
                            dve.wait_ge(acc_added, c + (2 + done))
                            win = acc[:, 0:comps, bass.ds(b, WIN)]
                            nc.vector.tensor_tensor(
                                win, win, bank[u % 2][:, 0:comps * WIN].rearrange("p (k n) -> p k n", n=WIN),
                                ALU.add).then_inc(acc_added, 1)

                        with dve.If(wide < 1):
                            chunks(dve, [(add, 2), (select, 0)])
                        with dve.Else():
                            dve.sem_inc(gen_free, 1)
                            with dve.Fori(0, CH) as c:
                                with dve.Fori(0, NBLK) as k:
                                    q = c * NBLK + k
                                    nc.vector.tensor_scalar(
                                        gen_rel, dst_col[:, bass.ds(c, 1), :].rearrange("p c j -> p (c j)"),
                                        blk_start[:, bass.ds(k, 1)], None, ALU.subtract).then_inc(gen_rel_ready, 1)
                                    dve.wait_ge(gen_rel_ready, q + 1)
                                    for j in range(J):
                                        wj = w_col[:, bass.ds(c, 1), j:j + 1].rearrange("p c j -> p (c j)")
                                        ins = nc.vector.tensor_scalar(gen_onehot[:, j, :], iota_blk[:, :],
                                                                      gen_rel[:, j:j + 1], wj, ALU.is_equal, ALU.mult)
                                    if first:
                                        ins = nc.vector.tensor_tensor(gen_plain, bcast(iota_blk[:, :], 1, J),
                                                                      bcast(gen_rel, 2, BLK), ALU.is_equal)
                                    ins.then_inc(gen_ready, 1)
                                    dve.wait_ge(gen_summed, q + 1)
                                    for comp in range(comps):
                                        win = acc[:, comp, bass.ds(k * BLK, BLK)]
                                        ins = nc.vector.tensor_tensor(win, win, bank[comp][:, 0:BLK], ALU.add)
                                    ins.then_inc(gen_added, 1)
                                    dve.wait_ge(gen_added, q + 1)
                                dve.sem_inc(gen_free, 1)

                    @block.tensor
                    def _(pe):
                        wide = pe.value_load(wide_int[0:1, 0:1], min_val=0, max_val=1)
                        if first:
                            pe.sem_inc(ea_turned, SLOTS)
                            pe.sem_inc(score_done, 2)

                        def add_up(c, u, turn):
                            pe.wait_ge(onehot_ready, c + (done + 1))
                            pe.wait_ge(acc_added, c + (done + 1))
                            pe.wait_ge(rows_landed[u], turn * LAND + LAND * (layer * ITERS + 1))
                            for j in range(J):
                                ins = nc.tensor.matmul(bank[u % 2][:, 0:WIN], rows[:, u, j, 0:P],
                                                       onehot[:, u, j, :], start=(j == 0), stop=(j == J - 1))
                            if first:
                                for j in range(J):
                                    ins = nc.tensor.matmul(bank[u % 2][:, WIN:2 * WIN], ones_b[:, :],
                                                           plain[:, u, j, :], start=(j == 0), stop=(j == J - 1))
                            ins.then_inc(rows_done, 1)

                        def turn_attr(c, u, turn):
                            pe.wait_ge(ea_landed[u], turn * 16 + 16)
                            pe.wait_ge(eat_saved, c + 1)
                            for k in range(J // 2):
                                ins = nc.tensor.transpose(bank[2 + u % 2][:, k * P:(k + 1) * P],
                                                          ea_slot[:, u, k * P:(k + 1) * P], ident[:, :])
                            ins.then_inc(ea_turned, 1)

                        def score_attr(c, u, turn):
                            pe.wait_ge(eat_saved, c + 3)
                            pe.wait_ge(score_saved, c + 1)
                            for k in range(J // 2):
                                ins = nc.tensor.matmul(bank[4 + u % 2][:, k * 2 * HEADS:(k + 1) * 2 * HEADS],
                                                       ea_turned_sb[:, u % 2, k * P:(k + 1) * P], edge_fold[:, :],
                                                       start=True, stop=True)
                            ins.then_inc(score_done, 1)

                        attr = [(turn_attr, 0), (score_attr, 1)] if first else []
                        with pe.If(wide < 1):
                            chunks(pe, attr + [(add_up, 0)])
                        with pe.Else():
                            if first:
                                chunks(pe, attr)
                            with pe.Fori(0, CH) as c:
                                with pe.Fori(0, NBLK) as k:
                                    pe.wait_ge(rows_landed[0], c * LAND + LAND * (layer * CH + 1))
                                    pe.wait_ge(gen_ready, c * NBLK + k + 1)
                                    for j in range(J):
                                        ins = nc.tensor.matmul(bank[0][:, 0:BLK], rows[:, 0, j, 0:P],
                                                               gen_onehot[:, j, :], start=(j == 0), stop=(j == J - 1))
                                    if first:
                                        for j in range(J):
                                            ins = nc.tensor.matmul(bank[1][:, 0:BLK], ones_b[:, :], gen_plain[:, j, :],
                                                                   start=(j == 0), stop=(j == J - 1))
                                    ins.then_inc(gen_summed, 1)

                    @block.scalar
                    def _(act):
                        wide = act.value_load(wide_int[0:1, 0:1], min_val=0, max_val=1)
                        if first:
                            act.sem_inc(eat_saved, 2)
                            act.sem_inc(score_saved, 2)

                        def save_turned(c, u, turn):
                            act.wait_ge(ea_turned, c + (SLOTS + 1))
                            act.wait_ge(score_done, c + 1)
                            nc.scalar.copy(ea_turned_sb[:, u % 2, :], bank[2 + u % 2][:, 0:J * FE]).then_inc(eat_saved, 1)

                        def save_score(c, u, turn):
                            act.wait_ge(score_done, c + 3)
                            nc.scalar.copy(edge_score[:, bass.ds(c, 1), :].rearrange("p c k -> p (c k)"),
                                           bank[4 + u % 2][:, 0:J * HEADS]).then_inc(score_saved, 1)

                        attr = [(save_turned, 0), (save_score, 1)] if first else []
                        with act.If(wide < 1):
                            chunks(act, attr + [(copy_idx(act, layer), 0)])
                        with act.Else():
                            if first:
                                chunks(act, attr)
                            general_idx(act, layer, gen_idx)

        def general_idx(act, run, gen_idx):
            act.wait_ge(idx_copied, SLOTS)
            if run:
                act.wait_ge(rows_landed[0], LAND * run * CH)
            nc.scalar.copy(idx[:, 0, :], src_col[:, 0, :]).then_inc(gen_idx, 1)
            with act.Fori(1, CH) as c:
                act.wait_ge(rows_landed[0], c * LAND + LAND * run * CH)
                nc.scalar.copy(idx[:, 0, :], src_col[:, bass.ds(c, 1), :].rearrange("p c j -> p (c j)")).then_inc(gen_idx, 1)

        bn_scale, bn_shift = sb("bn_scale", [P, 1]), sb("bn_shift", [P, 1])

        def fold_norm(dve, which, layer, var_ready, std_ready, chain, folded):
            n = [0]

            def link(ins):
                n[0] += 1
                ins.then_inc(chain, 1)
                dve.wait_ge(chain, n[0])
            g, b = (bn[:, 2 * which + k, layer:layer + 1] for k in range(2))
            link(nc.vector.bn_aggr(small[:, 0:2], stats[:, 0:NBLK, :].rearrange("p b s -> p (b s)")))
            nc.vector.tensor_scalar(small[:, 2:3], small[:, 1:2], BN_EPS, None, ALU.add).then_inc(var_ready, 1)
            dve.wait_ge(std_ready, 1)
            link(nc.vector.reciprocal(small[:, 4:5], small[:, 3:4]))
            link(nc.vector.tensor_tensor(bn_scale[:, :], small[:, 4:5], g, ALU.mult))
            link(nc.vector.tensor_tensor(small[:, 5:6], small[:, 0:1], bn_scale[:, :], ALU.mult))
            nc.vector.tensor_tensor(bn_shift[:, :], b, small[:, 5:6], ALU.subtract).then_inc(folded, 1)

        def std(act, var_ready, std_ready):
            act.wait_ge(var_ready, 1)
            nc.scalar.activation(small[:, 3:4], small[:, 2:3], ACT.Sqrt).then_inc(std_ready, 1)

        def first_product(layer):
            with phase() as new:
                product, saved, deg_out = new("product"), new("saved"), new("deg_out")
                with nc.Block() as block:
                    @block.sync
                    def _(sp):
                        if layer == 0:
                            sp.dma_start(deg_row, acc[0:1, 1, 0:N]).then_inc(deg_out, 16)
                            sp.wait_ge(deg_out, 16)

                    @block.tensor
                    def _(pe):
                        def f(b, s):
                            pe.wait_ge(saved, b + 1)
                            nc.tensor.matmul(bank[s][:, 0:BLK], w0[:, layer, :], fblk(acc[:, 0, :], b),
                                             start=True, stop=True).then_inc(product, 1)
                        blocks(pe, f)

                    @block.scalar
                    def _(act):
                        act.sem_inc(saved, BS)

                        def f(b, s):
                            act.wait_ge(product, b + 1)
                            nc.scalar.copy(fblk(mid, b), bank[s][:, 0:BLK]).then_inc(saved, 1)
                        blocks(act, f)

                    @block.vector
                    def _(dve):
                        def f(b, s):
                            dve.wait_ge(saved, b + BS + 1)
                            nc.vector.bn_stats(stats[:, bass.ds(b, 1), :].rearrange("p b s -> p (b s)"), fblk(mid, b))
                        blocks(dve, f)

        def second_product(layer):
            with phase() as new:
                var_ready, std_ready, chain, folded = new("var_ready"), new("std_ready"), new("chain"), new("folded")
                product, saved, normed, save_go = (new(n) for n in ("product", "saved", "normed", "save_go"))
                with nc.Block() as block:
                    @block.tensor
                    def _(pe):
                        def f(b, s):
                            pe.wait_ge(normed, b + 1)
                            pe.wait_ge(saved, b + 1)
                            nc.tensor.matmul(bank[s][:, 0:BLK], w1[:, layer, :], fblk(mid, b),
                                             start=True, stop=True).then_inc(product, 1)
                        blocks(pe, f)

                    @block.scalar
                    def _(act):
                        act.sem_inc(saved, BS)
                        std(act, var_ready, std_ready)
                        act.wait_ge(folded, 1)
                        with act.Fori(0, BITERS) as i:
                            for s in range(BS):
                                nc.scalar.activation(fblk(mid, i * BS + s), fblk(mid, i * BS + s), ACT.Relu,
                                                     bias=bn_shift[:, :], scale=bn_scale[:, :]).then_inc(normed, 1)
                            for s in range(BS):
                                act.wait_ge(product, i * BS + s + 1)
                                act.sem_inc(save_go, 1)
                                nc.scalar.copy(fblk(mid, i * BS + s), bank[s][:, 0:BLK]).then_inc(saved, 1)

                    @block.vector
                    def _(dve):
                        fold_norm(dve, 0, layer, var_ready, std_ready, chain, folded)

                        def f(b, s):
                            dve.wait_ge(saved, b + BS + 1)
                            nc.vector.bn_stats(stats[:, bass.ds(b, 1), :].rearrange("p b s -> p (b s)"), fblk(mid, b))
                        blocks(dve, f)

        def second_norm(layer):
            with phase() as new:
                var_ready, std_ready, chain, folded = new("var_ready"), new("std_ready"), new("chain"), new("folded")
                normed = new("normed")
                with nc.Block() as block:
                    @block.scalar
                    def _(act):
                        std(act, var_ready, std_ready)
                        act.wait_ge(folded, 1)

                        def f(b, s):
                            nc.scalar.activation(fblk(mid, b), fblk(mid, b), ACT.Relu, bias=bn_shift[:, :],
                                                 scale=bn_scale[:, :]).then_inc(normed, 1)
                        blocks(act, f)

                    @block.vector
                    def _(dve):
                        fold_norm(dve, 1, layer, var_ready, std_ready, chain, folded)

                        def f(b, s):
                            dve.wait_ge(normed, b + 1)
                            nc.vector.bn_stats(stats[:, bass.ds(b, 1), :].rearrange("p b s -> p (b s)"), fblk(mid, b))
                        blocks(dve, f)

        def third_norm(layer):
            with phase() as new:
                var_ready, std_ready, chain, folded = new("var_ready"), new("std_ready"), new("chain"), new("folded")
                normed, kept, turned, saved, stored = (new(n) for n in ("normed", "kept", "turned", "saved", "stored"))
                with nc.Block() as block:
                    @block.scalar
                    def _(act):
                        std(act, var_ready, std_ready)
                        act.wait_ge(folded, 1)

                        def f(b, s):
                            act.wait_ge(kept, b + 1)
                            act.wait_ge(turned, b + 1)
                            nc.scalar.activation(slot_f[:, s, :], fblk(mid, b), ACT.Relu, bias=bn_shift[:, :],
                                                 scale=bn_scale[:, :]).then_inc(normed, 1)
                        blocks(act, f)

                    @block.vector
                    def _(dve):
                        dve.sem_inc(kept, BS)
                        dve.sem_inc(saved, BS)
                        fold_norm(dve, 2, layer, var_ready, std_ready, chain, folded)

                        def f(b, s):
                            dve.wait_ge(normed, b + 1)
                            nc.vector.tensor_copy(fblk(acc[:, 0, :], b), slot_f[:, s, :]).then_inc(kept, 1)
                            dve.wait_ge(turned, b + BS + 1)
                            dve.wait_ge(stored, b + 1)
                            nc.vector.tensor_copy(slot_x[0:TILE, s].rearrange("p t d -> p (t d)"),
                                                  bank[s][0:TILE, 0:2 * P]).then_inc(saved, 1)
                        blocks(dve, f)

                    @block.tensor
                    def _(pe):
                        pe.sem_inc(turned, BS)

                        def f(b, s):
                            pe.wait_ge(normed, b + 1)
                            pe.wait_ge(saved, b + 1)
                            for t in range(2):
                                ins = nc.tensor.transpose(bank[s][0:TILE, t * P:(t + 1) * P],
                                                          slot_f[:, s, t * TILE:(t + 1) * TILE], ident[:, :])
                            ins.then_inc(turned, 1)
                        blocks(pe, f)

                    @block.gpsimd
                    def _(pool):
                        store_rows(pool, lambda s: slot_x[0:TILE, s], h_rows, saved, stored, layer)

        rows_out = [sem(f"rows_out{s}") for s in range(BS)]
        table_out = [sem(f"table_out{s}") for s in range(BS)]

        def store_rows(pool, slot, table, saved, stored, run):
            pool.sem_inc(stored, BS)
            with pool.Fori(0, BITERS) as i:
                for s in range(BS):
                    pool.wait_ge(saved, i * BS + (BS + s + 1))
                    pool.sem_inc(gather_go, 1)
                    pool.dma_start(node_rows(table)[:, bass.ds(2 * (i * BS + s), 2), :], slot(s)).then_inc(rows_out[s], 16)
                for s in range(BS):
                    pool.wait_ge(rows_out[s], i * 16 + 16 * (run * BITERS + 1))
                    pool.sem_inc(stored, 1)

        def to_rows(source, xn, residual, norm_layer=None):
            with phase() as new:
                var_ready, std_ready, chain, folded = new("var_ready"), new("std_ready"), new("chain"), new("folded")
                made, turned, added = new("made"), new("turned"), new("added")
                res_landed, deg_landed = new("res_landed", BS), new("deg_landed", BS)
                exp_done, den_done, deg_used = new("exp_done"), new("den_done"), new("deg_used")
                with nc.Block() as block:
                    @block.sync
                    def _(sp):
                        with sp.Fori(0, BITERS) as i:
                            for s in range(BS):
                                b = i * BS + s
                                sp.wait_ge(added, b + 1)
                                sp.dma_start(slot_x[0:TILE, s], node_rows(residual)[:, bass.ds(2 * b, 2), :]
                                             ).then_inc(res_landed[s], 16)
                                if source == "attention":
                                    sp.wait_ge(deg_used, b + 1)
                                    sp.dma_start(slot_d[:, s, :], deg_row[:, bass.ds(b * BLK, BLK)]
                                                 .broadcast_to([P, BLK])).then_inc(deg_landed[s], 16)

                    @block.scalar
                    def _(act):
                        if source == "norm":
                            std(act, var_ready, std_ready)
                            act.wait_ge(folded, 1)

                            def f(b, s):
                                act.wait_ge(turned, b + 1)
                                nc.scalar.activation(slot_f[:, s, :], fblk(mid, b), ACT.Identity, bias=bn_shift[:, :],
                                                     scale=bn_scale[:, :]).then_inc(made, 1)
                        else:
                            def f(b, s):
                                act.wait_ge(den_done, b + 1)
                                nc.scalar.activation(slot_g[:, s, :], fblk(mid, b), ACT.Exp,
                                                     scale=-1.0).then_inc(exp_done, 1)
                        blocks(act, f)

                    @block.tensor
                    def _(pe):
                        pe.sem_inc(turned, BS)

                        def f(b, s):
                            pe.wait_ge(made, b + 1)
                            pe.wait_ge(added, b + 1)
                            for t in range(2):
                                ins = nc.tensor.transpose(bank[s][0:TILE, t * P:(t + 1) * P],
                                                          slot_f[:, s, t * TILE:(t + 1) * TILE], ident[:, :])
                            ins.then_inc(turned, 1)
                        blocks(pe, f)

                    @block.vector
                    def _(dve):
                        dve.sem_inc(added, BS)
                        if source == "norm":
                            fold_norm(dve, 2, norm_layer, var_ready, std_ready, chain, folded)
                        else:
                            dve.sem_inc(deg_used, BS)
                            dve.sem_inc(den_done, BS)

                        def divide(b, s, i):
                            dve.wait_ge(deg_landed[s], i * 16 + 16)
                            nc.vector.tensor_scalar(slot_d[:, s, :], slot_d[:, s, :], -1.0, float(E),
                                                    ALU.mult, ALU.add).then_inc(chain, 1)
                            dve.wait_ge(exp_done, b + 1)
                            dve.wait_ge(chain, 4 * b + 1)
                            nc.vector.tensor_tensor(slot_g[:, s, :], slot_g[:, s, :], slot_d[:, s, :],
                                                    ALU.mult).then_inc(chain, 1)
                            dve.wait_ge(chain, 4 * b + 2)
                            nc.vector.tensor_tensor(slot_g[:, s, :], slot_g[:, s, :], fblk(acc[:, 1, :], b),
                                                    ALU.add).then_inc(chain, 1)
                            dve.sem_inc(deg_used, 1)
                            dve.wait_ge(chain, 4 * b + 3)
                            nc.vector.reciprocal(slot_g[:, s, :], slot_g[:, s, :]).then_inc(chain, 1)
                            dve.wait_ge(chain, 4 * b + 4)
                            dve.wait_ge(turned, b + 1)
                            nc.vector.tensor_tensor(slot_f[:, s, :], slot_g[:, s, :], fblk(acc[:, 0, :], b),
                                                    ALU.mult).then_inc(made, 1)
                            dve.wait_ge(made, b + 1)
                            dve.sem_inc(den_done, 1)

                        def add(b, s, i):
                            dve.wait_ge(turned, b + BS + 1)
                            dve.wait_ge(res_landed[s], i * 16 + 16)
                            nc.vector.tensor_tensor(xn[0:TILE, bass.ds(2 * b, 2), :],
                                                    bank[s][0:TILE, 0:2 * P].rearrange("p (t d) -> p t d", t=2),
                                                    slot_x[0:TILE, s], ALU.add).then_inc(added, 1)
                            dve.wait_ge(added, b + BS + 1)
                            for t in range(2):
                                nc.vector.bn_stats(
                                    stats[0:TILE, bass.ds(2 * b + t, 1), :].rearrange("p b s -> p (b s)"),
                                    xn[0:TILE, bass.ds(2 * b + t, 1), :].rearrange("p t d -> p (t d)"))
                        with dve.Fori(0, BITERS) as i:
                            if source == "attention":
                                for s in range(BS):
                                    divide(i * BS + s, s, i)
                            for s in range(BS):
                                add(i * BS + s, s, i)

        mean, rstd, ln_tmp = (sb(n, [P, NT, 1]) for n in ("mean", "rstd", "ln_tmp"))

        def layer_norm(xn, final):
            with phase() as new:
                chain, var_ready, std_ready, folded = new("chain"), new("var_ready"), new("std_ready"), new("folded")
                normed, saved, stored = new("normed"), new("saved"), new("stored")
                turned, kept, product, packed, packed_out = (
                    new(n) for n in ("turned", "kept", "product", "packed", "packed_out"))
                with nc.Block() as block:
                    @block.vector
                    def _(dve):
                        n = [0]

                        def link(ins):
                            n[0] += 1
                            ins.then_inc(chain, 1)
                            dve.wait_ge(chain, n[0])
                        even, odd = (stats[0:TILE, :, k:k + 1] for k in (1, 4))
                        m, r, t = (v[0:TILE] for v in (mean, rstd, ln_tmp))
                        link(nc.vector.tensor_tensor(m, even, odd, ALU.add))
                        link(nc.vector.tensor_tensor(t, even, odd, ALU.subtract))
                        link(nc.vector.tensor_scalar(m, m, 0.5, None, ALU.mult))
                        link(nc.vector.tensor_tensor(t, t, t, ALU.mult))
                        link(nc.vector.tensor_tensor(r, stats[0:TILE, :, 2:3], stats[0:TILE, :, 5:6], ALU.add))
                        link(nc.vector.tensor_scalar(t, t, 0.25, 1e-5, ALU.mult, ALU.add))
                        link(nc.vector.tensor_scalar(r, r, 1.0 / P, None, ALU.mult))
                        nc.vector.tensor_tensor(t, r, t, ALU.add).then_inc(var_ready, 1)
                        dve.wait_ge(std_ready, 1)
                        link(nc.vector.reciprocal(r, r))

                        def f(b, s):
                            dve.wait_ge(stored, b + 1)
                            if not final:
                                dve.wait_ge(turned, b + 1)
                            for t in range(2):
                                col = lambda v: v[0:TILE, bass.ds(2 * b + t, 1), :].rearrange("p t d -> p (t d)")
                                ins = nc.vector.tensor_scalar(slot_x[0:TILE, s, t, :], col(xn), col(mean), col(rstd),
                                                              ALU.subtract, ALU.mult)
                            ins.then_inc(normed, 1)
                        dve.sem_inc(normed, BS)
                        if final:
                            blocks(dve, f)
                            return
                        dve.sem_inc(kept, BS)

                        def keep(b, s):
                            dve.wait_ge(turned, b + BS + 1)
                            dve.wait_ge(product, b + 1)
                            nc.vector.tensor_copy(slot_f[:, s, :], bank[s][:, 0:BLK]).then_inc(kept, 1)
                        with dve.Fori(0, BITERS) as i:
                            for s in range(BS):
                                f(i * BS + s, s)
                            for s in range(BS):
                                keep(i * BS + s, s)

                    @block.scalar
                    def _(act):
                        act.wait_ge(var_ready, 1)
                        nc.scalar.activation(rstd[0:TILE], ln_tmp[0:TILE], ACT.Sqrt).then_inc(std_ready, 1)
                        if final:
                            return

                        act.sem_inc(packed, BS)

                        def pack(b, s):
                            act.wait_ge(product, b + BS + 1)
                            act.wait_ge(packed_out, b + 1)
                            h = bank[5 + s % 2]
                            nc.scalar.copy(slot_n[0:TILE, s].rearrange("p t d -> p (t d)"), h[0:TILE, 0:2 * ROW])
                            nc.scalar.copy(tgt_score[:, bass.ds(b * BLK, BLK)], bank[7][0:HEADS, 0:BLK]).then_inc(packed, 1)
                        blocks(act, pack)

                    @block.tensor
                    def _(pe):
                        if final:
                            return
                        pe.sem_inc(turned, BS)
                        pe.sem_inc(product, BS)

                        def turn(b, s):
                            pe.wait_ge(normed, b + BS + 1)
                            pe.wait_ge(kept, b + 1)
                            for t in range(2):
                                ins = nc.tensor.transpose(bank[s][:, t * TILE:(t + 1) * TILE], slot_x[0:TILE, s, t, :],
                                                          ident[0:TILE, 0:TILE])
                            ins.then_inc(turned, 1)

                        def project(b, s):
                            pe.wait_ge(kept, b + BS + 1)
                            pe.wait_ge(packed, b + BS)
                            h = bank[5 + s % 2]
                            for t in range(2):
                                nc.tensor.matmul(h[0:TILE, t * ROW:(t + 1) * ROW], slot_f[:, s, t * TILE:(t + 1) * TILE],
                                                 proj[:, 0:ROW], start=True, stop=True)
                            nc.tensor.matmul(bank[7][0:HEADS, 0:BLK], proj[:, ROW:ROW + HEADS], slot_f[:, s, :],
                                             start=True, stop=True).then_inc(product, 1)
                        with pe.Fori(0, BITERS) as i:
                            for s in range(BS):
                                turn(i * BS + s, s)
                            for s in range(BS):
                                project(i * BS + s, s)

                    @block.gpsimd
                    def _(pool):
                        if final:
                            store_rows(pool, lambda s: slot_x[0:TILE, s], out, normed, stored, LAYERS)
                            return
                        pool.sem_inc(stored, BS)
                        pool.sem_inc(packed_out, BS)
                        with pool.Fori(0, BITERS) as i:
                            for s in range(BS):
                                pool.wait_ge(normed, i * BS + (BS + s + 1))
                                pool.sem_inc(gather_go, 1)
                                pool.dma_start(node_rows(x1_rows)[:, bass.ds(2 * (i * BS + s), 2), :],
                                               slot_x[0:TILE, s]).then_inc(rows_out[s], 16)
                            for s in range(BS):
                                pool.wait_ge(packed, i * BS + (BS + s + 1))
                                pool.sem_inc(gather_go, 1)
                                pool.dma_start(node_rows(att_rows)[:, bass.ds(2 * (i * BS + s), 2), :],
                                               slot_n[0:TILE, s]).then_inc(table_out[s], 16)
                            for s in range(BS):
                                pool.wait_ge(rows_out[s], i * 16 + 16 * ((LAYERS - 1) * BITERS + 1))
                                pool.sem_inc(stored, 1)
                                pool.wait_ge(table_out[s], i * 16 + 16)
                                pool.sem_inc(packed_out, 1)

        lr = cut(0, 2, CHUNK)
        score = cut(1024, 2, CHUNK)
        prob = cut(2048, 2, CHUNK)
        msg = cut(3072, 2, CHUNK)
        z = sb("z", [P, 2, J * HEADS])
        z_wide = cut(4096, 2, CHUNK)
        onehot_wide = onehot_b[:, :].rearrange("p (d k) -> p d k", k=CHUNK)
        tgt_win = sb("tgt_win", [HEADS, 2, HEADS * WIN])
        top = sb("top", [P, 2, 3])
        diag = sb("diag", [P, 2, 2, WIN])
        new_top = sb("new_top", [P, 2, WIN])
        diff = sb("diff", [P, 2, 2, WIN])
        fac = sb("fac", [P, 2, 2, WIN])
        old_part, new_part = sb("old_part", [P, 2, WIN]), sb("new_part", [P, 2, WIN])
        att_rel = sb("att_rel", [P, J])

        def attention():
            RUN = LAYERS
            with phase() as new:
                names = ("prepped widened scored lrelued maxed topped exped probbed summed spread messaged summed_up "
                         "differed newtop factored merged parts gen_idx gen_free gen_rel_ready max_go relued").split()
                (prepped, widened, scored, lrelued, maxed, topped, exped, probbed, summed, spread_, messaged, summed_up,
                 differed, newtop, factored, merged, parts, gen_idx, gen_free, gen_rel_ready, max_go, relued) = (new(n) for n in names)
                with nc.Block() as block:
                    @block.gpsimd
                    def _(pool):
                        wide = pool.value_load(wide_int[0:1, 0:1], min_val=0, max_val=1)
                        with pool.If(wide < 1):
                            gather(pool, att_rows, ROW, RUN, messaged, 0)
                        with pool.Else():
                            with pool.Fori(0, CH) as c:
                                pool.wait_ge(gen_idx, c + 1)
                                pool.wait_ge(gen_free, c + 1)
                                pool.sem_inc(gather_go, 1)
                                gather_chunk(pool, 0, att_rows, ROW)

                    @block.vector
                    def _(dve):
                        wide = dve.value_load(wide_int[0:1, 0:1], min_val=0, max_val=1)

                        def col(arr, c):
                            return arr[:, bass.ds(c, 1), :].rearrange("p c j -> p (c j)")

                        def prepare(c, q, u, rel, base, landed, serial=False):
                            if not serial:
                                after(dve, summed_up, q - (SLOTS - 1))
                                after(dve, widened, q - 1)
                                after(dve, scored, q - 1)
                            nc.vector.tensor_tensor(onehot[:, u], bcast(iota_win, 1, J), bcast(rel, 2, WIN), ALU.is_equal)
                            nc.vector.tensor_tensor(
                                tgt_win[:, u % 2, :].rearrange("k (h n) -> k h n", n=WIN),
                                bcast(tgt_score[:, bass.ds(base, WIN)], 1, HEADS),
                                bcast(ident[0:HEADS, 0:HEADS], 2, WIN), ALU.mult)
                            dve.wait_ge(rows_landed[u], landed)
                            nc.vector.tensor_tensor(z[:, u % 2, :].rearrange("p (j h) -> p j h", h=HEADS),
                                                    rows[:, u, :, P:ROW],
                                                    edge_score[:, bass.ds(c, 1), :].rearrange("p c (j h) -> p (c j) h", h=HEADS),
                                                    ALU.add).then_inc(prepped, 1)

                        def maximum(q, u, serial=False):
                            d = u % 2
                            dve.wait_ge(lrelued, q + 1)
                            nc.vector.tensor_tensor(lr[:, d, :], bank[d][:, :], lr[:, d, :], ALU.max).then_inc(relued, 1)
                            if not serial:
                                after(dve, exped, q - 1)
                            dve.wait_ge(relued, q + 1)
                            dve.sem_inc(max_go, 1)
                            nc.vector.tensor_tensor_reduce(out=score[:, d, :], in0=lr[:, d, :], in1=bank[2 + d][:, :],
                                                           scale=1.0, scalar=0.0, op0=ALU.add, op1=ALU.max,
                                                           accum_out=top[:, d, 0:1]).then_inc(maxed, 1)
                            dve.wait_ge(maxed, q + 1)
                            nc.vector.tensor_scalar(top[:, d, 2:3], top[:, d, 0:1], -1.0, None, ALU.mult).then_inc(topped, 1)

                        def diagonals(q, u, serial=False):
                            d = u % 2
                            dve.wait_ge(exped, q + 1)
                            if not serial:
                                after(dve, spread_, q - 1)
                            nc.vector.tensor_tensor(diag[:, d], bcast(node_sel[:, :], 1, 2), bcast(top[:, d, 0:2], 2, WIN),
                                                    ALU.mult).then_inc(probbed, 1)

                        def weigh(q, u, serial=False):
                            d = u % 2
                            dve.wait_ge(spread_, q + 1)
                            if not serial:
                                after(dve, summed_up, q - 1)
                            nc.vector.tensor_tensor(
                                msg[:, d, :].rearrange("p (j h k) -> p j h k", j=J, h=HEADS),
                                rows[:, u, :, 0:P].rearrange("p j (h k) -> p j h k", h=HEADS),
                                bcast(bank[4 + d][:, 0:J * HEADS].rearrange("p (j h) -> p j h", h=HEADS), 3, HD),
                                ALU.mult).then_inc(messaged, 1)

                        def raise_top(q, u, base, serial=False):
                            d = u % 2
                            dve.wait_ge(spread_, q + 1)
                            if not serial:
                                after(dve, factored, q - 1)
                                after(dve, differed, q)
                            run = mid[:, bass.ds(base, WIN)]
                            nc.vector.tensor_tensor(new_top[:, d, :], run, bank[4 + d][:, 2 * WIN:3 * WIN],
                                                    ALU.max).then_inc(newtop, 1)
                            dve.wait_ge(newtop, q * 2 + 1)
                            nc.vector.tensor_tensor(diff[:, d, 0, :], run, new_top[:, d, :],
                                                    ALU.subtract).then_inc(newtop, 1)
                            nc.vector.tensor_tensor(diff[:, d, 1, :], bank[4 + d][:, 2 * WIN:3 * WIN], new_top[:, d, :],
                                                    ALU.subtract)
                            dve.wait_ge(newtop, q * 2 + 2)
                            nc.vector.tensor_tensor(run, run, bank[4 + d][:, 2 * WIN:3 * WIN], ALU.max).then_inc(differed, 1)

                        def merge(q, u, base, serial=False):
                            d = u % 2
                            dve.wait_ge(factored, q + 1)
                            dve.wait_ge(summed_up, q + 1)
                            if not serial:
                                after(dve, merged, q)
                            run = acc[:, :, bass.ds(base, WIN)]
                            nc.vector.tensor_tensor(old_part[:, :, :], run, bcast(fac[:, d, 0, :], 1, 2), ALU.mult)
                            nc.vector.tensor_tensor(new_part[:, :, :],
                                                    bank[6 + d][:, 0:2 * WIN].rearrange("p (k n) -> p k n", n=WIN),
                                                    bcast(fac[:, d, 1, :], 1, 2), ALU.mult).then_inc(parts, 1)
                            dve.wait_ge(parts, q + 1)
                            nc.vector.tensor_tensor(run, old_part[:, :, :], new_part[:, :, :], ALU.add).then_inc(merged, 1)

                        def base_of(c):
                            return dve.value_load(base_int[0:1, bass.ds(c, 1)], min_val=0, max_val=N - 1)

                        with dve.If(wide < 1):
                            dve.sem_inc(messaged, SLOTS)
                            chunks(dve, [
                                (lambda c, u, t: merge(c, u, base_of(c)), 5),
                                (lambda c, u, t: raise_top(c, u, base_of(c)), 4),
                                (lambda c, u, t: weigh(c, u), 3),
                                (lambda c, u, t: diagonals(c, u), 2),
                                (lambda c, u, t: prepare(c, c, u, col(dst_rel, c), base_of(c),
                                                         t * LAND + LAND * (RUN * ITERS + 1)), 0),
                                (lambda c, u, t: maximum(c, u), 1)])
                        with dve.Else():
                            dve.sem_inc(gen_free, 1)
                            with dve.Fori(0, CH) as c:
                                with dve.Fori(0, NWIN) as k:
                                    q = c * NWIN + k
                                    nc.vector.tensor_scalar(att_rel[:, :], col(dst_col, c), win_start[:, bass.ds(k, 1)],
                                                            None, ALU.subtract).then_inc(gen_rel_ready, 1)
                                    dve.wait_ge(gen_rel_ready, q + 1)
                                    prepare(c, q, 0, att_rel[:, :], k * WIN, c * LAND + LAND * (RUN * CH + 1), serial=True)
                                    maximum(q, 0, serial=True)
                                    diagonals(q, 0, serial=True)
                                    weigh(q, 0, serial=True)
                                    raise_top(q, 0, k * WIN, serial=True)
                                    merge(q, 0, k * WIN, serial=True)
                                    dve.wait_ge(merged, q + 1)
                                dve.sem_inc(gen_free, 1)

                    @block.scalar
                    def _(act):
                        wide = act.value_load(wide_int[0:1, 0:1], min_val=0, max_val=1)

                        def leaky(q, u, serial=False):
                            d = u % 2
                            act.wait_ge(scored, q + 1)
                            if not serial:
                                after(act, maxed, q - 1)
                            nc.scalar.activation(lr[:, d, :], bank[d][:, :], ACT.Copy, scale=0.2).then_inc(lrelued, 1)

                        def widen(q, u, serial=False):
                            d = u % 2
                            act.wait_ge(prepped, q + 1)
                            if not serial:
                                after(act, scored, q - 1)
                            nc.scalar.copy(z_wide[:, d, :].rearrange("p (k n) -> p k n", n=WIN), bcast(z[:, d, :], 2, WIN))
                            nc.scalar.activation(onehot_wide[:, d, :].rearrange("p (j h n) -> p j h n", j=J, h=HEADS),
                                                 bcast(onehot[:, u], 2, HEADS), ACT.Copy, scale=MASK,
                                                 bias=-MASK).then_inc(widened, 1)

                        def exp(q, u, serial=False):
                            d = u % 2
                            act.wait_ge(topped, q + 1)
                            if not serial:
                                after(act, spread_, q - 1)
                            nc.scalar.activation(prob[:, d, :], score[:, d, :], ACT.Exp, bias=top[:, d, 2:3],
                                                 accum_out=top[:, d, 1:2]).then_inc(exped, 1)

                        def factors(q, u, serial=False):
                            d = u % 2
                            act.wait_ge(differed, q + 1)
                            if not serial:
                                after(act, merged, q - 1)
                            nc.scalar.activation(fac[:, d].rearrange("p k n -> p (k n)"),
                                                 diff[:, d].rearrange("p k n -> p (k n)"), ACT.Exp).then_inc(factored, 1)

                        with act.If(wide < 1):
                            chunks(act, [
                                (lambda c, u, t: exp(c, u), 2),
                                (lambda c, u, t: factors(c, u), 4),
                                (lambda c, u, t: leaky(c, u), 1),
                                (lambda c, u, t: widen(c, u), 0),
                                (copy_idx(act, RUN), 0)])
                        with act.Else():
                            act.wait_ge(rows_landed[0], LAND * RUN * CH)
                            with act.Fori(0, CH) as c:
                                act.wait_ge(rows_landed[0], c * LAND + LAND * RUN * CH)
                                nc.scalar.copy(idx[:, 0, :], src_col[:, bass.ds(c, 1), :].rearrange("p c j -> p (c j)")
                                               ).then_inc(gen_idx, 1)
                                with act.Fori(0, NWIN) as k:
                                    q = c * NWIN + k
                                    widen(q, 0, serial=True)
                                    leaky(q, 0, serial=True)
                                    exp(q, 0, serial=True)
                                    factors(q, 0, serial=True)

                    @block.tensor
                    def _(pe):
                        wide = pe.value_load(wide_int[0:1, 0:1], min_val=0, max_val=1)

                        def scores(q, u, serial=False):
                            d = u % 2
                            pe.wait_ge(widened, q + 1)
                            if not serial:
                                after(pe, maxed, q - 1)
                            nc.tensor.matmul(bank[d][:, :], tgt_win[:, d, :], ones4[:, :], start=True, stop=False)
                            for j in range(J):
                                nc.tensor.matmul(bank[d][:, j * P:(j + 1) * P],
                                                 z_wide[:, d, j * P:(j + 1) * P], ident[:, :],
                                                 start=False, stop=(j == J - 1))
                            for j in range(J):
                                ins = nc.tensor.matmul(bank[2 + d][:, j * P:(j + 1) * P],
                                                       onehot_wide[:, d, j * P:(j + 1) * P], ident_b[:, :],
                                                       start=True, stop=True)
                            ins.then_inc(scored, 1)

                        def spread(q, u, serial=False):
                            d = u % 2
                            pe.wait_ge(probbed, q + 1)
                            if not serial:
                                after(pe, messaged, q + (SLOTS - 1))
                                after(pe, differed, q - 1)
                                after(pe, merged, q - 1)
                            for j in range(J):
                                nc.tensor.matmul(bank[4 + d][:, j * HEADS:(j + 1) * HEADS], prob[:, d, j * P:(j + 1) * P],
                                                 head_sel[:, :], start=True, stop=True)
                            nc.tensor.matmul(bank[4 + d][:, 2 * WIN:3 * WIN], head_blk[:, :], diag[:, d, 0, :],
                                             start=True, stop=True)
                            nc.tensor.matmul(bank[6 + d][:, WIN:2 * WIN], head_blk[:, :], diag[:, d, 1, :],
                                             start=True, stop=True).then_inc(spread_, 1)

                        def sum_up(q, u, serial=False):
                            d = u % 2
                            pe.wait_ge(messaged, q + 1 if serial else q + (SLOTS + 1))
                            for j in range(J):
                                ins = nc.tensor.matmul(bank[6 + d][:, 0:WIN], msg[:, d, j * P:(j + 1) * P],
                                                       onehot[:, u, j, :], start=(j == 0), stop=(j == J - 1))
                            ins.then_inc(summed_up, 1)

                        with pe.If(wide < 1):
                            chunks(pe, [(lambda c, u, t: sum_up(c, u), 3), (lambda c, u, t: spread(c, u), 2),
                                        (lambda c, u, t: scores(c, u), 0)])
                        with pe.Else():
                            with pe.Fori(0, CH * NWIN) as q:
                                scores(q, 0, serial=True)
                                spread(q, 0, serial=True)
                                sum_up(q, 0, serial=True)

        def clear_running():
            with nc.Block() as block:
                @block.vector
                def _(dve):
                    nc.vector.memset(acc[:, 0, :], 0.0)
                    nc.vector.memset(mid[:, :], 0.0)

                @block.gpsimd
                def _(pool):
                    pool.memset(acc[:, 1, :], 0.0)

        for layer in range(LAYERS):
            messages(layer)
            first_product(layer)
            second_product(layer)
            second_norm(layer)
            if layer < LAYERS - 1:
                third_norm(layer)
        xn = flat[:, 0:NT * P].rearrange("p (t d) -> p t d", d=P)
        to_rows("norm", xn, x, LAYERS - 1)
        layer_norm(xn, final=False)
        clear_running()
        attention()
        xn = edge_score[:, :, :].rearrange("p c k -> p (c k)")[:, 0:NT * P].rearrange("p (t d) -> p t d", d=P)
        to_rows("attention", xn, x1_rows)
        layer_norm(xn, final=True)


_INS = ["x", "src", "dst", "edge_attr_64", "edge_weight", "L0_gnn_W0s", "L0_gnn_W1s", "L0_gnn_bn1_g",
        "L0_gnn_bn1_b", "L0_gnn_bn2_g", "L0_gnn_bn2_b", "L0_gnn_bn3_g", "L0_gnn_bn3_b", "L1_gnn_W_node",
        "L1_gnn_W_edge", "L1_gnn_a"]


def kernel(**inputs):
    import concourse.bacc as _bacc
    from concourse.bass_utils import run_bass_kernel_spmd as _run

    nc = _bacc.Bacc("TRN2", target_bir_lowering=False, num_devices=1)
    arrays, args = {}, []
    for name in _INS:
        v = np.ascontiguousarray(inputs[name])
        arrays[f"in_{name}"] = v
        args.append(nc.dram_tensor(f"in_{name}", v.shape, mybir.dt.from_np(v.dtype), kind="ExternalInput").ap())
    out = nc.dram_tensor("out_0", inputs["x"].shape, F32, kind="ExternalOutput").ap()
    gnn_program(nc, *args[:7], args[7:13], *args[13:], out)
    return _run(nc, [arrays], core_ids=[0]).results[0]["out_0"]
```

```python
from contextlib import ExitStack, contextmanager

import numpy as np

import concourse.bass as bass
from concourse import mybir
from concourse.alu_op_type import AluOpType as ALU

F32, BF16 = mybir.dt.float32, mybir.dt.bfloat16
I32, I16 = mybir.dt.int32, mybir.dt.int16
ACT = mybir.ActivationFunctionType
AX = mybir.AxisListType.X

P = 128
J = 4
CHUNK = P * J
WIN = 32
HEADS, HD = 4, 32
ROW = P + HEADS
SLOTS = 8
LOOK = 4
TILE = 125
BLK = 2 * TILE
BS = 5
BN_EPS = 1e-5
FAR = float(1 << 20)
MASK = 2.0**64


def gnn_program(nc, x, src, dst, edge_attr, edge_weight, W0s, W1s, bns, W_node, W_edge, a, out):
    N, E = x.shape[0], src.shape[0]
    LAYERS, FE = W0s.shape[0], edge_attr.shape[1]
    CHR = -(-E // CHUNK)
    CH = -(-CHR // SLOTS) * SLOTS
    ITERS = CH // SLOTS
    GRP = -(-CH // P)
    FULL, TAIL = (CHR - 1) // P, (CHR - 1) % P
    LAST = E - (CHR - 1) * CHUNK
    NP = N + WIN
    NBLK, NT = N // BLK, N // TILE
    BITERS = NBLK // BS
    NWIN = -(-N // WIN)
    assert N % (BLK * BS) == 0 and FE * 2 == P and NP * 2 >= 4 * GRP * CHUNK

    ctx = ExitStack()
    with ctx:
        def sb(name, shape, dt=F32):
            return ctx.enter_context(nc.sbuf_tensor(name, shape, dt))

        def sem(name):
            return ctx.enter_context(nc.semaphore(name))

        def dram(name, shape, dt=F32):
            return nc.dram_tensor(name, shape, dt).ap()

        h_rows = dram("h_rows", (N, P))
        att_rows = dram("att_rows", (N, ROW))
        x1_rows = dram("x1_rows", (N, P))
        deg_row = dram("deg_row", (1, N))
        base_rows = dram("base_rows", (2 * GRP, P))

        src_col = sb("src_col", [P, CH + SLOTS, J], I16)
        dst_col = sb("dst_col", [P, CH, J], I16)
        dst_rel = sb("dst_rel", [P, CH, J])
        w_col = sb("w_col", [P, CH, J])
        edge_score = sb("edge_score", [P, CH, J * HEADS])
        acc = sb("acc", [P, 2, NP])
        mid = sb("mid", [P, NP])
        tgt_score = sb("tgt_score", [HEADS, NP])
        rows = sb("rows", [P, SLOTS, J, ROW])
        idx = sb("idx", [P, SLOTS, J], I32)
        base_int = sb("base_int", [1, GRP * P], I32)
        wide_int = sb("wide_int", [1, 1], I32)
        work = sb("work", [P, 5400])
        w0 = sb("w0", [P, LAYERS, P])
        w1 = sb("w1", [P, LAYERS, P])
        bn = sb("bn", [P, 6, LAYERS])
        proj = sb("proj", [P, ROW + HEADS])
        edge_fold = sb("edge_fold", [P, 2 * HEADS])
        ident = sb("ident", [P, P])
        ident_b = sb("ident_b", [P, P], BF16)
        ones_b = sb("ones_b", [P, P], BF16)
        ones4 = sb("ones4", [HEADS, CHUNK])
        iota_blk = sb("iota_blk", [P, BLK])
        iota_win = iota_blk[:, 0:WIN]
        head_sel = sb("head_sel", [P, HEADS])
        head_blk = sb("head_blk", [P, P])
        node_sel = sb("node_sel", [P, WIN])
        win_start = sb("win_start", [P, NWIN])
        blk_start = sb("blk_start", [P, NBLK])
        stats = sb("stats", [P, NT, 6])
        small = sb("small", [P, 16])
        onehot = sb("onehot", [P, SLOTS, J, WIN])
        onehot_b = sb("onehot_b", [P, SLOTS * J * WIN], BF16)

        bank = [ctx.enter_context(nc.psum_tensor(f"bank{i}", [P, 512], F32)) for i in range(8)]

        flat = acc[:, :, :].rearrange("p c n -> p (c n)")

        def cut(start, *shape, dt=F32, of=None):
            n = int(np.prod(shape))
            v = (work if of is None else of)[:, start:start + n]
            if dt != F32:
                v = v.bitcast(dt)
            if len(shape) == 2:
                v = v.rearrange("p (a b) -> p a b", b=shape[1])
            if len(shape) == 3:
                v = v.rearrange("p (a b c) -> p a b c", b=shape[1], c=shape[2])
            return v

        def bcast(v, axis, n):
            v = v.unsqueeze(axis)
            return v.broadcast_to([*v.shape[:axis], n, *v.shape[axis + 1:]])

        def after(eng, s, n):
            if not isinstance(n, int) or n >= 1:
                eng.wait_ge(s, n)

        def chunks(eng, stages, load_bases=None):
            def bases(start, n):
                return dict(enumerate(load_bases(start, n))) if load_bases else {}

            def run(f, c, k, turn, base):
                f(c, k % SLOTS, turn, *([base[k + LOOK]] if load_bases else []))

            base = bases(0, SLOTS)
            base = {k + LOOK: v for k, v in base.items()}
            for u in range(SLOTS):
                for f, lag in stages:
                    if u >= lag:
                        run(f, u - lag, u - lag, 0, base)
            with eng.Fori(1, ITERS) as i:
                base = bases(i * SLOTS - LOOK, SLOTS + LOOK)
                for u in range(SLOTS):
                    for f, lag in stages:
                        run(f, i * SLOTS + (u - lag), u - lag, i if u >= lag else i - 1, base)
            base = bases(CH - LOOK, LOOK)
            for u in range(max(lag for _, lag in stages)):
                for f, lag in stages:
                    if u < lag:
                        run(f, CH + u - lag, u - lag, ITERS - 1, base)

        s_load, s_pad, s_const = sem("s_load"), sem("s_pad"), sem("s_const")
        s_wload, s_dve, s_tr, s_trs = sem("s_wload"), sem("s_dve"), sem("s_tr"), sem("s_trs")
        s_act, s_base, s_baseld = sem("s_act"), sem("s_base"), sem("s_baseld")
        s_fold, s_basetr = sem("s_fold"), sem("s_basetr")

        raw_src = cut(0, GRP, CHUNK, dt=I32, of=flat)
        raw_min = cut(GRP * CHUNK, GRP, CHUNK, dt=I32, of=flat)
        raw_max = cut(2 * GRP * CHUNK, GRP, CHUNK, dt=I32, of=flat)
        raw_w = cut(3 * GRP * CHUNK, GRP, CHUNK, of=flat)
        scores_flat = edge_score[:, :, :].rearrange("p c k -> p (c k)")
        src_f = cut(0, GRP, CHUNK, of=scores_flat)
        dst_f = cut(GRP * CHUNK, GRP, CHUNK, of=scores_flat)
        iota_i = cut(0, BLK, dt=I32)
        base_bc = cut(250, GRP * P)
        base_f = cut(250 + GRP * P, 2 * GRP * P)
        bs = cut(1900, 2 * GRP)
        bs_t = cut(1920, P)
        win_i = cut(2600, NWIN, dt=I32)
        blk_i = cut(2900, NBLK, dt=I32)
        wn_nat, we_twice = cut(2200, P), cut(2360, 2, FE)
        a_col = cut(2500, 3)
        a_mask = cut(2520, 3, HEADS)
        spread = cut(2580, 8)

        by_chunk = [(raw_src, src), (raw_min, dst), (raw_max, dst), (raw_w, edge_weight)]
        n_loads = len(by_chunk) * ((FULL > 0) + (TAIL > 0) + 1)
        with nc.Block() as block:
            @block.sync
            def _(sp):
                sp.wait_ge(s_pad, 4)
                for raw, d in by_chunk:
                    if FULL:
                        sp.dma_start(raw[:, 0:FULL, :], d[0:FULL * P * CHUNK].rearrange(
                            "(g r c) -> r g c", r=P, c=CHUNK)).then_inc(s_load, 16)
                    if TAIL:
                        sp.dma_start(raw[0:TAIL, FULL, :], d[FULL * P * CHUNK:(CHR - 1) * CHUNK].rearrange(
                            "(r c) -> r c", c=CHUNK)).then_inc(s_load, 16)
                    sp.dma_start(raw[TAIL:TAIL + 1, FULL, 0:LAST],
                                 d[(CHR - 1) * CHUNK:E].rearrange("(r c) -> r c", r=1)).then_inc(s_load, 16)
                sp.wait_ge(s_basetr, 2)
                sp.dma_start(base_rows, bs_t[0:2 * GRP, :]).then_inc(s_base, 16)
                sp.wait_ge(s_base, 16)
                row = base_rows.rearrange("(o g) r -> o (g r)", o=1)
                sp.dma_start(base_f[0:1, :], row).then_inc(s_baseld, 16)
                sp.dma_start(base_bc[:, :], row[:, 0:GRP * P].broadcast_to([P, GRP * P])).then_inc(s_baseld, 16)

            @block.scalar
            def _(act):
                act.dma_start(w0[:, :, :], W0s.rearrange("l i o -> i l o")).then_inc(s_wload, 16)
                act.dma_start(w1[:, :, :], W1s.rearrange("l i o -> i l o")).then_inc(s_wload, 16)
                for k, v in enumerate(bns):
                    act.dma_start(bn[:, k, :], v.rearrange("l d -> d l"),
                                  allow_slow_non_contiguous=True).then_inc(s_wload, 16)
                act.dma_start(wn_nat, W_node).then_inc(s_wload, 16)
                for k in range(2):
                    act.dma_start(we_twice[:, k, :], W_edge).then_inc(s_wload, 16)
                for h in range(HEADS):
                    act.dma_start(a_col[h * HD:(h + 1) * HD, :], a[h, :].rearrange("(s k) -> k s", k=HD),
                                  allow_slow_non_contiguous=True).then_inc(s_wload, 16)

            @block.gpsimd
            def _(pool):
                pool.memset(raw_src[:, FULL:, :], 0).then_inc(s_pad, 1)
                pool.memset(raw_min[:, FULL:, :], int(FAR)).then_inc(s_pad, 1)
                pool.memset(raw_max[:, FULL:, :], -1).then_inc(s_pad, 1)
                pool.memset(raw_w[:, FULL:, :], 0.0).then_inc(s_pad, 1)
                pool.memset(ident[:, :], 0.0).then_inc(s_const, 1)
                pool.memset(head_sel[:, :], 1.0).then_inc(s_const, 1)
                pool.iota(blk_i, pattern=[[BLK, NBLK]], base=0, channel_multiplier=0)
                pool.iota(iota_i, pattern=[[1, BLK]], base=0, channel_multiplier=0).then_inc(s_const, 1)
                pool.iota(win_i, pattern=[[WIN, NWIN]], base=0, channel_multiplier=0).then_inc(s_const, 1)
                pool.wait_ge(s_const, 2)
                pool.affine_select(out=ident[:, :], in_=ident[:, :], compare_op=ALU.not_equal, fill=1.0,
                                   base=0, pattern=[[-1, P]], channel_multiplier=1).then_inc(s_const, 1)
                pool.affine_select(out=head_sel[:, :], in_=head_sel[:, :], compare_op=ALU.is_ge, fill=0.0,
                                   base=0, pattern=[[-HD, HEADS]], channel_multiplier=1).then_inc(s_const, 1)
                pool.wait_ge(s_const, 6)
                pool.affine_select(out=head_sel[:, :], in_=head_sel[:, :], compare_op=ALU.is_ge, fill=0.0,
                                   base=HD - 1, pattern=[[HD, HEADS]], channel_multiplier=-1).then_inc(s_const, 1)
                pool.memset(ones_b[:, :], 1.0).then_inc(s_const, 1)
                pool.memset(ones4[:, :], 1.0).then_inc(s_const, 1)
                pool.memset(tgt_score[:, :], 0.0).then_inc(s_const, 1)
                pool.memset(mid[:, :], 0.0).then_inc(s_const, 1)
                pool.memset(edge_fold[:, :], 0.0).then_inc(s_const, 1)

            @block.vector
            def _(dve):
                done = [0]

                def link(ins):
                    done[0] += 1
                    ins.then_inc(s_dve, 1)
                    dve.wait_ge(s_dve, done[0])

                dve.wait_ge(s_const, 12)
                nc.vector.tensor_copy(iota_blk[:, :], iota_i)
                nc.vector.tensor_copy(blk_start[:, :], blk_i)
                nc.vector.tensor_copy(win_start[:, :], win_i)
                nc.vector.tensor_copy(ident_b[:, :], ident[:, :])
                nc.vector.tensor_copy(head_blk[:, :].rearrange("p (h k) -> p h k", h=HEADS),
                                      bcast(head_sel[:, :], 2, HD))
                nc.vector.tensor_reduce(node_sel[:, :], ident[:, :].rearrange("p (h n) -> p n h", h=HEADS),
                                        AX, ALU.add)
                dve.wait_ge(s_load, 16 * n_loads)
                link(nc.vector.tensor_copy(src_f, raw_src))
                link(nc.vector.tensor_copy(dst_f, raw_max))
                link(nc.vector.tensor_reduce(spread[:, 0:GRP], raw_min, AX, ALU.min))
                link(nc.vector.tensor_reduce(spread[:, 4:4 + GRP], raw_max, AX, ALU.max))
                link(nc.vector.tensor_scalar(bs[:, 0:GRP], spread[:, 0:GRP], float(N - 1), None, ALU.min))
                link(nc.vector.tensor_tensor(bs[:, GRP:], spread[:, 4:4 + GRP], bs[:, 0:GRP], ALU.subtract))
                dve.wait_ge(s_wload, 16 * 15)
                link(nc.vector.tensor_tensor(a_mask, bcast(a_col, 2, HEADS), bcast(head_sel[:, :], 1, 3), ALU.mult))
                k = 0
                for g in range(GRP):
                    n = min(P, CH - g * P)
                    for what in range(3):
                        for j in range(J):
                            k += 1
                            dve.wait_ge(s_tr, k)
                            t = bank[k % 4][:, 0:n]
                            if what == 0:
                                nc.vector.tensor_copy(src_col[:, g * P:g * P + n, j], t).then_inc(s_trs, 1)
                            elif what == 1:
                                nc.vector.tensor_copy(dst_col[:, g * P:g * P + n, j], t)
                                nc.vector.tensor_copy(dst_rel[:, g * P:g * P + n, j], t).then_inc(s_trs, 1)
                            else:
                                nc.vector.tensor_copy(w_col[:, g * P:g * P + n, j], t).then_inc(s_trs, 1)
                dve.wait_ge(s_trs, k)
                nc.vector.tensor_copy(src_col[:, CH:CH + SLOTS, :], src_col[:, 0:SLOTS, :])
                dve.wait_ge(s_basetr, 1)
                nc.vector.tensor_copy(bs_t[0:2 * GRP, :], bank[4][0:2 * GRP, 0:P]).then_inc(s_basetr, 1)
                dve.wait_ge(s_baseld, 32)
                nc.vector.tensor_copy(base_int[:, :], base_f[0:1, 0:GRP * P])
                link(nc.vector.tensor_reduce(small[0:1, 0:1], base_f[0:1, GRP * P:], AX, ALU.max))
                nc.vector.tensor_scalar(wide_int[:, :], small[0:1, 0:1], float(WIN), None, ALU.is_ge)
                nc.vector.tensor_tensor(dst_rel[:, :, :], dst_rel[:, :, :],
                                        bcast(base_bc[:, 0:CH], 2, J), ALU.subtract)
                dve.wait_ge(s_fold, 1)
                nc.vector.tensor_copy(proj[:, 0:P], bank[5][:, 0:P])
                nc.vector.tensor_scalar(proj[:, P:ROW], bank[5][:, P:ROW], 1 / MASK, None, ALU.mult)
                nc.vector.tensor_copy(proj[:, ROW:ROW + HEADS], bank[5][:, ROW:ROW + HEADS])
                for k in range(2):
                    nc.vector.tensor_scalar(edge_fold[k * FE:(k + 1) * FE, k * HEADS:(k + 1) * HEADS],
                                            bank[6][k * FE:(k + 1) * FE, 0:HEADS], 1 / MASK, None, ALU.mult)

            @block.tensor
            def _(pe):
                pe.wait_ge(s_const, 12)
                pe.wait_ge(s_load, 16 * n_loads)
                pe.wait_ge(s_dve, 2)
                k = 0
                for g in range(GRP):
                    n = min(P, CH - g * P)
                    for f in (src_f, dst_f, raw_w):
                        for j in range(J):
                            k += 1
                            if k > 4:
                                pe.wait_ge(s_trs, k - 4)
                            nc.tensor.transpose(bank[k % 4][:, 0:P], f[:, g, j::J], ident[:, :]).then_inc(s_tr, 1)
                pe.wait_ge(s_dve, 7)
                nc.tensor.transpose(bank[4][0:2 * GRP, 0:P], bs, ident[:, :]).then_inc(s_basetr, 1)
                nc.tensor.transpose(bank[5][:, 0:P], wn_nat, ident[:, :])
                for k in range(2):
                    nc.tensor.matmul(bank[5][:, P + k * HEADS:P + (k + 1) * HEADS], wn_nat, a_mask[:, k, :],
                                     start=True, stop=True)
                nc.tensor.matmul(bank[6][:, 0:HEADS], we_twice.rearrange("p k f -> p (k f)"), a_mask[:, 2, :],
                                 start=True, stop=True).then_inc(s_fold, 1)

        @contextmanager
        def phase():
            with ExitStack() as st:
                held = []

                def new(name, n=None):
                    got = [st.enter_context(nc.semaphore(name if n is None else f"{name}{k}")) for k in range(n or 1)]
                    held.extend(got)
                    return got if n else got[0]
                yield new
                nums = sorted(h.num for h in held)
                with nc.Block() as block:
                    @block.sync
                    def _(sp):
                        start = nums[0]
                        for k, num in enumerate(nums):
                            if k + 1 == len(nums) or nums[k + 1] != num + 1:
                                sp.sem_clear(range(start, num + 1))
                                start = nums[k + 1] if k + 1 < len(nums) else None

        def blocks(eng, f):
            with eng.Fori(0, BITERS) as i:
                for s in range(BS):
                    f(i * BS + s, s)

        def node_rows(table):
            return table.rearrange("(t p) d -> p t d", p=TILE)

        slot_x = cut(0, BS, 2, P)
        slot_f = cut(1280, BS, BLK)
        slot_n = cut(2560, BS, 2, ROW)
        slot_g = cut(2560, BS, BLK)
        slot_d = cut(3900, BS, BLK)

        def fblk(arr, b):
            return arr[:, bass.ds(b * BLK, BLK)]

        with phase() as new:
            x_landed, x_turned, x_saved, zeroed = new("x_landed", BS), new("x_turned"), new("x_saved"), new("zeroed")
            with nc.Block() as block:
                @block.sync
                def _(sp):
                    def load(b, s):
                        sp.wait_ge(x_turned, b + 1)
                        sp.dma_start(slot_x[0:TILE, s], node_rows(x)[:, bass.ds(2 * b, 2), :]).then_inc(x_landed[s], 16)
                    blocks(sp, load)

                @block.tensor
                def _(pe):
                    pe.sem_inc(x_turned, BS)

                    def turn(b, s, i=None):
                        pe.wait_ge(x_saved, b + 1)
                        for t in range(2):
                            ins = nc.tensor.transpose(bank[s][:, t * TILE:(t + 1) * TILE], slot_x[0:TILE, s, t, :],
                                                      ident[0:TILE, 0:TILE])
                        ins.then_inc(x_turned, 1)
                    with pe.Fori(0, BITERS) as i:
                        for s in range(BS):
                            pe.wait_ge(x_landed[s], i * 16 + 16)
                            turn(i * BS + s, s)

                @block.scalar
                def _(act):
                    act.sem_inc(x_saved, BS)

                    def save(b, s):
                        act.wait_ge(x_turned, b + BS + 1)
                        nc.scalar.copy(acc[:, 0, bass.ds(b * BLK, BLK)], bank[s][:, 0:BLK]).then_inc(x_saved, 1)
                    blocks(act, save)

                @block.vector
                def _(dve):
                    nc.vector.memset(acc[:, 0, N:NP], 0.0)
                    nc.vector.memset(acc[:, 1, :], 0.0)

        rows_landed = [sem(f"rows_landed{u}") for u in range(SLOTS)]
        idx_copied, rows_done, gather_go = sem("idx_copied"), sem("rows_done"), sem("gather_go")
        onehot_ready, acc_added = sem("onehot_ready"), sem("acc_added")
        LAND = 16 * J

        def gather_chunk(pool, u, table, width):
            for j in range(J):
                pool.indirect_dma_start(
                    out=rows[:, u, j, 0:width], out_offset=None, in_=table,
                    in_offset=bass.IndirectOffsetOnAxis(ap=idx[:, u, j:j + 1], axis=0),
                ).then_inc(rows_landed[u], 16)

        def gather(pool, table, width, run, freed, freed_base):
            with pool.Fori(0, ITERS) as i:
                for u in range(SLOTS):
                    pool.wait_ge(idx_copied, i * SLOTS + (run * CH + u + 1))
                    pool.wait_ge(freed, i * SLOTS + (freed_base + u + 1))
                    pool.sem_inc(gather_go, 1)
                    gather_chunk(pool, u, table, width)

        def copy_idx(act, run):
            def f(c, u, turn):
                act.wait_ge(rows_landed[u], turn * LAND + LAND * (run * ITERS + 1))
                nc.scalar.copy(idx[:, u, :], src_col[:, bass.ds(c + SLOTS, 1), :]
                               .rearrange("p c j -> p (c j)")).then_inc(idx_copied, 1)
            return f

        ea_slot = cut(0, SLOTS, J * FE)
        ea_turned_sb = cut(SLOTS * J * FE, 2, J * FE)
        gen_onehot = cut(2560, J, BLK)
        gen_plain = cut(3560, J, BLK // 2)
        gen_rel = cut(4100, J)
        gen_plain = gen_plain.rearrange("p j n -> p (j n)").bitcast(BF16).rearrange("p (j n) -> p j n", n=BLK)

        with nc.Block() as block:
            @block.scalar
            def _(act):
                for u in range(SLOTS):
                    nc.scalar.copy(idx[:, u, :], src_col[:, u, :]).then_inc(idx_copied, 1)

            @block.tensor
            def _(pe):
                pe.sem_inc(rows_done, SLOTS)

            @block.vector
            def _(dve):
                dve.sem_inc(acc_added, 2)

        def load_bases(start, n):
            return nc.values_load_multi_w_load_instructions(
                base_int[0:1, bass.ds(start, n)], engines=[mybir.EngineType.DVE], min_val=0, max_val=N - 1)[1]

        def messages(layer):
            table = x if layer == 0 else h_rows
            plain = onehot_b[:, :].rearrange("p (u j n) -> p u j n", u=SLOTS, j=J)
            first = layer == 0
            done, comps = layer * CH, 2 if first else 1
            with phase() as new:
                if first:
                    ea_landed, ea_under, ea_turned = new("ea_landed", SLOTS), new("ea_under"), new("ea_turned")
                    eat_saved, score_done, score_saved = new("eat_saved"), new("score_done"), new("score_saved")
                gen_ready, gen_summed, gen_added = new("gen_ready"), new("gen_summed"), new("gen_added")
                gen_rel_ready, gen_idx, gen_free = new("gen_rel_ready"), new("gen_idx"), new("gen_free")

                with nc.Block() as block:
                    @block.sync
                    def _(sp):
                        if not first:
                            return
                        per_chunk = edge_attr[0:(CHR - 1) * CHUNK, :].rearrange("(c p j) f -> p c (j f)", p=P, j=J)
                        with sp.Fori(0, ITERS - 1) as i:
                            for u in range(SLOTS):
                                sp.wait_ge(ea_turned, i * SLOTS + u + 1)
                                sp.dma_start(ea_slot[:, u, :], per_chunk[:, bass.ds(i * SLOTS + u, 1), :]
                                             .rearrange("p c f -> p (c f)")).then_inc(ea_landed[u], 16)
                        for u in range(SLOTS):
                            c = CH - SLOTS + u
                            sp.wait_ge(ea_turned, c + 1)
                            if c < CHR - 1:
                                sp.dma_start(ea_slot[:, u, :], per_chunk[:, c, :]).then_inc(ea_landed[u], 16)
                                continue
                            if c > CHR - 1:
                                sp.dma_start(ea_slot[:, u, :], per_chunk[:, 0, :]).then_inc(ea_landed[u], 16)
                                continue
                            sp.dma_start(ea_slot[:, u, :], per_chunk[:, 0, :]).then_inc(ea_under, 16)
                            sp.wait_ge(ea_under, 16)
                            n, tail = 1, edge_attr[(CHR - 1) * CHUNK:E, :]
                            full, part = LAST // J, LAST % J
                            if full:
                                sp.dma_start(ea_slot[0:full, u, :], tail[0:full * J, :].rearrange(
                                    "(p j) f -> p (j f)", j=J)).then_inc(ea_under, 16)
                                n += 1
                            if part:
                                sp.dma_start(ea_slot[full:full + 1, u, 0:part * FE], tail[full * J:LAST, :]
                                             .rearrange("(p j) f -> p (j f)", p=1)).then_inc(ea_under, 16)
                                n += 1
                            sp.wait_ge(ea_under, 16 * n)
                            sp.sem_inc(ea_landed[u], 16)

                    @block.gpsimd
                    def _(pool):
                        wide = pool.value_load(wide_int[0:1, 0:1], min_val=0, max_val=1)
                        with pool.If(wide < 1):
                            gather(pool, table, P, layer, rows_done, done)
                        with pool.Else():
                            with pool.Fori(0, CH) as c:
                                pool.wait_ge(gen_idx, c + 1)
                                pool.wait_ge(gen_free, c + 1)
                                pool.sem_inc(gather_go, 1)
                                gather_chunk(pool, 0, table, P)

                    @block.vector
                    def _(dve):
                        wide = dve.value_load(wide_int[0:1, 0:1], min_val=0, max_val=1)

                        def select(c, u, turn):
                            dve.wait_ge(rows_done, c + (done + 1))
                            for j in range(J):
                                col = lambda arr: arr[:, bass.ds(c, 1), j:j + 1].rearrange("p c j -> p (c j)")
                                ins = nc.vector.tensor_scalar(onehot[:, u, j, :], iota_win[:, :], col(dst_rel),
                                                              col(w_col), ALU.is_equal, ALU.mult)
                            if first:
                                ins = nc.vector.tensor_tensor(
                                    plain[:, u], bcast(iota_win[:, :], 1, J),
                                    bcast(dst_rel[:, bass.ds(c, 1), :].rearrange("p c j -> p (c j)"), 2, WIN),
                                    ALU.is_equal)
                            ins.then_inc(onehot_ready, 1)

                        def add(c, u, turn):
                            b = dve.value_load(base_int[0:1, bass.ds(c, 1)], min_val=0, max_val=N - 1)
                            dve.wait_ge(rows_done, c + (SLOTS + done + 1))
                            dve.wait_ge(acc_added, c + (2 + done))
                            win = acc[:, 0:comps, bass.ds(b, WIN)]
                            nc.vector.tensor_tensor(
                                win, win, bank[u % 2][:, 0:comps * WIN].rearrange("p (k n) -> p k n", n=WIN),
                                ALU.add).then_inc(acc_added, 1)

                        with dve.If(wide < 1):
                            chunks(dve, [(add, 2), (select, 0)])
                        with dve.Else():
                            dve.sem_inc(gen_free, 1)
                            with dve.Fori(0, CH) as c:
                                with dve.Fori(0, NBLK) as k:
                                    q = c * NBLK + k
                                    nc.vector.tensor_scalar(
                                        gen_rel, dst_col[:, bass.ds(c, 1), :].rearrange("p c j -> p (c j)"),
                                        blk_start[:, bass.ds(k, 1)], None, ALU.subtract).then_inc(gen_rel_ready, 1)
                                    dve.wait_ge(gen_rel_ready, q + 1)
                                    for j in range(J):
                                        wj = w_col[:, bass.ds(c, 1), j:j + 1].rearrange("p c j -> p (c j)")
                                        ins = nc.vector.tensor_scalar(gen_onehot[:, j, :], iota_blk[:, :],
                                                                      gen_rel[:, j:j + 1], wj, ALU.is_equal, ALU.mult)
                                    if first:
                                        ins = nc.vector.tensor_tensor(gen_plain, bcast(iota_blk[:, :], 1, J),
                                                                      bcast(gen_rel, 2, BLK), ALU.is_equal)
                                    ins.then_inc(gen_ready, 1)
                                    dve.wait_ge(gen_summed, q + 1)
                                    for comp in range(comps):
                                        win = acc[:, comp, bass.ds(k * BLK, BLK)]
                                        ins = nc.vector.tensor_tensor(win, win, bank[comp][:, 0:BLK], ALU.add)
                                    ins.then_inc(gen_added, 1)
                                    dve.wait_ge(gen_added, q + 1)
                                dve.sem_inc(gen_free, 1)

                    @block.tensor
                    def _(pe):
                        wide = pe.value_load(wide_int[0:1, 0:1], min_val=0, max_val=1)
                        if first:
                            pe.sem_inc(ea_turned, SLOTS)
                            pe.sem_inc(score_done, 2)

                        def add_up(c, u, turn):
                            pe.wait_ge(onehot_ready, c + (done + 1))
                            pe.wait_ge(acc_added, c + (done + 1))
                            pe.wait_ge(rows_landed[u], turn * LAND + LAND * (layer * ITERS + 1))
                            for j in range(J):
                                ins = nc.tensor.matmul(bank[u % 2][:, 0:WIN], rows[:, u, j, 0:P],
                                                       onehot[:, u, j, :], start=(j == 0), stop=(j == J - 1))
                            if first:
                                for j in range(J):
                                    ins = nc.tensor.matmul(bank[u % 2][:, WIN:2 * WIN], ones_b[:, :],
                                                           plain[:, u, j, :], start=(j == 0), stop=(j == J - 1))
                            ins.then_inc(rows_done, 1)

                        def turn_attr(c, u, turn):
                            pe.wait_ge(ea_landed[u], turn * 16 + 16)
                            pe.wait_ge(eat_saved, c + 1)
                            for k in range(J // 2):
                                ins = nc.tensor.transpose(bank[2 + u % 2][:, k * P:(k + 1) * P],
                                                          ea_slot[:, u, k * P:(k + 1) * P], ident[:, :])
                            ins.then_inc(ea_turned, 1)

                        def score_attr(c, u, turn):
                            pe.wait_ge(eat_saved, c + 3)
                            pe.wait_ge(score_saved, c + 1)
                            for k in range(J // 2):
                                ins = nc.tensor.matmul(bank[4 + u % 2][:, k * 2 * HEADS:(k + 1) * 2 * HEADS],
                                                       ea_turned_sb[:, u % 2, k * P:(k + 1) * P], edge_fold[:, :],
                                                       start=True, stop=True)
                            ins.then_inc(score_done, 1)

                        attr = [(turn_attr, 0), (score_attr, 1)] if first else []
                        with pe.If(wide < 1):
                            chunks(pe, attr + [(add_up, 0)])
                        with pe.Else():
                            if first:
                                chunks(pe, attr)
                            with pe.Fori(0, CH) as c:
                                with pe.Fori(0, NBLK) as k:
                                    pe.wait_ge(rows_landed[0], c * LAND + LAND * (layer * CH + 1))
                                    pe.wait_ge(gen_ready, c * NBLK + k + 1)
                                    for j in range(J):
                                        ins = nc.tensor.matmul(bank[0][:, 0:BLK], rows[:, 0, j, 0:P],
                                                               gen_onehot[:, j, :], start=(j == 0), stop=(j == J - 1))
                                    if first:
                                        for j in range(J):
                                            ins = nc.tensor.matmul(bank[1][:, 0:BLK], ones_b[:, :], gen_plain[:, j, :],
                                                                   start=(j == 0), stop=(j == J - 1))
                                    ins.then_inc(gen_summed, 1)

                    @block.scalar
                    def _(act):
                        wide = act.value_load(wide_int[0:1, 0:1], min_val=0, max_val=1)
                        if first:
                            act.sem_inc(eat_saved, 2)
                            act.sem_inc(score_saved, 2)

                        def save_turned(c, u, turn):
                            act.wait_ge(ea_turned, c + (SLOTS + 1))
                            act.wait_ge(score_done, c + 1)
                            nc.scalar.copy(ea_turned_sb[:, u % 2, :], bank[2 + u % 2][:, 0:J * FE]).then_inc(eat_saved, 1)

                        def save_score(c, u, turn):
                            act.wait_ge(score_done, c + 3)
                            nc.scalar.copy(edge_score[:, bass.ds(c, 1), :].rearrange("p c k -> p (c k)"),
                                           bank[4 + u % 2][:, 0:J * HEADS]).then_inc(score_saved, 1)

                        attr = [(save_turned, 0), (save_score, 1)] if first else []
                        with act.If(wide < 1):
                            chunks(act, attr + [(copy_idx(act, layer), 0)])
                        with act.Else():
                            if first:
                                chunks(act, attr)
                            general_idx(act, layer, gen_idx)

        def general_idx(act, run, gen_idx):
            act.wait_ge(idx_copied, SLOTS)
            if run:
                act.wait_ge(rows_landed[0], LAND * run * CH)
            nc.scalar.copy(idx[:, 0, :], src_col[:, 0, :]).then_inc(gen_idx, 1)
            with act.Fori(1, CH) as c:
                act.wait_ge(rows_landed[0], c * LAND + LAND * run * CH)
                nc.scalar.copy(idx[:, 0, :], src_col[:, bass.ds(c, 1), :].rearrange("p c j -> p (c j)")).then_inc(gen_idx, 1)

        bn_scale, bn_shift = sb("bn_scale", [P, 1]), sb("bn_shift", [P, 1])

        def fold_norm(dve, which, layer, var_ready, std_ready, chain, folded):
            n = [0]

            def link(ins):
                n[0] += 1
                ins.then_inc(chain, 1)
                dve.wait_ge(chain, n[0])
            g, b = (bn[:, 2 * which + k, layer:layer + 1] for k in range(2))
            link(nc.vector.bn_aggr(small[:, 0:2], stats[:, 0:NBLK, :].rearrange("p b s -> p (b s)")))
            nc.vector.tensor_scalar(small[:, 2:3], small[:, 1:2], BN_EPS, None, ALU.add).then_inc(var_ready, 1)
            dve.wait_ge(std_ready, 1)
            link(nc.vector.reciprocal(small[:, 4:5], small[:, 3:4]))
            link(nc.vector.tensor_tensor(bn_scale[:, :], small[:, 4:5], g, ALU.mult))
            link(nc.vector.tensor_tensor(small[:, 5:6], small[:, 0:1], bn_scale[:, :], ALU.mult))
            nc.vector.tensor_tensor(bn_shift[:, :], b, small[:, 5:6], ALU.subtract).then_inc(folded, 1)

        def std(act, var_ready, std_ready):
            act.wait_ge(var_ready, 1)
            nc.scalar.activation(small[:, 3:4], small[:, 2:3], ACT.Sqrt).then_inc(std_ready, 1)

        def first_product(layer):
            with phase() as new:
                product, saved, deg_out = new("product"), new("saved"), new("deg_out")
                with nc.Block() as block:
                    @block.sync
                    def _(sp):
                        if layer == 0:
                            sp.dma_start(deg_row, acc[0:1, 1, 0:N]).then_inc(deg_out, 16)
                            sp.wait_ge(deg_out, 16)

                    @block.tensor
                    def _(pe):
                        def f(b, s):
                            pe.wait_ge(saved, b + 1)
                            nc.tensor.matmul(bank[s][:, 0:BLK], w0[:, layer, :], fblk(acc[:, 0, :], b),
                                             start=True, stop=True).then_inc(product, 1)
                        blocks(pe, f)

                    @block.scalar
                    def _(act):
                        act.sem_inc(saved, BS)

                        def f(b, s):
                            act.wait_ge(product, b + 1)
                            nc.scalar.copy(fblk(mid, b), bank[s][:, 0:BLK]).then_inc(saved, 1)
                        blocks(act, f)

                    @block.vector
                    def _(dve):
                        def f(b, s):
                            dve.wait_ge(saved, b + BS + 1)
                            nc.vector.bn_stats(stats[:, bass.ds(b, 1), :].rearrange("p b s -> p (b s)"), fblk(mid, b))
                        blocks(dve, f)

        def second_product(layer):
            with phase() as new:
                var_ready, std_ready, chain, folded = new("var_ready"), new("std_ready"), new("chain"), new("folded")
                product, saved, normed, save_go = (new(n) for n in ("product", "saved", "normed", "save_go"))
                with nc.Block() as block:
                    @block.tensor
                    def _(pe):
                        def f(b, s):
                            pe.wait_ge(normed, b + 1)
                            pe.wait_ge(saved, b + 1)
                            nc.tensor.matmul(bank[s][:, 0:BLK], w1[:, layer, :], fblk(mid, b),
                                             start=True, stop=True).then_inc(product, 1)
                        blocks(pe, f)

                    @block.scalar
                    def _(act):
                        act.sem_inc(saved, BS)
                        std(act, var_ready, std_ready)
                        act.wait_ge(folded, 1)
                        with act.Fori(0, BITERS) as i:
                            for s in range(BS):
                                nc.scalar.activation(fblk(mid, i * BS + s), fblk(mid, i * BS + s), ACT.Relu,
                                                     bias=bn_shift[:, :], scale=bn_scale[:, :]).then_inc(normed, 1)
                            for s in range(BS):
                                act.wait_ge(product, i * BS + s + 1)
                                act.sem_inc(save_go, 1)
                                nc.scalar.copy(fblk(mid, i * BS + s), bank[s][:, 0:BLK]).then_inc(saved, 1)

                    @block.vector
                    def _(dve):
                        fold_norm(dve, 0, layer, var_ready, std_ready, chain, folded)

                        def f(b, s):
                            dve.wait_ge(saved, b + BS + 1)
                            nc.vector.bn_stats(stats[:, bass.ds(b, 1), :].rearrange("p b s -> p (b s)"), fblk(mid, b))
                        blocks(dve, f)

        def second_norm(layer):
            with phase() as new:
                var_ready, std_ready, chain, folded = new("var_ready"), new("std_ready"), new("chain"), new("folded")
                normed = new("normed")
                with nc.Block() as block:
                    @block.scalar
                    def _(act):
                        std(act, var_ready, std_ready)
                        act.wait_ge(folded, 1)

                        def f(b, s):
                            nc.scalar.activation(fblk(mid, b), fblk(mid, b), ACT.Relu, bias=bn_shift[:, :],
                                                 scale=bn_scale[:, :]).then_inc(normed, 1)
                        blocks(act, f)

                    @block.vector
                    def _(dve):
                        fold_norm(dve, 1, layer, var_ready, std_ready, chain, folded)

                        def f(b, s):
                            dve.wait_ge(normed, b + 1)
                            nc.vector.bn_stats(stats[:, bass.ds(b, 1), :].rearrange("p b s -> p (b s)"), fblk(mid, b))
                        blocks(dve, f)

        def third_norm(layer):
            with phase() as new:
                var_ready, std_ready, chain, folded = new("var_ready"), new("std_ready"), new("chain"), new("folded")
                normed, kept, turned, saved, stored = (new(n) for n in ("normed", "kept", "turned", "saved", "stored"))
                with nc.Block() as block:
                    @block.scalar
                    def _(act):
                        std(act, var_ready, std_ready)
                        act.wait_ge(folded, 1)

                        def f(b, s):
                            act.wait_ge(kept, b + 1)
                            act.wait_ge(turned, b + 1)
                            nc.scalar.activation(slot_f[:, s, :], fblk(mid, b), ACT.Relu, bias=bn_shift[:, :],
                                                 scale=bn_scale[:, :]).then_inc(normed, 1)
                        blocks(act, f)

                    @block.vector
                    def _(dve):
                        dve.sem_inc(kept, BS)
                        dve.sem_inc(saved, BS)
                        fold_norm(dve, 2, layer, var_ready, std_ready, chain, folded)

                        def f(b, s):
                            dve.wait_ge(normed, b + 1)
                            nc.vector.tensor_copy(fblk(acc[:, 0, :], b), slot_f[:, s, :]).then_inc(kept, 1)
                            dve.wait_ge(turned, b + BS + 1)
                            dve.wait_ge(stored, b + 1)
                            nc.vector.tensor_copy(slot_x[0:TILE, s].rearrange("p t d -> p (t d)"),
                                                  bank[s][0:TILE, 0:2 * P]).then_inc(saved, 1)
                        blocks(dve, f)

                    @block.tensor
                    def _(pe):
                        pe.sem_inc(turned, BS)

                        def f(b, s):
                            pe.wait_ge(normed, b + 1)
                            pe.wait_ge(saved, b + 1)
                            for t in range(2):
                                ins = nc.tensor.transpose(bank[s][0:TILE, t * P:(t + 1) * P],
                                                          slot_f[:, s, t * TILE:(t + 1) * TILE], ident[:, :])
                            ins.then_inc(turned, 1)
                        blocks(pe, f)

                    @block.gpsimd
                    def _(pool):
                        store_rows(pool, lambda s: slot_x[0:TILE, s], h_rows, saved, stored, layer)

        rows_out = [sem(f"rows_out{s}") for s in range(BS)]
        table_out = [sem(f"table_out{s}") for s in range(BS)]

        def store_rows(pool, slot, table, saved, stored, run):
            pool.sem_inc(stored, BS)
            with pool.Fori(0, BITERS) as i:
                for s in range(BS):
                    pool.wait_ge(saved, i * BS + (BS + s + 1))
                    pool.sem_inc(gather_go, 1)
                    pool.dma_start(node_rows(table)[:, bass.ds(2 * (i * BS + s), 2), :], slot(s)).then_inc(rows_out[s], 16)
                for s in range(BS):
                    pool.wait_ge(rows_out[s], i * 16 + 16 * (run * BITERS + 1))
                    pool.sem_inc(stored, 1)

        def to_rows(source, xn, residual, norm_layer=None):
            with phase() as new:
                var_ready, std_ready, chain, folded = new("var_ready"), new("std_ready"), new("chain"), new("folded")
                made, turned, added = new("made"), new("turned"), new("added")
                res_landed, deg_landed = new("res_landed", BS), new("deg_landed", BS)
                exp_done, den_done, deg_used = new("exp_done"), new("den_done"), new("deg_used")
                with nc.Block() as block:
                    @block.sync
                    def _(sp):
                        with sp.Fori(0, BITERS) as i:
                            for s in range(BS):
                                b = i * BS + s
                                sp.wait_ge(added, b + 1)
                                sp.dma_start(slot_x[0:TILE, s], node_rows(residual)[:, bass.ds(2 * b, 2), :]
                                             ).then_inc(res_landed[s], 16)
                                if source == "attention":
                                    sp.wait_ge(deg_used, b + 1)
                                    sp.dma_start(slot_d[:, s, :], deg_row[:, bass.ds(b * BLK, BLK)]
                                                 .broadcast_to([P, BLK])).then_inc(deg_landed[s], 16)

                    @block.scalar
                    def _(act):
                        if source == "norm":
                            std(act, var_ready, std_ready)
                            act.wait_ge(folded, 1)

                            def f(b, s):
                                act.wait_ge(turned, b + 1)
                                nc.scalar.activation(slot_f[:, s, :], fblk(mid, b), ACT.Identity, bias=bn_shift[:, :],
                                                     scale=bn_scale[:, :]).then_inc(made, 1)
                        else:
                            def f(b, s):
                                act.wait_ge(den_done, b + 1)
                                nc.scalar.activation(slot_g[:, s, :], fblk(mid, b), ACT.Exp,
                                                     scale=-1.0).then_inc(exp_done, 1)
                        blocks(act, f)

                    @block.tensor
                    def _(pe):
                        pe.sem_inc(turned, BS)

                        def f(b, s):
                            pe.wait_ge(made, b + 1)
                            pe.wait_ge(added, b + 1)
                            for t in range(2):
                                ins = nc.tensor.transpose(bank[s][0:TILE, t * P:(t + 1) * P],
                                                          slot_f[:, s, t * TILE:(t + 1) * TILE], ident[:, :])
                            ins.then_inc(turned, 1)
                        blocks(pe, f)

                    @block.vector
                    def _(dve):
                        dve.sem_inc(added, BS)
                        if source == "norm":
                            fold_norm(dve, 2, norm_layer, var_ready, std_ready, chain, folded)
                        else:
                            dve.sem_inc(deg_used, BS)
                            dve.sem_inc(den_done, BS)

                        def divide(b, s, i):
                            dve.wait_ge(deg_landed[s], i * 16 + 16)
                            nc.vector.tensor_scalar(slot_d[:, s, :], slot_d[:, s, :], -1.0, float(E),
                                                    ALU.mult, ALU.add).then_inc(chain, 1)
                            dve.wait_ge(exp_done, b + 1)
                            dve.wait_ge(chain, 4 * b + 1)
                            nc.vector.tensor_tensor(slot_g[:, s, :], slot_g[:, s, :], slot_d[:, s, :],
                                                    ALU.mult).then_inc(chain, 1)
                            dve.wait_ge(chain, 4 * b + 2)
                            nc.vector.tensor_tensor(slot_g[:, s, :], slot_g[:, s, :], fblk(acc[:, 1, :], b),
                                                    ALU.add).then_inc(chain, 1)
                            dve.sem_inc(deg_used, 1)
                            dve.wait_ge(chain, 4 * b + 3)
                            nc.vector.reciprocal(slot_g[:, s, :], slot_g[:, s, :]).then_inc(chain, 1)
                            dve.wait_ge(chain, 4 * b + 4)
                            dve.wait_ge(turned, b + 1)
                            nc.vector.tensor_tensor(slot_f[:, s, :], slot_g[:, s, :], fblk(acc[:, 0, :], b),
                                                    ALU.mult).then_inc(made, 1)
                            dve.wait_ge(made, b + 1)
                            dve.sem_inc(den_done, 1)

                        def add(b, s, i):
                            dve.wait_ge(turned, b + BS + 1)
                            dve.wait_ge(res_landed[s], i * 16 + 16)
                            nc.vector.tensor_tensor(xn[0:TILE, bass.ds(2 * b, 2), :],
                                                    bank[s][0:TILE, 0:2 * P].rearrange("p (t d) -> p t d", t=2),
                                                    slot_x[0:TILE, s], ALU.add).then_inc(added, 1)
                            dve.wait_ge(added, b + BS + 1)
                            for t in range(2):
                                nc.vector.bn_stats(
                                    stats[0:TILE, bass.ds(2 * b + t, 1), :].rearrange("p b s -> p (b s)"),
                                    xn[0:TILE, bass.ds(2 * b + t, 1), :].rearrange("p t d -> p (t d)"))
                        with dve.Fori(0, BITERS) as i:
                            if source == "attention":
                                for s in range(BS):
                                    divide(i * BS + s, s, i)
                            for s in range(BS):
                                add(i * BS + s, s, i)

        mean, rstd, ln_tmp = (sb(n, [P, NT, 1]) for n in ("mean", "rstd", "ln_tmp"))

        def layer_norm(xn, final):
            with phase() as new:
                chain, var_ready, std_ready, folded = new("chain"), new("var_ready"), new("std_ready"), new("folded")
                normed, saved, stored = new("normed"), new("saved"), new("stored")
                turned, kept, product, packed, packed_out = (
                    new(n) for n in ("turned", "kept", "product", "packed", "packed_out"))
                with nc.Block() as block:
                    @block.vector
                    def _(dve):
                        n = [0]

                        def link(ins):
                            n[0] += 1
                            ins.then_inc(chain, 1)
                            dve.wait_ge(chain, n[0])
                        even, odd = (stats[0:TILE, :, k:k + 1] for k in (1, 4))
                        m, r, t = (v[0:TILE] for v in (mean, rstd, ln_tmp))
                        link(nc.vector.tensor_tensor(m, even, odd, ALU.add))
                        link(nc.vector.tensor_tensor(t, even, odd, ALU.subtract))
                        link(nc.vector.tensor_scalar(m, m, 0.5, None, ALU.mult))
                        link(nc.vector.tensor_tensor(t, t, t, ALU.mult))
                        link(nc.vector.tensor_tensor(r, stats[0:TILE, :, 2:3], stats[0:TILE, :, 5:6], ALU.add))
                        link(nc.vector.tensor_scalar(t, t, 0.25, 1e-5, ALU.mult, ALU.add))
                        link(nc.vector.tensor_scalar(r, r, 1.0 / P, None, ALU.mult))
                        nc.vector.tensor_tensor(t, r, t, ALU.add).then_inc(var_ready, 1)
                        dve.wait_ge(std_ready, 1)
                        link(nc.vector.reciprocal(r, r))

                        def f(b, s):
                            dve.wait_ge(stored, b + 1)
                            if not final:
                                dve.wait_ge(turned, b + 1)
                            for t in range(2):
                                col = lambda v: v[0:TILE, bass.ds(2 * b + t, 1), :].rearrange("p t d -> p (t d)")
                                ins = nc.vector.tensor_scalar(slot_x[0:TILE, s, t, :], col(xn), col(mean), col(rstd),
                                                              ALU.subtract, ALU.mult)
                            ins.then_inc(normed, 1)
                        dve.sem_inc(normed, BS)
                        if final:
                            blocks(dve, f)
                            return
                        dve.sem_inc(kept, BS)

                        def keep(b, s):
                            dve.wait_ge(turned, b + BS + 1)
                            dve.wait_ge(product, b + 1)
                            nc.vector.tensor_copy(slot_f[:, s, :], bank[s][:, 0:BLK]).then_inc(kept, 1)
                        with dve.Fori(0, BITERS) as i:
                            for s in range(BS):
                                f(i * BS + s, s)
                            for s in range(BS):
                                keep(i * BS + s, s)

                    @block.scalar
                    def _(act):
                        act.wait_ge(var_ready, 1)
                        nc.scalar.activation(rstd[0:TILE], ln_tmp[0:TILE], ACT.Sqrt).then_inc(std_ready, 1)
                        if final:
                            return

                        act.sem_inc(packed, BS)

                        def pack(b, s):
                            act.wait_ge(product, b + BS + 1)
                            act.wait_ge(packed_out, b + 1)
                            h = bank[5 + s % 2]
                            nc.scalar.copy(slot_n[0:TILE, s].rearrange("p t d -> p (t d)"), h[0:TILE, 0:2 * ROW])
                            nc.scalar.copy(tgt_score[:, bass.ds(b * BLK, BLK)], bank[7][0:HEADS, 0:BLK]).then_inc(packed, 1)
                        blocks(act, pack)

                    @block.tensor
                    def _(pe):
                        if final:
                            return
                        pe.sem_inc(turned, BS)
                        pe.sem_inc(product, BS)

                        def turn(b, s):
                            pe.wait_ge(normed, b + BS + 1)
                            pe.wait_ge(kept, b + 1)
                            for t in range(2):
                                ins = nc.tensor.transpose(bank[s][:, t * TILE:(t + 1) * TILE], slot_x[0:TILE, s, t, :],
                                                          ident[0:TILE, 0:TILE])
                            ins.then_inc(turned, 1)

                        def project(b, s):
                            pe.wait_ge(kept, b + BS + 1)
                            pe.wait_ge(packed, b + BS)
                            h = bank[5 + s % 2]
                            for t in range(2):
                                nc.tensor.matmul(h[0:TILE, t * ROW:(t + 1) * ROW], slot_f[:, s, t * TILE:(t + 1) * TILE],
                                                 proj[:, 0:ROW], start=True, stop=True)
                            nc.tensor.matmul(bank[7][0:HEADS, 0:BLK], proj[:, ROW:ROW + HEADS], slot_f[:, s, :],
                                             start=True, stop=True).then_inc(product, 1)
                        with pe.Fori(0, BITERS) as i:
                            for s in range(BS):
                                turn(i * BS + s, s)
                            for s in range(BS):
                                project(i * BS + s, s)

                    @block.gpsimd
                    def _(pool):
                        if final:
                            store_rows(pool, lambda s: slot_x[0:TILE, s], out, normed, stored, LAYERS)
                            return
                        pool.sem_inc(stored, BS)
                        pool.sem_inc(packed_out, BS)
                        with pool.Fori(0, BITERS) as i:
                            for s in range(BS):
                                pool.wait_ge(normed, i * BS + (BS + s + 1))
                                pool.sem_inc(gather_go, 1)
                                pool.dma_start(node_rows(x1_rows)[:, bass.ds(2 * (i * BS + s), 2), :],
                                               slot_x[0:TILE, s]).then_inc(rows_out[s], 16)
                            for s in range(BS):
                                pool.wait_ge(packed, i * BS + (BS + s + 1))
                                pool.sem_inc(gather_go, 1)
                                pool.dma_start(node_rows(att_rows)[:, bass.ds(2 * (i * BS + s), 2), :],
                                               slot_n[0:TILE, s]).then_inc(table_out[s], 16)
                            for s in range(BS):
                                pool.wait_ge(rows_out[s], i * 16 + 16 * ((LAYERS - 1) * BITERS + 1))
                                pool.sem_inc(stored, 1)
                                pool.wait_ge(table_out[s], i * 16 + 16)
                                pool.sem_inc(packed_out, 1)

        masked = cut(0, 2, CHUNK)
        score = cut(1024, 2, CHUNK)
        rise = cut(2048, 2, CHUNK)
        prob = cut(3072, 2, CHUNK)
        prob_turned = cut(4096, 2, CHUNK)
        z = sb("z", [P, 2, J * HEADS])
        tgt_win = sb("tgt_win", [HEADS, 2, HEADS * WIN])
        slopes = sb("slopes", [HEADS, 2])
        tgt_part = sb("tgt_part", [P, 2, 2])
        top = sb("top", [P, 2, 3])
        diag = sb("diag", [P, 2, 2, WIN])
        fall = sb("fall", [P, WIN])
        diff = sb("diff", [P, 2, 2, WIN])
        fac = sb("fac", [P, 2, 2, WIN])
        old_part, new_part = sb("old_part", [P, 2, WIN]), sb("new_part", [P, 2, WIN])
        att_rel = sb("att_rel", [P, J])
        S_COL, TOP_COL = HEADS * WIN, (HEADS + 1) * WIN

        def attention():
            RUN = LAYERS
            with phase() as new:
                names = ("slopes_set z_done prepped scored tgt_copied lrelued max_go maxed topped exped turned saved "
                         "diagonal spread summed_up fell differed factored parts merged gen_idx gen_free "
                         "gen_rel_ready").split()
                (slopes_set, z_done, prepped, scored, tgt_copied, lrelued, max_go, maxed, topped, exped, turned, saved,
                 diagonal, spread, summed_up, fell, differed, factored, parts, merged, gen_idx, gen_free,
                 gen_rel_ready) = (new(n) for n in names)
                with nc.Block() as block:
                    @block.gpsimd
                    def _(pool):
                        wide = pool.value_load(wide_int[0:1, 0:1], min_val=0, max_val=1)
                        with pool.If(wide < 1):
                            gather(pool, att_rows, ROW, RUN, summed_up, 0)
                        with pool.Else():
                            with pool.Fori(0, CH) as c:
                                pool.wait_ge(gen_idx, c + 1)
                                pool.wait_ge(gen_free, c + 1)
                                pool.sem_inc(gather_go, 1)
                                gather_chunk(pool, 0, att_rows, ROW)

                    @block.vector
                    def _(dve):
                        wide = dve.value_load(wide_int[0:1, 0:1], min_val=0, max_val=1)
                        nc.vector.memset(slopes[:, 0:1], 1.0)
                        nc.vector.memset(slopes[:, 1:2], -0.8).then_inc(slopes_set, 1)

                        def col(arr, c):
                            return arr[:, bass.ds(c, 1), :].rearrange("p c j -> p (c j)")

                        def own_parts(c, q, u, base, landed, serial=False):
                            d = u % 2
                            if not serial:
                                after(dve, scored, q - 1)
                            nc.vector.tensor_tensor(
                                tgt_win[:, d, :].rearrange("k (h n) -> k h n", n=WIN),
                                bcast(tgt_score[:, bass.ds(base, WIN)], 1, HEADS),
                                bcast(ident[0:HEADS, 0:HEADS], 2, WIN), ALU.mult)
                            dve.wait_ge(rows_landed[u], landed)
                            nc.vector.tensor_tensor(z[:, d, :].rearrange("p (j h) -> p j h", h=HEADS),
                                                    rows[:, u, :, P:ROW],
                                                    edge_score[:, bass.ds(c, 1), :].rearrange("p c (j h) -> p (c j) h", h=HEADS),
                                                    ALU.add).then_inc(z_done, 1)

                        def mask(q, u, rel):
                            d = u % 2
                            dve.wait_ge(z_done, q + 1)
                            for j in range(J):
                                ins = nc.vector.scalar_tensor_tensor(
                                    masked[:, d, j * P:(j + 1) * P].rearrange("p (h n) -> p h n", n=WIN),
                                    bcast(iota_win, 1, HEADS), rel(j),
                                    bcast(z[:, d, j * HEADS:(j + 1) * HEADS], 2, WIN), ALU.not_equal, ALU.subtract)
                            ins.then_inc(prepped, 1)

                        def maximum(q, u):
                            d = u % 2
                            dve.wait_ge(lrelued, q + 1)
                            dve.sem_inc(max_go, 1)
                            nc.vector.tensor_tensor_reduce(out=score[:, d, :], in0=score[:, d, :], in1=rise[:, d, :],
                                                           scale=1.0, scalar=0.0, op0=ALU.add, op1=ALU.max,
                                                           accum_out=top[:, d, 1:2]).then_inc(maxed, 1)

                        def negate(q, u):
                            d = u % 2
                            dve.wait_ge(maxed, q + 1)
                            nc.vector.tensor_scalar(top[:, d, 2:3], top[:, d, 1:2], -1.0, None, ALU.mult).then_inc(topped, 1)

                        def diagonals(q, u, serial=False):
                            d = u % 2
                            dve.wait_ge(exped, q + 1)
                            if not serial:
                                after(dve, spread, q - 1)
                            nc.vector.tensor_tensor(diag[:, d], bcast(node_sel[:, :], 1, 2), bcast(top[:, d, 0:2], 2, WIN),
                                                    ALU.mult).then_inc(diagonal, 1)

                        def chunk_top(u):
                            return bank[4 + u % 2][:, TOP_COL:TOP_COL + WIN]

                        def compare_tops(q, u, base, serial=False):
                            dve.wait_ge(spread, q + 1)
                            if not serial:
                                after(dve, differed, q)
                            nc.vector.tensor_tensor(fall[:, :], mid[:, bass.ds(base, WIN)], chunk_top(u),
                                                    ALU.subtract).then_inc(fell, 1)

                        def raise_top(q, u, base, serial=False):
                            d = u % 2
                            dve.wait_ge(fell, q + 1)
                            if not serial:
                                after(dve, factored, q - 1)
                            nc.vector.tensor_scalar(diff[:, d, 0, :], fall[:, :], 0.0, None, ALU.min)
                            nc.vector.tensor_scalar(diff[:, d, 1, :], fall[:, :], -1.0, 0.0, ALU.mult, ALU.min)
                            run = mid[:, bass.ds(base, WIN)]
                            nc.vector.tensor_tensor(run, run, chunk_top(u), ALU.max).then_inc(differed, 1)

                        def scale_parts(q, u, base, serial=False):
                            d = u % 2
                            dve.wait_ge(factored, q + 1)
                            dve.wait_ge(summed_up, q + 1 if serial else q + (SLOTS + 1))
                            if not serial:
                                after(dve, merged, q)
                            nc.vector.tensor_tensor(old_part[:, :, :], acc[:, :, bass.ds(base, WIN)],
                                                    bcast(fac[:, d, 0, :], 1, 2), ALU.mult)
                            for h in range(HEADS):
                                mine = slice(h * HD, (h + 1) * HD)
                                nc.vector.tensor_tensor(new_part[mine, 0, :], bank[4 + d][mine, h * WIN:(h + 1) * WIN],
                                                        fac[mine, d, 1, :], ALU.mult)
                            nc.vector.tensor_tensor(new_part[:, 1, :], bank[4 + d][:, S_COL:S_COL + WIN], fac[:, d, 1, :],
                                                    ALU.mult).then_inc(parts, 1)

                        def merge(q, base):
                            dve.wait_ge(parts, q + 1)
                            nc.vector.tensor_tensor(acc[:, :, bass.ds(base, WIN)], old_part[:, :, :], new_part[:, :, :],
                                                    ALU.add).then_inc(merged, 1)

                        with dve.If(wide < 1):
                            def rel_of(c):
                                return lambda j: dst_rel[:, bass.ds(c, 1), j:j + 1].rearrange("p c j -> p (c j)")

                            chunks(dve, [
                                (lambda c, u, t, base: compare_tops(c, u, base), 3),
                                (lambda c, u, t, base: negate(c, u), 2),
                                (lambda c, u, t, base: scale_parts(c, u, base), 4),
                                (lambda c, u, t, base: raise_top(c, u, base), 3),
                                (lambda c, u, t, base: merge(c, base), 4),
                                (lambda c, u, t, base: own_parts(c, c, u, base, t * LAND + LAND * (RUN * ITERS + 1)), 0),
                                (lambda c, u, t, base: diagonals(c, u), 2),
                                (lambda c, u, t, base: mask(c, u, rel_of(c)), 0),
                                (lambda c, u, t, base: maximum(c, u), 1)], load_bases)
                        with dve.Else():
                            dve.sem_inc(gen_free, 1)
                            with dve.Fori(0, CH) as c:
                                with dve.Fori(0, NWIN) as k:
                                    q = c * NWIN + k
                                    nc.vector.tensor_scalar(att_rel[:, :], col(dst_col, c), win_start[:, bass.ds(k, 1)],
                                                            None, ALU.subtract).then_inc(gen_rel_ready, 1)
                                    dve.wait_ge(gen_rel_ready, q + 1)
                                    own_parts(c, q, 0, k * WIN, c * LAND + LAND * (RUN * CH + 1), serial=True)
                                    mask(q, 0, lambda j: att_rel[:, j:j + 1])
                                    maximum(q, 0)
                                    negate(q, 0)
                                    diagonals(q, 0, serial=True)
                                    compare_tops(q, 0, k * WIN, serial=True)
                                    raise_top(q, 0, k * WIN, serial=True)
                                    scale_parts(q, 0, k * WIN, serial=True)
                                    merge(q, k * WIN)
                                    dve.wait_ge(merged, q + 1)
                                dve.sem_inc(gen_free, 1)

                    @block.scalar
                    def _(act):
                        wide = act.value_load(wide_int[0:1, 0:1], min_val=0, max_val=1)

                        def leaky(q, u, serial=False):
                            d = u % 2
                            act.wait_ge(scored, q + 1)
                            nc.scalar.copy(tgt_part[:, d, :], bank[6 + d][:, 0:2]).then_inc(tgt_copied, 1)
                            if not serial:
                                after(act, maxed, q - 1)
                                after(act, exped, q - 1)
                            act.wait_ge(tgt_copied, q + 1)
                            nc.scalar.activation(score[:, d, :], bank[d][:, :], ACT.Identity, bias=tgt_part[:, d, 0:1],
                                                 scale=-MASK)
                            nc.scalar.activation(rise[:, d, :], bank[d][:, :], ACT.Relu, bias=tgt_part[:, d, 1:2],
                                                 scale=0.8 * MASK).then_inc(lrelued, 1)

                        def exp(q, u, serial=False):
                            d = u % 2
                            act.wait_ge(topped, q + 1)
                            if not serial:
                                after(act, turned, q - 1)
                                after(act, diagonal, q - 1)
                            nc.scalar.activation(prob[:, d, :], score[:, d, :], ACT.Exp, bias=top[:, d, 2:3],
                                                 accum_out=top[:, d, 0:1]).then_inc(exped, 1)

                        def save(q, u, serial=False):
                            d = u % 2
                            act.wait_ge(turned, q + 1)
                            if not serial:
                                after(act, summed_up, q + (SLOTS - 1))
                            nc.scalar.copy(prob_turned[:, d, :], bank[2 + d][:, :]).then_inc(saved, 1)

                        def factors(q, u, serial=False):
                            d = u % 2
                            act.wait_ge(differed, q + 1)
                            if not serial:
                                after(act, merged, q - 1)
                            nc.scalar.activation(fac[:, d].rearrange("p k n -> p (k n)"),
                                                 diff[:, d].rearrange("p k n -> p (k n)"), ACT.Exp).then_inc(factored, 1)

                        with act.If(wide < 1):
                            chunks(act, [
                                (lambda c, u, t: save(c, u), 3),
                                (lambda c, u, t: exp(c, u), 2),
                                (lambda c, u, t: leaky(c, u), 1),
                                (lambda c, u, t: factors(c, u), 3),
                                (copy_idx(act, RUN), 0)])
                        with act.Else():
                            act.wait_ge(rows_landed[0], LAND * RUN * CH)
                            with act.Fori(0, CH) as c:
                                act.wait_ge(rows_landed[0], c * LAND + LAND * RUN * CH)
                                nc.scalar.copy(idx[:, 0, :], src_col[:, bass.ds(c, 1), :].rearrange("p c j -> p (c j)")
                                               ).then_inc(gen_idx, 1)
                                with act.Fori(0, NWIN) as k:
                                    q = c * NWIN + k
                                    leaky(q, 0, serial=True)
                                    exp(q, 0, serial=True)
                                    save(q, 0, serial=True)
                                    factors(q, 0, serial=True)

                    @block.tensor
                    def _(pe):
                        wide = pe.value_load(wide_int[0:1, 0:1], min_val=0, max_val=1)
                        pe.wait_ge(slopes_set, 1)

                        def turn_scores(q, u, serial=False):
                            d = u % 2
                            pe.wait_ge(prepped, q + 1)
                            if not serial:
                                after(pe, lrelued, q - 1)
                            nc.tensor.matmul(bank[6 + d][:, 0:2], tgt_win[:, d, :], slopes[:, :], start=True, stop=True)
                            for j in range(J):
                                ins = nc.tensor.transpose(bank[d][:, j * P:(j + 1) * P], masked[:, d, j * P:(j + 1) * P],
                                                          ident[:, :])
                            ins.then_inc(scored, 1)

                        def turn_probs(q, u, serial=False):
                            d = u % 2
                            pe.wait_ge(exped, q + 1)
                            if not serial:
                                after(pe, saved, q - 1)
                            for j in range(J):
                                ins = nc.tensor.transpose(bank[2 + d][:, j * P:(j + 1) * P], prob[:, d, j * P:(j + 1) * P],
                                                          ident[:, :])
                            ins.then_inc(turned, 1)

                        def spread_sums(q, u, serial=False):
                            d = u % 2
                            pe.wait_ge(diagonal, q + 1)
                            if not serial:
                                after(pe, merged, q - 1)
                            nc.tensor.matmul(bank[4 + d][:, S_COL:S_COL + 2 * WIN], head_blk[:, :],
                                             diag[:, d].rearrange("p k n -> p (k n)"), start=True, stop=True
                                             ).then_inc(spread, 1)

                        def sum_up(q, u, serial=False):
                            d = u % 2
                            pe.wait_ge(saved, q + 1)
                            pe.wait_ge(differed, q + 1)
                            for j in range(J):
                                ins = nc.tensor.matmul(bank[4 + d][:, 0:P], rows[:, u, j, 0:P],
                                                       prob_turned[:, d, j * P:(j + 1) * P], start=(j == 0), stop=(j == J - 1))
                            ins.then_inc(summed_up, 1)

                        with pe.If(wide < 1):
                            pe.sem_inc(summed_up, SLOTS)
                            chunks(pe, [(lambda c, u, t: sum_up(c, u), 3),
                                        (lambda c, u, t: turn_probs(c, u), 2),
                                        (lambda c, u, t: spread_sums(c, u), 2),
                                        (lambda c, u, t: turn_scores(c, u), 0)])
                        with pe.Else():
                            with pe.Fori(0, CH * NWIN) as q:
                                turn_scores(q, 0, serial=True)
                                turn_probs(q, 0, serial=True)
                                spread_sums(q, 0, serial=True)
                                sum_up(q, 0, serial=True)

        def clear_running():
            with nc.Block() as block:
                @block.vector
                def _(dve):
                    nc.vector.memset(acc[:, 0, :], 0.0)
                    nc.vector.memset(mid[:, :], 0.0)

                @block.gpsimd
                def _(pool):
                    pool.memset(acc[:, 1, :], 0.0)

        for layer in range(LAYERS):
            messages(layer)
            first_product(layer)
            second_product(layer)
            second_norm(layer)
            if layer < LAYERS - 1:
                third_norm(layer)
        xn = flat[:, 0:NT * P].rearrange("p (t d) -> p t d", d=P)
        to_rows("norm", xn, x, LAYERS - 1)
        layer_norm(xn, final=False)
        clear_running()
        attention()
        xn = edge_score[:, :, :].rearrange("p c k -> p (c k)")[:, 0:NT * P].rearrange("p (t d) -> p t d", d=P)
        to_rows("attention", xn, x1_rows)
        layer_norm(xn, final=True)


_INS = ["x", "src", "dst", "edge_attr_64", "edge_weight", "L0_gnn_W0s", "L0_gnn_W1s", "L0_gnn_bn1_g",
        "L0_gnn_bn1_b", "L0_gnn_bn2_g", "L0_gnn_bn2_b", "L0_gnn_bn3_g", "L0_gnn_bn3_b", "L1_gnn_W_node",
        "L1_gnn_W_edge", "L1_gnn_a"]


def kernel(**inputs):
    import concourse.bacc as _bacc
    from concourse.bass_utils import run_bass_kernel_spmd as _run

    nc = _bacc.Bacc("TRN2", target_bir_lowering=False, num_devices=1)
    arrays, args = {}, []
    for name in _INS:
        v = np.ascontiguousarray(inputs[name])
        arrays[f"in_{name}"] = v
        args.append(nc.dram_tensor(f"in_{name}", v.shape, mybir.dt.from_np(v.dtype), kind="ExternalInput").ap())
    out = nc.dram_tensor("out_0", inputs["x"].shape, F32, kind="ExternalOutput").ap()
    gnn_program(nc, *args[:7], args[7:13], *args[13:], out)
    return _run(nc, [arrays], core_ids=[0]).results[0]["out_0"]
```

```python
from contextlib import ExitStack, contextmanager

import numpy as np

import concourse.bass as bass
from concourse import mybir
from concourse.alu_op_type import AluOpType as ALU

F32, BF16 = mybir.dt.float32, mybir.dt.bfloat16
I32, I16 = mybir.dt.int32, mybir.dt.int16
ACT = mybir.ActivationFunctionType
AX = mybir.AxisListType.X

P = 128
J = 4
CHUNK = P * J
WIN = 32
HEADS, HD = 4, 32
ROW = P + HEADS
SLOTS = 8
LOOK = 4
TILE = 125
BLK = 2 * TILE
BS = 5
BN_EPS = 1e-5
FAR = float(1 << 20)
MASK = 2.0**64


def gnn_program(nc, x, src, dst, edge_attr, edge_weight, W0s, W1s, bns, W_node, W_edge, a, out):
    N, E = x.shape[0], src.shape[0]
    LAYERS, FE = W0s.shape[0], edge_attr.shape[1]
    CH = -(-E // CHUNK)
    TURNS = (CH - 1) // SLOTS
    GRP = -(-CH // P)
    FULL, TAIL = (CH - 1) // P, (CH - 1) % P
    LAST = E - (CH - 1) * CHUNK
    NP = N + WIN
    NBLK, NT = N // BLK, N // TILE
    BITERS = NBLK // BS
    NWIN = -(-N // WIN)
    assert N % (BLK * BS) == 0 and FE * 2 == P and NP * 2 >= 4 * GRP * CHUNK

    ctx = ExitStack()
    with ctx:
        def sb(name, shape, dt=F32):
            return ctx.enter_context(nc.sbuf_tensor(name, shape, dt))

        def sem(name):
            return ctx.enter_context(nc.semaphore(name))

        def dram(name, shape, dt=F32):
            return nc.dram_tensor(name, shape, dt).ap()

        h_rows = dram("h_rows", (N, P))
        att_rows = dram("att_rows", (N, ROW))
        x1_rows = dram("x1_rows", (N, P))
        deg_row = dram("deg_row", (1, N))
        base_rows = dram("base_rows", (2 * GRP, P))

        src_col = sb("src_col", [P, CH + SLOTS, J], I16)
        dst_col = sb("dst_col", [P, CH, J], I16)
        dst_rel = sb("dst_rel", [P, CH, J])
        w_col = sb("w_col", [P, CH, J])
        edge_score = sb("edge_score", [P, CH, J * HEADS])
        acc = sb("acc", [P, 2, NP])
        mid = sb("mid", [P, NP])
        tgt_score = sb("tgt_score", [HEADS, NP])
        rows = sb("rows", [P, SLOTS, J, ROW])
        idx = sb("idx", [P, SLOTS, J], I32)
        base_int = sb("base_int", [1, GRP * P], I32)
        wide_int = sb("wide_int", [1, 1], I32)
        work = sb("work", [P, 5400])
        w0 = sb("w0", [P, LAYERS, P])
        w1 = sb("w1", [P, LAYERS, P])
        bn = sb("bn", [P, 6, LAYERS])
        proj = sb("proj", [P, ROW + HEADS])
        edge_fold = sb("edge_fold", [P, 2 * HEADS])
        ident = sb("ident", [P, P])
        ones_b = sb("ones_b", [P, P], BF16)
        iota_blk = sb("iota_blk", [P, BLK])
        iota_win = iota_blk[:, 0:WIN]
        head_sel = sb("head_sel", [P, HEADS])
        head_blk = sb("head_blk", [P, P])
        node_sel = sb("node_sel", [P, WIN])
        win_start = sb("win_start", [P, NWIN])
        blk_start = sb("blk_start", [P, NBLK])
        stats = sb("stats", [P, NT, 6])
        small = sb("small", [P, 16])
        onehot = sb("onehot", [P, SLOTS, J, WIN])
        plain = sb("plain", [P, SLOTS, J, WIN], BF16)

        bank = [ctx.enter_context(nc.psum_tensor(f"bank{i}", [P, 512], F32)) for i in range(8)]

        flat = acc[:, :, :].rearrange("p c n -> p (c n)")

        def cut(start, *shape, dt=F32, of=None):
            n = int(np.prod(shape))
            v = (work if of is None else of)[:, start:start + n]
            if dt != F32:
                v = v.bitcast(dt)
            if len(shape) == 2:
                v = v.rearrange("p (a b) -> p a b", b=shape[1])
            if len(shape) == 3:
                v = v.rearrange("p (a b c) -> p a b c", b=shape[1], c=shape[2])
            return v

        def bcast(v, axis, n):
            v = v.unsqueeze(axis)
            return v.broadcast_to([*v.shape[:axis], n, *v.shape[axis + 1:]])

        def after(eng, s, n):
            if not isinstance(n, int) or n >= 1:
                eng.wait_ge(s, n)

        def chunks(eng, stages, load_bases=None):
            def run(f, c, k, turn, base):
                f(c, k % SLOTS, turn, *([base[k + LOOK]] if load_bases else []))

            base = [None] * LOOK + list(load_bases(0, SLOTS)) if load_bases else None
            for u in range(SLOTS):
                for f, lag in stages:
                    if u >= lag:
                        run(f, u - lag, u - lag, 0, base)
            with eng.Fori(1, TURNS) as i:
                base = load_bases(i * SLOTS - LOOK, SLOTS + LOOK) if load_bases else None
                for u in range(SLOTS):
                    for f, lag in stages:
                        run(f, i * SLOTS + (u - lag), u - lag, i if u >= lag else i - 1, base)
            left = CH - TURNS * SLOTS
            base = load_bases(TURNS * SLOTS - LOOK, left + LOOK) if load_bases else None
            for u in range(left + max(lag for _, lag in stages)):
                for f, lag in stages:
                    if u - lag < left:
                        run(f, TURNS * SLOTS + u - lag, u - lag, TURNS if u >= lag else TURNS - 1, base)

        s_load, s_pad, s_const = sem("s_load"), sem("s_pad"), sem("s_const")
        s_wload, s_dve, s_tr, s_trs = sem("s_wload"), sem("s_dve"), sem("s_tr"), sem("s_trs")
        s_base, s_baseld = sem("s_base"), sem("s_baseld")
        s_fold, s_basetr = sem("s_fold"), sem("s_basetr")

        raw_src = cut(0, GRP, CHUNK, dt=I32, of=flat)
        raw_min = cut(GRP * CHUNK, GRP, CHUNK, dt=I32, of=flat)
        raw_max = cut(2 * GRP * CHUNK, GRP, CHUNK, dt=I32, of=flat)
        raw_w = cut(3 * GRP * CHUNK, GRP, CHUNK, of=flat)
        scores_flat = edge_score[:, :, :].rearrange("p c k -> p (c k)")
        src_f = cut(0, GRP, CHUNK, of=scores_flat)
        dst_f = cut(GRP * CHUNK, GRP, CHUNK, of=scores_flat)
        iota_i = cut(0, BLK, dt=I32)
        base_bc = cut(250, GRP * P)
        base_f = cut(250 + GRP * P, 2 * GRP * P)
        bs = cut(1900, 2 * GRP)
        bs_t = cut(1920, P)
        win_i = cut(2600, NWIN, dt=I32)
        blk_i = cut(2900, NBLK, dt=I32)
        wn_nat, we_twice = cut(2200, P), cut(2360, 2, FE)
        a_col = cut(2500, 3)
        a_mask = cut(2520, 3, HEADS)
        spread = cut(2580, 8)

        by_chunk = [(raw_src, src), (raw_min, dst), (raw_max, dst), (raw_w, edge_weight)]
        n_loads = len(by_chunk) * ((FULL > 0) + (TAIL > 0) + 1)
        with nc.Block() as block:
            @block.sync
            def _(sp):
                sp.wait_ge(s_pad, 4)
                for raw, d in by_chunk:
                    if FULL:
                        sp.dma_start(raw[:, 0:FULL, :], d[0:FULL * P * CHUNK].rearrange(
                            "(g r c) -> r g c", r=P, c=CHUNK)).then_inc(s_load, 16)
                    if TAIL:
                        sp.dma_start(raw[0:TAIL, FULL, :], d[FULL * P * CHUNK:(CH - 1) * CHUNK].rearrange(
                            "(r c) -> r c", c=CHUNK)).then_inc(s_load, 16)
                    sp.dma_start(raw[TAIL:TAIL + 1, FULL, 0:LAST],
                                 d[(CH - 1) * CHUNK:E].rearrange("(r c) -> r c", r=1)).then_inc(s_load, 16)
                sp.wait_ge(s_basetr, 2)
                sp.dma_start(base_rows, bs_t[0:2 * GRP, :]).then_inc(s_base, 16)
                sp.wait_ge(s_base, 16)
                row = base_rows.rearrange("(o g) r -> o (g r)", o=1)
                sp.dma_start(base_f[0:1, :], row).then_inc(s_baseld, 16)
                sp.dma_start(base_bc[:, :], row[:, 0:GRP * P].broadcast_to([P, GRP * P])).then_inc(s_baseld, 16)

            @block.scalar
            def _(act):
                act.dma_start(w0[:, :, :], W0s.rearrange("l i o -> i l o")).then_inc(s_wload, 16)
                act.dma_start(w1[:, :, :], W1s.rearrange("l i o -> i l o")).then_inc(s_wload, 16)
                for k, v in enumerate(bns):
                    act.dma_start(bn[:, k, :], v.rearrange("l d -> d l"),
                                  allow_slow_non_contiguous=True).then_inc(s_wload, 16)
                act.dma_start(wn_nat, W_node).then_inc(s_wload, 16)
                for k in range(2):
                    act.dma_start(we_twice[:, k, :], W_edge).then_inc(s_wload, 16)
                for h in range(HEADS):
                    act.dma_start(a_col[h * HD:(h + 1) * HD, :], a[h, :].rearrange("(s k) -> k s", k=HD),
                                  allow_slow_non_contiguous=True).then_inc(s_wload, 16)

            @block.gpsimd
            def _(pool):
                pool.memset(raw_src[:, FULL:, :], 0).then_inc(s_pad, 1)
                pool.memset(raw_min[:, FULL:, :], int(FAR)).then_inc(s_pad, 1)
                pool.memset(raw_max[:, FULL:, :], -1).then_inc(s_pad, 1)
                pool.memset(raw_w[:, FULL:, :], 0.0).then_inc(s_pad, 1)
                pool.memset(ident[:, :], 0.0).then_inc(s_const, 1)
                pool.memset(head_sel[:, :], 1.0).then_inc(s_const, 1)
                pool.iota(blk_i, pattern=[[BLK, NBLK]], base=0, channel_multiplier=0)
                pool.iota(iota_i, pattern=[[1, BLK]], base=0, channel_multiplier=0).then_inc(s_const, 1)
                pool.iota(win_i, pattern=[[WIN, NWIN]], base=0, channel_multiplier=0).then_inc(s_const, 1)
                pool.wait_ge(s_const, 2)
                pool.affine_select(out=ident[:, :], in_=ident[:, :], compare_op=ALU.not_equal, fill=1.0,
                                   base=0, pattern=[[-1, P]], channel_multiplier=1).then_inc(s_const, 1)
                pool.affine_select(out=head_sel[:, :], in_=head_sel[:, :], compare_op=ALU.is_ge, fill=0.0,
                                   base=0, pattern=[[-HD, HEADS]], channel_multiplier=1).then_inc(s_const, 1)
                pool.wait_ge(s_const, 6)
                pool.affine_select(out=head_sel[:, :], in_=head_sel[:, :], compare_op=ALU.is_ge, fill=0.0,
                                   base=HD - 1, pattern=[[HD, HEADS]], channel_multiplier=-1).then_inc(s_const, 1)
                pool.memset(ones_b[:, :], 1.0).then_inc(s_const, 1)
                pool.memset(tgt_score[:, :], 0.0).then_inc(s_const, 1)
                pool.memset(mid[:, :], 0.0).then_inc(s_const, 1)
                pool.memset(edge_fold[:, :], 0.0).then_inc(s_const, 1)

            @block.vector
            def _(dve):
                done = [0]

                def link(ins):
                    done[0] += 1
                    ins.then_inc(s_dve, 1)
                    dve.wait_ge(s_dve, done[0])

                wrap = CH + SLOTS - CH % SLOTS
                dve.wait_ge(s_const, 11)
                nc.vector.tensor_copy(iota_blk[:, :], iota_i)
                nc.vector.tensor_copy(blk_start[:, :], blk_i)
                nc.vector.tensor_copy(win_start[:, :], win_i)
                nc.vector.tensor_copy(head_blk[:, :].rearrange("p (h k) -> p h k", h=HEADS),
                                      bcast(head_sel[:, :], 2, HD))
                nc.vector.tensor_reduce(node_sel[:, :], ident[:, :].rearrange("p (h n) -> p n h", h=HEADS),
                                        AX, ALU.add)
                dve.wait_ge(s_load, 16 * n_loads)
                link(nc.vector.tensor_copy(src_f, raw_src))
                link(nc.vector.tensor_copy(dst_f, raw_max))
                link(nc.vector.tensor_reduce(spread[:, 0:GRP], raw_min, AX, ALU.min))
                link(nc.vector.tensor_reduce(spread[:, 4:4 + GRP], raw_max, AX, ALU.max))
                link(nc.vector.tensor_scalar(bs[:, 0:GRP], spread[:, 0:GRP], float(N - 1), None, ALU.min))
                link(nc.vector.tensor_tensor(bs[:, GRP:], spread[:, 4:4 + GRP], bs[:, 0:GRP], ALU.subtract))
                dve.wait_ge(s_basetr, 1)
                nc.vector.tensor_copy(bs_t[0:2 * GRP, :], bank[4][0:2 * GRP, 0:P]).then_inc(s_basetr, 1)
                dve.wait_ge(s_wload, 16 * 15)
                link(nc.vector.tensor_tensor(a_mask, bcast(a_col, 2, HEADS), bcast(head_sel[:, :], 1, 3), ALU.mult))
                k = 0
                for g in range(GRP):
                    n = min(P, CH - g * P)
                    for what in range(3):
                        for j in range(J):
                            k += 1
                            dve.wait_ge(s_tr, k)
                            t = bank[k % 4][:, 0:n]
                            if what == 0:
                                nc.vector.tensor_copy(src_col[:, g * P:g * P + n, j], t).then_inc(s_trs, 1)
                            elif what == 1:
                                nc.vector.tensor_copy(dst_col[:, g * P:g * P + n, j], t)
                                nc.vector.tensor_copy(dst_rel[:, g * P:g * P + n, j], t).then_inc(s_trs, 1)
                            else:
                                nc.vector.tensor_copy(w_col[:, g * P:g * P + n, j], t).then_inc(s_trs, 1)
                dve.wait_ge(s_trs, k)
                nc.vector.tensor_copy(src_col[:, CH:wrap, :], src_col[:, CH % SLOTS:SLOTS, :])
                if CH % SLOTS:
                    nc.vector.tensor_copy(src_col[:, wrap:CH + SLOTS, :], src_col[:, 0:CH % SLOTS, :])
                dve.wait_ge(s_baseld, 32)
                nc.vector.tensor_copy(base_int[:, :], base_f[0:1, 0:GRP * P])
                link(nc.vector.tensor_reduce(small[0:1, 0:1], base_f[0:1, GRP * P:], AX, ALU.max))
                nc.vector.tensor_scalar(wide_int[:, :], small[0:1, 0:1], float(WIN), None, ALU.is_ge)
                nc.vector.tensor_tensor(dst_rel[:, :, :], dst_rel[:, :, :],
                                        bcast(base_bc[:, 0:CH], 2, J), ALU.subtract)
                dve.wait_ge(s_fold, 1)
                nc.vector.tensor_copy(proj[:, 0:P], bank[5][:, 0:P])
                nc.vector.tensor_scalar(proj[:, P:ROW], bank[5][:, P:ROW], 1 / MASK, None, ALU.mult)
                nc.vector.tensor_copy(proj[:, ROW:ROW + HEADS], bank[5][:, ROW:ROW + HEADS])
                for k in range(2):
                    nc.vector.tensor_scalar(edge_fold[k * FE:(k + 1) * FE, k * HEADS:(k + 1) * HEADS],
                                            bank[6][k * FE:(k + 1) * FE, 0:HEADS], 1 / MASK, None, ALU.mult)

            @block.tensor
            def _(pe):
                pe.wait_ge(s_const, 11)
                pe.wait_ge(s_load, 16 * n_loads)
                pe.wait_ge(s_dve, 6)
                nc.tensor.transpose(bank[4][0:2 * GRP, 0:P], bs, ident[:, :]).then_inc(s_basetr, 1)
                k = 0
                for g in range(GRP):
                    n = min(P, CH - g * P)
                    for f in (src_f, dst_f, raw_w):
                        for j in range(J):
                            k += 1
                            if k > 4:
                                pe.wait_ge(s_trs, k - 4)
                            nc.tensor.transpose(bank[k % 4][:, 0:P], f[:, g, j::J], ident[:, :]).then_inc(s_tr, 1)
                pe.wait_ge(s_dve, 7)
                nc.tensor.transpose(bank[5][:, 0:P], wn_nat, ident[:, :])
                for k in range(2):
                    nc.tensor.matmul(bank[5][:, P + k * HEADS:P + (k + 1) * HEADS], wn_nat, a_mask[:, k, :],
                                     start=True, stop=True)
                nc.tensor.matmul(bank[6][:, 0:HEADS], we_twice.rearrange("p k f -> p (k f)"), a_mask[:, 2, :],
                                 start=True, stop=True).then_inc(s_fold, 1)


        @contextmanager
        def phase():
            with ExitStack() as st:
                held = []

                def new(name, n=None):
                    got = [st.enter_context(nc.semaphore(name if n is None else f"{name}{k}")) for k in range(n or 1)]
                    held.extend(got)
                    return got if n else got[0]
                yield new
                nums = sorted(h.num for h in held)
                with nc.Block() as block:
                    @block.sync
                    def _(sp):
                        start = nums[0]
                        for k, num in enumerate(nums):
                            if k + 1 == len(nums) or nums[k + 1] != num + 1:
                                sp.sem_clear(range(start, num + 1))
                                start = nums[k + 1] if k + 1 < len(nums) else None

        def blocks(eng, f):
            with eng.Fori(0, BITERS) as i:
                for s in range(BS):
                    f(i * BS + s, s)

        def node_rows(table):
            return table.rearrange("(t p) d -> p t d", p=TILE)

        slot_x = cut(0, BS, 2, P)
        slot_f = cut(1280, BS, BLK)
        slot_n = cut(2560, BS, 2, ROW)

        def fblk(arr, b):
            return arr[:, bass.ds(b * BLK, BLK)]

        rows_landed = [sem(f"rows_landed{u}") for u in range(SLOTS)]
        idx_copied, rows_done, pool_go = sem("idx_copied"), sem("rows_done"), sem("pool_go")
        onehot_ready, acc_added = sem("onehot_ready"), sem("acc_added")
        LAND = 16 * J

        def gather_chunk(pool, u, table, width):
            for j in range(J):
                pool.indirect_dma_start(
                    out=rows[:, u, j, 0:width], out_offset=None, in_=table,
                    in_offset=bass.IndirectOffsetOnAxis(ap=idx[:, u, j:j + 1], axis=0),
                ).then_inc(rows_landed[u], 16)

        def gather(pool, table, width, run, freed, freed_base):
            def turn(i, n):
                for u in range(n):
                    pool.wait_ge(idx_copied, i * SLOTS + (run * CH + u + 1))
                    pool.wait_ge(freed, i * SLOTS + (freed_base + u + 1))
                    pool.sem_inc(pool_go, 1)
                    gather_chunk(pool, u, table, width)
            with pool.Fori(0, TURNS) as i:
                turn(i, SLOTS)
            turn(TURNS, CH - TURNS * SLOTS)

        def landed_at(run, u, turn):
            return turn * LAND + LAND * (run * (-(-(CH - u) // SLOTS)) + 1)

        def copy_idx(act, run):
            def f(c, u, turn):
                act.wait_ge(rows_landed[u], landed_at(run, u, turn))
                nc.scalar.copy(idx[:, u, :], src_col[:, bass.ds(c + SLOTS, 1), :]
                               .rearrange("p c j -> p (c j)")).then_inc(idx_copied, 1)
            return f

        ea_slot = cut(0, SLOTS, J * FE)
        ea_turned_sb = cut(SLOTS * J * FE, 2, J * FE)
        gen_onehot = cut(2560, J, BLK)
        gen_plain = cut(3560, J, BLK // 2)
        gen_rel = cut(4100, J)
        gen_plain = gen_plain.rearrange("p j n -> p (j n)").bitcast(BF16).rearrange("p (j n) -> p j n", n=BLK)

        with nc.Block() as block:
            @block.scalar
            def _(act):
                for u in range(SLOTS):
                    nc.scalar.copy(idx[:, u, :], src_col[:, u, :]).then_inc(idx_copied, 1)

            @block.tensor
            def _(pe):
                pe.sem_inc(rows_done, SLOTS)

            @block.vector
            def _(dve):
                dve.sem_inc(acc_added, 2)

        def load_bases(start, n):
            return nc.values_load_multi_w_load_instructions(
                base_int[0:1, bass.ds(start, n)], engines=[mybir.EngineType.DVE], min_val=0, max_val=N - 1)[1]

        def messages(layer):
            table = x if layer == 0 else h_rows
            first = layer == 0
            done, comps = layer * CH, 2 if first else 1
            with phase() as new:
                if first:
                    x_landed, x_turned, x_saved, acc_cleared = (
                        new("x_landed", BS), new("x_turned"), new("x_saved"), new("acc_cleared"))
                    ea_landed, ea_under, ea_turned = new("ea_landed", SLOTS), new("ea_under"), new("ea_turned")
                    eat_saved, score_done, score_saved = new("eat_saved"), new("score_done"), new("score_saved")
                gen_ready, gen_summed, gen_added = new("gen_ready"), new("gen_summed"), new("gen_added")
                gen_rel_ready, gen_idx, gen_free = new("gen_rel_ready"), new("gen_idx"), new("gen_free")

                with nc.Block() as block:
                    @block.sync
                    def _(sp):
                        if not first:
                            return
                        with sp.Fori(0, BITERS) as i:
                            for s in range(BS):
                                sp.wait_ge(x_turned, i * BS + s + 1)
                                sp.dma_start(slot_x[0:TILE, s], node_rows(x)[:, bass.ds(2 * (i * BS + s), 2), :]
                                             ).then_inc(x_landed[s], 16)
                        sp.wait_ge(x_turned, NBLK + BS)
                        per_chunk = edge_attr[0:(CH - 1) * CHUNK, :].rearrange("(c p j) f -> p c (j f)", p=P, j=J)
                        with sp.Fori(0, TURNS) as i:
                            for u in range(SLOTS):
                                sp.wait_ge(ea_turned, i * SLOTS + u + 1)
                                sp.dma_start(ea_slot[:, u, :], per_chunk[:, bass.ds(i * SLOTS + u, 1), :]
                                             .rearrange("p c f -> p (c f)")).then_inc(ea_landed[u], 16)
                        for c in range(TURNS * SLOTS, CH - 1):
                            sp.wait_ge(ea_turned, c + 1)
                            sp.dma_start(ea_slot[:, c % SLOTS, :], per_chunk[:, c, :]).then_inc(ea_landed[c % SLOTS], 16)
                        u = (CH - 1) % SLOTS
                        sp.wait_ge(ea_turned, CH)
                        sp.dma_start(ea_slot[:, u, :], per_chunk[:, 0, :]).then_inc(ea_under, 16)
                        sp.wait_ge(ea_under, 16)
                        n, tail = 1, edge_attr[(CH - 1) * CHUNK:E, :]
                        full, part = LAST // J, LAST % J
                        if full:
                            sp.dma_start(ea_slot[0:full, u, :], tail[0:full * J, :].rearrange(
                                "(p j) f -> p (j f)", j=J)).then_inc(ea_under, 16)
                            n += 1
                        if part:
                            sp.dma_start(ea_slot[full:full + 1, u, 0:part * FE], tail[full * J:LAST, :]
                                         .rearrange("(p j) f -> p (j f)", p=1)).then_inc(ea_under, 16)
                            n += 1
                        sp.wait_ge(ea_under, 16 * n)
                        sp.sem_inc(ea_landed[u], 16)

                    @block.gpsimd
                    def _(pool):
                        wide = pool.value_load(wide_int[0:1, 0:1], min_val=0, max_val=1)
                        with pool.If(wide < 1):
                            gather(pool, table, P, layer, rows_done, done)
                        with pool.Else():
                            with pool.Fori(0, CH) as c:
                                pool.wait_ge(gen_idx, c + 1)
                                pool.wait_ge(gen_free, c + 1)
                                pool.sem_inc(pool_go, 1)
                                gather_chunk(pool, 0, table, P)

                    @block.vector
                    def _(dve):
                        wide = dve.value_load(wide_int[0:1, 0:1], min_val=0, max_val=1)

                        def select(c, u, turn):
                            dve.wait_ge(rows_done, c + (done + 1))
                            for j in range(J):
                                col = lambda arr: arr[:, bass.ds(c, 1), j:j + 1].rearrange("p c j -> p (c j)")
                                ins = nc.vector.tensor_scalar(onehot[:, u, j, :], iota_win[:, :], col(dst_rel),
                                                              col(w_col), ALU.is_equal, ALU.mult)
                            if first:
                                ins = nc.vector.tensor_tensor(
                                    plain[:, u], bcast(iota_win[:, :], 1, J),
                                    bcast(dst_rel[:, bass.ds(c, 1), :].rearrange("p c j -> p (c j)"), 2, WIN),
                                    ALU.is_equal)
                            ins.then_inc(onehot_ready, 1)

                        def add(c, u, turn):
                            b = dve.value_load(base_int[0:1, bass.ds(c, 1)], min_val=0, max_val=N - 1)
                            dve.wait_ge(rows_done, c + (SLOTS + done + 1))
                            dve.wait_ge(acc_added, c + (2 + done))
                            win = acc[:, 0:comps, bass.ds(b, WIN)]
                            nc.vector.tensor_tensor(
                                win, win, bank[u % 2][:, 0:comps * WIN].rearrange("p (k n) -> p k n", n=WIN),
                                ALU.add).then_inc(acc_added, 1)

                        if first:
                            nc.vector.memset(acc[:, 0, N:NP], 0.0)
                            nc.vector.memset(acc[:, 1, :], 0.0).then_inc(acc_cleared, 1)
                            dve.wait_ge(acc_cleared, 1)
                            dve.wait_ge(x_saved, NBLK + BS)
                        with dve.If(wide < 1):
                            chunks(dve, [(add, 2), (select, 0)])
                        with dve.Else():
                            dve.sem_inc(gen_free, 1)
                            with dve.Fori(0, CH) as c:
                                with dve.Fori(0, NBLK) as k:
                                    q = c * NBLK + k
                                    nc.vector.tensor_scalar(
                                        gen_rel, dst_col[:, bass.ds(c, 1), :].rearrange("p c j -> p (c j)"),
                                        blk_start[:, bass.ds(k, 1)], None, ALU.subtract).then_inc(gen_rel_ready, 1)
                                    dve.wait_ge(gen_rel_ready, q + 1)
                                    for j in range(J):
                                        wj = w_col[:, bass.ds(c, 1), j:j + 1].rearrange("p c j -> p (c j)")
                                        ins = nc.vector.tensor_scalar(gen_onehot[:, j, :], iota_blk[:, :],
                                                                      gen_rel[:, j:j + 1], wj, ALU.is_equal, ALU.mult)
                                    if first:
                                        ins = nc.vector.tensor_tensor(gen_plain, bcast(iota_blk[:, :], 1, J),
                                                                      bcast(gen_rel, 2, BLK), ALU.is_equal)
                                    ins.then_inc(gen_ready, 1)
                                    dve.wait_ge(gen_summed, q + 1)
                                    for comp in range(comps):
                                        win = acc[:, comp, bass.ds(k * BLK, BLK)]
                                        ins = nc.vector.tensor_tensor(win, win, bank[comp][:, 0:BLK], ALU.add)
                                    ins.then_inc(gen_added, 1)
                                    dve.wait_ge(gen_added, q + 1)
                                dve.sem_inc(gen_free, 1)

                    @block.tensor
                    def _(pe):
                        wide = pe.value_load(wide_int[0:1, 0:1], min_val=0, max_val=1)
                        if first:
                            pe.sem_inc(ea_turned, SLOTS)
                            pe.sem_inc(score_done, 2)

                        def add_up(c, u, turn):
                            pe.wait_ge(onehot_ready, c + (done + 1))
                            pe.wait_ge(acc_added, c + (done + 1))
                            pe.wait_ge(rows_landed[u], landed_at(layer, u, turn))
                            for j in range(J):
                                ins = nc.tensor.matmul(bank[u % 2][:, 0:WIN], rows[:, u, j, 0:P],
                                                       onehot[:, u, j, :], start=(j == 0), stop=(j == J - 1))
                            if first:
                                for j in range(J):
                                    ins = nc.tensor.matmul(bank[u % 2][:, WIN:2 * WIN], ones_b[:, :],
                                                           plain[:, u, j, :], start=(j == 0), stop=(j == J - 1))
                            ins.then_inc(rows_done, 1)

                        def turn_attr(c, u, turn):
                            pe.wait_ge(ea_landed[u], turn * 16 + 16)
                            pe.wait_ge(eat_saved, c + 1)
                            for k in range(J // 2):
                                ins = nc.tensor.transpose(bank[2 + u % 2][:, k * P:(k + 1) * P],
                                                          ea_slot[:, u, k * P:(k + 1) * P], ident[:, :])
                            ins.then_inc(ea_turned, 1)

                        def score_attr(c, u, turn):
                            pe.wait_ge(eat_saved, c + 3)
                            pe.wait_ge(score_saved, c + 1)
                            for k in range(J // 2):
                                ins = nc.tensor.matmul(bank[4 + u % 2][:, k * 2 * HEADS:(k + 1) * 2 * HEADS],
                                                       ea_turned_sb[:, u % 2, k * P:(k + 1) * P], edge_fold[:, :],
                                                       start=True, stop=True)
                            ins.then_inc(score_done, 1)

                        if first:
                            pe.sem_inc(x_turned, BS)
                            with pe.Fori(0, BITERS) as i:
                                for s in range(BS):
                                    pe.wait_ge(x_landed[s], i * 16 + 16)
                                    pe.wait_ge(x_saved, i * BS + s + 1)
                                    for t in range(2):
                                        ins = nc.tensor.transpose(bank[s][:, t * TILE:(t + 1) * TILE],
                                                                  slot_x[0:TILE, s, t, :], ident[0:TILE, 0:TILE])
                                    ins.then_inc(x_turned, 1)
                            pe.wait_ge(x_saved, NBLK + BS)
                        attr = [(turn_attr, 0), (score_attr, 1)] if first else []
                        with pe.If(wide < 1):
                            chunks(pe, attr + [(add_up, 0)])
                        with pe.Else():
                            if first:
                                chunks(pe, attr)
                            with pe.Fori(0, CH) as c:
                                with pe.Fori(0, NBLK) as k:
                                    pe.wait_ge(rows_landed[0], c * LAND + LAND * (layer * CH + 1))
                                    pe.wait_ge(gen_ready, c * NBLK + k + 1)
                                    for j in range(J):
                                        ins = nc.tensor.matmul(bank[0][:, 0:BLK], rows[:, 0, j, 0:P],
                                                               gen_onehot[:, j, :], start=(j == 0), stop=(j == J - 1))
                                    if first:
                                        for j in range(J):
                                            ins = nc.tensor.matmul(bank[1][:, 0:BLK], ones_b[:, :], gen_plain[:, j, :],
                                                                   start=(j == 0), stop=(j == J - 1))
                                    ins.then_inc(gen_summed, 1)

                    @block.scalar
                    def _(act):
                        wide = act.value_load(wide_int[0:1, 0:1], min_val=0, max_val=1)
                        if first:
                            act.sem_inc(eat_saved, 2)
                            act.sem_inc(score_saved, 2)

                        def save_turned(c, u, turn):
                            act.wait_ge(ea_turned, c + (SLOTS + 1))
                            act.wait_ge(score_done, c + 1)
                            nc.scalar.copy(ea_turned_sb[:, u % 2, :], bank[2 + u % 2][:, 0:J * FE]).then_inc(eat_saved, 1)

                        def save_score(c, u, turn):
                            act.wait_ge(score_done, c + 3)
                            nc.scalar.copy(edge_score[:, bass.ds(c, 1), :].rearrange("p c k -> p (c k)"),
                                           bank[4 + u % 2][:, 0:J * HEADS]).then_inc(score_saved, 1)

                        if first:
                            act.sem_inc(x_saved, BS)
                            with act.Fori(0, BITERS) as i:
                                for s in range(BS):
                                    act.wait_ge(x_turned, i * BS + (s + BS + 1))
                                    nc.scalar.copy(fblk(acc[:, 0, :], i * BS + s), bank[s][:, 0:BLK]).then_inc(x_saved, 1)
                        attr = [(save_turned, 0), (save_score, 1)] if first else []
                        with act.If(wide < 1):
                            chunks(act, attr + [(copy_idx(act, layer), 0)])
                        with act.Else():
                            if first:
                                chunks(act, attr)
                            general_idx(act, layer, gen_idx)

        def general_idx(act, run, gen_idx):
            act.wait_ge(idx_copied, SLOTS)
            if run:
                act.wait_ge(rows_landed[0], LAND * run * CH)
            nc.scalar.copy(idx[:, 0, :], src_col[:, 0, :]).then_inc(gen_idx, 1)
            with act.Fori(1, CH) as c:
                act.wait_ge(rows_landed[0], c * LAND + LAND * run * CH)
                nc.scalar.copy(idx[:, 0, :], src_col[:, bass.ds(c, 1), :].rearrange("p c j -> p (c j)")).then_inc(gen_idx, 1)

        bn_scale, bn_shift = sb("bn_scale", [P, 1]), sb("bn_shift", [P, 1])

        def fold_norm(dve, which, layer, var_ready, std_ready, chain, folded):
            n = [0]

            def link(ins):
                n[0] += 1
                ins.then_inc(chain, 1)
                dve.wait_ge(chain, n[0])
            g, b = (bn[:, 2 * which + k, layer:layer + 1] for k in range(2))
            link(nc.vector.bn_aggr(small[:, 0:2], stats[:, 0:NBLK, :].rearrange("p b s -> p (b s)")))
            nc.vector.tensor_scalar(small[:, 2:3], small[:, 1:2], BN_EPS, None, ALU.add).then_inc(var_ready, 1)
            dve.wait_ge(std_ready, 1)
            link(nc.vector.reciprocal(small[:, 4:5], small[:, 3:4]))
            link(nc.vector.tensor_tensor(bn_scale[:, :], small[:, 4:5], g, ALU.mult))
            link(nc.vector.tensor_tensor(small[:, 5:6], small[:, 0:1], bn_scale[:, :], ALU.mult))
            nc.vector.tensor_tensor(bn_shift[:, :], b, small[:, 5:6], ALU.subtract).then_inc(folded, 1)

        def std(act, var_ready, std_ready):
            act.wait_ge(var_ready, 1)
            nc.scalar.activation(small[:, 3:4], small[:, 2:3], ACT.Sqrt).then_inc(std_ready, 1)

        deg_tile = sb("deg_tile", [P, NT])
        deg_out, deg_landed = sem("deg_out"), sem("deg_landed")

        def first_product(layer):
            with phase() as new:
                product, saved = new("product"), new("saved")
                with nc.Block() as block:
                    @block.sync
                    def _(sp):
                        if layer == 0:
                            sp.dma_start(deg_row, acc[0:1, 1, 0:N]).then_inc(deg_out, 16)
                            sp.wait_ge(deg_out, 16)
                            sp.dma_start(deg_tile[0:TILE, :], deg_row.rearrange("o (t p) -> p (o t)", p=TILE),
                                         allow_slow_non_contiguous=True).then_inc(deg_landed, 16)

                    @block.tensor
                    def _(pe):
                        def f(b, s):
                            pe.wait_ge(saved, b + 1)
                            nc.tensor.matmul(bank[s][:, 0:BLK], w0[:, layer, :], fblk(acc[:, 0, :], b),
                                             start=True, stop=True).then_inc(product, 1)
                        blocks(pe, f)

                    @block.scalar
                    def _(act):
                        act.sem_inc(saved, BS)

                        def f(b, s):
                            act.wait_ge(product, b + 1)
                            nc.scalar.copy(fblk(mid, b), bank[s][:, 0:BLK]).then_inc(saved, 1)
                        blocks(act, f)

                    @block.vector
                    def _(dve):
                        def f(b, s):
                            dve.wait_ge(saved, b + BS + 1)
                            nc.vector.bn_stats(stats[:, bass.ds(b, 1), :].rearrange("p b s -> p (b s)"), fblk(mid, b))
                        blocks(dve, f)

        def norm_turn(i, function):
            here = mid[:, bass.ds(i * BS * BLK, BS * BLK)]
            return nc.scalar.activation(here, here, function, bias=bn_shift[:, :], scale=bn_scale[:, :])

        def second_product(layer):
            with phase() as new:
                var_ready, std_ready, chain, folded = new("var_ready"), new("std_ready"), new("chain"), new("folded")
                product, saved, normed, save_go, product_go = (
                    new(n) for n in ("product", "saved", "normed", "save_go", "product_go"))
                with nc.Block() as block:
                    @block.tensor
                    def _(pe):
                        def f(b, s):
                            pe.wait_ge(saved, b + 1)
                            nc.tensor.matmul(bank[s][:, 0:BLK], w1[:, layer, :], fblk(mid, b),
                                             start=True, stop=True).then_inc(product, 1)
                        with pe.Fori(0, BITERS) as i:
                            pe.wait_ge(normed, i + 1)
                            pe.sem_inc(product_go, 1)
                            for s in range(BS):
                                f(i * BS + s, s)

                    @block.scalar
                    def _(act):
                        act.sem_inc(saved, BS)
                        std(act, var_ready, std_ready)
                        act.wait_ge(folded, 1)

                        def save(i):
                            for s in range(BS):
                                act.wait_ge(product, i * BS + s + 1)
                                act.sem_inc(save_go, 1)
                                nc.scalar.copy(fblk(mid, i * BS + s), bank[s][:, 0:BLK]).then_inc(saved, 1)
                        norm_turn(0, ACT.Relu).then_inc(normed, 1)
                        with act.Fori(0, BITERS - 1) as i:
                            norm_turn(i + 1, ACT.Relu).then_inc(normed, 1)
                            save(i)
                        save(BITERS - 1)

                    @block.vector
                    def _(dve):
                        fold_norm(dve, 0, layer, var_ready, std_ready, chain, folded)

                        def f(b, s):
                            dve.wait_ge(saved, b + BS + 1)
                            nc.vector.bn_stats(stats[:, bass.ds(b, 1), :].rearrange("p b s -> p (b s)"), fblk(mid, b))
                        blocks(dve, f)

        def second_norm(layer):
            with phase() as new:
                var_ready, std_ready, chain, folded = new("var_ready"), new("std_ready"), new("chain"), new("folded")
                normed, stats_go = new("normed"), new("stats_go")
                with nc.Block() as block:
                    @block.scalar
                    def _(act):
                        std(act, var_ready, std_ready)
                        act.wait_ge(folded, 1)
                        with act.Fori(0, BITERS) as i:
                            norm_turn(i, ACT.Relu).then_inc(normed, 1)

                    @block.vector
                    def _(dve):
                        fold_norm(dve, 1, layer, var_ready, std_ready, chain, folded)
                        with dve.Fori(0, BITERS) as i:
                            dve.wait_ge(normed, i + 1)
                            dve.sem_inc(stats_go, 1)
                            for s in range(BS):
                                b = i * BS + s
                                nc.vector.bn_stats(stats[:, bass.ds(b, 1), :].rearrange("p b s -> p (b s)"), fblk(mid, b))

        def third_norm(layer):
            with phase() as new:
                var_ready, std_ready, chain, folded = new("var_ready"), new("std_ready"), new("chain"), new("folded")
                normed, kept, turned, saved = (new(n) for n in ("normed", "kept", "turned", "saved"))
                stored = new("stored", BS)
                with nc.Block() as block:
                    @block.scalar
                    def _(act):
                        std(act, var_ready, std_ready)
                        act.wait_ge(folded, 1)

                        def f(b, s):
                            act.wait_ge(kept, b + 1)
                            act.wait_ge(turned, b + 1)
                            nc.scalar.activation(slot_f[:, s, :], fblk(mid, b), ACT.Relu, bias=bn_shift[:, :],
                                                 scale=bn_scale[:, :]).then_inc(normed, 1)
                        blocks(act, f)

                    @block.vector
                    def _(dve):
                        dve.sem_inc(kept, BS)
                        dve.sem_inc(saved, BS)
                        fold_norm(dve, 2, layer, var_ready, std_ready, chain, folded)

                        def f(b, s, i):
                            dve.wait_ge(normed, b + 1)
                            nc.vector.tensor_copy(fblk(acc[:, 0, :], b), slot_f[:, s, :]).then_inc(kept, 1)
                            dve.wait_ge(turned, b + BS + 1)
                            dve.wait_ge(stored[s], i * 16 + 16)
                            nc.vector.tensor_copy(slot_x[0:TILE, s].rearrange("p t d -> p (t d)"),
                                                  bank[s][0:TILE, 0:2 * P]).then_inc(saved, 1)
                        with dve.Fori(0, BITERS) as i:
                            for s in range(BS):
                                f(i * BS + s, s, i)

                    @block.tensor
                    def _(pe):
                        pe.sem_inc(turned, BS)

                        def f(b, s):
                            pe.wait_ge(normed, b + 1)
                            pe.wait_ge(saved, b + 1)
                            for t in range(2):
                                ins = nc.tensor.transpose(bank[s][0:TILE, t * P:(t + 1) * P],
                                                          slot_f[:, s, t * TILE:(t + 1) * TILE], ident[:, :])
                            ins.then_inc(turned, 1)
                        blocks(pe, f)

                    @block.sync
                    def _(sp):
                        store_rows(sp, [(lambda s: slot_x[0:TILE, s], h_rows, saved, stored)])

        def store_rows(sp, steps):
            for _, _, _, stored in steps:
                for s in range(BS):
                    sp.sem_inc(stored[s], 16)
            with sp.Fori(0, BITERS) as i:
                for slot, table, saved, stored in steps:
                    for s in range(BS):
                        sp.wait_ge(saved, i * BS + (BS + s + 1))
                        sp.dma_start(node_rows(table)[:, bass.ds(2 * (i * BS + s), 2), :], slot(s)).then_inc(stored[s], 16)
            for _, _, _, stored in steps:
                for s in range(BS):
                    sp.wait_ge(stored[s], 16 * (BITERS + 1))

        def to_rows(xn):
            with phase() as new:
                var_ready, std_ready, chain, folded = new("var_ready"), new("std_ready"), new("chain"), new("folded")
                made, turned, added, res_landed = new("made"), new("turned"), new("added"), new("res_landed", BS)
                with nc.Block() as block:
                    @block.sync
                    def _(sp):
                        load_residual(sp, x, added, res_landed)

                    @block.scalar
                    def _(act):
                        std(act, var_ready, std_ready)
                        act.wait_ge(folded, 1)

                        def f(b, s):
                            act.wait_ge(turned, b + 1)
                            nc.scalar.activation(slot_f[:, s, :], fblk(mid, b), ACT.Identity, bias=bn_shift[:, :],
                                                 scale=bn_scale[:, :]).then_inc(made, 1)
                        blocks(act, f)

                    @block.tensor
                    def _(pe):
                        pe.sem_inc(turned, BS)

                        def f(b, s):
                            pe.wait_ge(made, b + 1)
                            pe.wait_ge(added, b + 1)
                            for t in range(2):
                                ins = nc.tensor.transpose(bank[s][0:TILE, t * P:(t + 1) * P],
                                                          slot_f[:, s, t * TILE:(t + 1) * TILE], ident[:, :])
                            ins.then_inc(turned, 1)
                        blocks(pe, f)

                    @block.vector
                    def _(dve):
                        dve.sem_inc(added, BS)
                        fold_norm(dve, 2, LAYERS - 1, var_ready, std_ready, chain, folded)
                        with dve.Fori(0, BITERS) as i:
                            for s in range(BS):
                                b = i * BS + s
                                dve.wait_ge(turned, b + BS + 1)
                                dve.wait_ge(res_landed[s], i * 16 + 16)
                                nc.vector.tensor_tensor(xn[0:TILE, bass.ds(2 * b, 2), :],
                                                        bank[s][0:TILE, 0:2 * P].rearrange("p (t d) -> p t d", t=2),
                                                        slot_x[0:TILE, s], ALU.add).then_inc(added, 1)
                                dve.wait_ge(added, b + BS + 1)
                                for t in range(2):
                                    nc.vector.bn_stats(
                                        stats[0:TILE, bass.ds(2 * b + t, 1), :].rearrange("p b s -> p (b s)"),
                                        xn[0:TILE, bass.ds(2 * b + t, 1), :].rearrange("p t d -> p (t d)"))

        def load_residual(sp, table, added, landed):
            with sp.Fori(0, BITERS) as i:
                for s in range(BS):
                    sp.wait_ge(added, i * BS + s + 1)
                    sp.dma_start(slot_x[0:TILE, s], node_rows(table)[:, bass.ds(2 * (i * BS + s), 2), :]
                                 ).then_inc(landed[s], 16)

        mean, rstd, ln_tmp = (sb(n, [P, NT, 1]) for n in ("mean", "rstd", "ln_tmp"))

        def norm_factors(link, n, var_ready):
            even, odd = (stats[0:TILE, 0:n, k:k + 1] for k in (1, 4))
            m, r, t = (v[0:TILE, 0:n] for v in (mean, rstd, ln_tmp))
            link(nc.vector.tensor_tensor(m, even, odd, ALU.add))
            link(nc.vector.tensor_tensor(t, even, odd, ALU.subtract))
            link(nc.vector.tensor_scalar(m, m, 0.5, None, ALU.mult))
            link(nc.vector.tensor_tensor(t, t, t, ALU.mult))
            link(nc.vector.tensor_tensor(r, stats[0:TILE, 0:n, 2:3], stats[0:TILE, 0:n, 5:6], ALU.add))
            link(nc.vector.tensor_scalar(t, t, 0.25, 1e-5, ALU.mult, ALU.add))
            link(nc.vector.tensor_scalar(r, r, 1.0 / P, None, ALU.mult))
            nc.vector.tensor_tensor(t, r, t, ALU.add).then_inc(var_ready, 1)

        TGT = 256

        def layer_norm(xn):
            with phase() as new:
                chain, var_ready, std_ready = new("chain"), new("var_ready"), new("std_ready")
                normed, turned, kept, product, packed = (
                    new(n) for n in ("normed", "turned", "kept", "product", "packed"))
                stored, packed_out = new("stored", BS), new("packed_out", BS)
                with nc.Block() as block:
                    @block.vector
                    def _(dve):
                        n = [0]

                        def link(ins):
                            n[0] += 1
                            ins.then_inc(chain, 1)
                            dve.wait_ge(chain, n[0])
                        norm_factors(link, NT, var_ready)
                        dve.wait_ge(std_ready, 1)
                        link(nc.vector.reciprocal(rstd[0:TILE], rstd[0:TILE]))

                        def f(b, s, i):
                            dve.wait_ge(stored[s], i * 16 + 16)
                            dve.wait_ge(turned, b + 1)
                            for t in range(2):
                                col = lambda v: v[0:TILE, bass.ds(2 * b + t, 1), :].rearrange("p t d -> p (t d)")
                                ins = nc.vector.tensor_scalar(slot_x[0:TILE, s, t, :], col(xn), col(mean), col(rstd),
                                                              ALU.subtract, ALU.mult)
                            ins.then_inc(normed, 1)
                        dve.sem_inc(normed, BS)
                        dve.sem_inc(kept, BS)

                        def keep(b, s):
                            dve.wait_ge(turned, b + BS + 1)
                            dve.wait_ge(product, b + 1)
                            nc.vector.tensor_copy(slot_f[:, s, :], bank[s][:, 0:BLK]).then_inc(kept, 1)
                        with dve.Fori(0, BITERS) as i:
                            for s in range(BS):
                                f(i * BS + s, s, i)
                            for s in range(BS):
                                keep(i * BS + s, s)

                    @block.scalar
                    def _(act):
                        act.wait_ge(var_ready, 1)
                        nc.scalar.activation(rstd[0:TILE], ln_tmp[0:TILE], ACT.Sqrt).then_inc(std_ready, 1)
                        act.sem_inc(packed, BS)

                        def pack(b, s, i):
                            act.wait_ge(product, b + BS + 1)
                            act.wait_ge(packed_out[s], i * 16 + 16)
                            h = bank[5 + s % 3]
                            nc.scalar.copy(slot_n[0:TILE, s].rearrange("p t d -> p (t d)"), h[0:TILE, 0:2 * ROW])
                            nc.scalar.copy(tgt_score[:, bass.ds(b * BLK, BLK)], bank[s][0:HEADS, TGT:TGT + BLK]
                                           ).then_inc(packed, 1)
                        with act.Fori(0, BITERS) as i:
                            for s in range(BS):
                                pack(i * BS + s, s, i)

                    @block.tensor
                    def _(pe):
                        pe.sem_inc(turned, BS)
                        pe.sem_inc(product, BS)

                        def turn(b, s):
                            pe.wait_ge(normed, b + BS + 1)
                            pe.wait_ge(kept, b + 1)
                            pe.wait_ge(packed, b + 1)
                            for t in range(2):
                                ins = nc.tensor.transpose(bank[s][:, t * TILE:(t + 1) * TILE], slot_x[0:TILE, s, t, :],
                                                          ident[0:TILE, 0:TILE])
                            ins.then_inc(turned, 1)

                        def project(b, s):
                            pe.wait_ge(kept, b + BS + 1)
                            pe.wait_ge(packed, b + BS - 1)
                            h = bank[5 + s % 3]
                            for t in range(2):
                                nc.tensor.matmul(h[0:TILE, t * ROW:(t + 1) * ROW], slot_f[:, s, t * TILE:(t + 1) * TILE],
                                                 proj[:, 0:ROW], start=True, stop=True)
                            nc.tensor.matmul(bank[s][0:HEADS, TGT:TGT + BLK], proj[:, ROW:ROW + HEADS], slot_f[:, s, :],
                                             start=True, stop=True).then_inc(product, 1)
                        with pe.Fori(0, BITERS) as i:
                            for s in range(BS):
                                turn(i * BS + s, s)
                            for s in range(BS):
                                project(i * BS + s, s)

                    @block.gpsimd
                    def _(pool):
                        pool.memset(mid[:, :], 0.0)
                        pool.memset(flat[:, NT * P:2 * NP], 0.0)

                    @block.sync
                    def _(sp):
                        store_rows(sp, [(lambda s: slot_x[0:TILE, s], x1_rows, normed, stored),
                                        (lambda s: slot_n[0:TILE, s], att_rows, packed, packed_out)])

        masked = cut(0, 2, CHUNK)
        score = cut(1024, 2, CHUNK)
        rise = cut(2048, 2, CHUNK)
        prob = cut(3072, 2, CHUNK)
        prob_turned = cut(4096, 2, CHUNK)
        z = sb("z", [P, 2, J * HEADS])
        far = sb("far", [P, 2, J, WIN])
        tgt_win = sb("tgt_win", [HEADS, 2, HEADS * WIN])
        slopes = sb("slopes", [HEADS, 2])
        tgt_part = sb("tgt_part", [P, 2, 2])
        top = sb("top", [P, 2, 3])
        diag = sb("diag", [P, 2, 2, WIN])
        fall = sb("fall", [P, WIN])
        diff = sb("diff", [P, 2, 2, WIN])
        fac = sb("fac", [P, 2, 2, WIN])
        old_part, new_part = sb("old_part", [P, 2, WIN]), sb("new_part", [P, 2, WIN])
        att_rel = sb("att_rel", [P, J])
        S_COL, TOP_COL = HEADS * WIN, (HEADS + 1) * WIN

        def attention():
            RUN = LAYERS
            with phase() as new:
                names = ("slopes_set sums_cleared z_done prepped scored tgt_copied lrelued max_go maxed topped exped "
                         "turned saved "
                         "diagonal spread summed_up fell differed factored parts merged gen_idx gen_free "
                         "gen_rel_ready").split()
                (slopes_set, sums_cleared, z_done, prepped, scored, tgt_copied, lrelued, max_go, maxed, topped, exped,
                 turned, saved,
                 diagonal, spread, summed_up, fell, differed, factored, parts, merged, gen_idx, gen_free,
                 gen_rel_ready) = (new(n) for n in names)
                with nc.Block() as block:
                    @block.gpsimd
                    def _(pool):
                        wide = pool.value_load(wide_int[0:1, 0:1], min_val=0, max_val=1)
                        with pool.If(wide < 1):
                            gather(pool, att_rows, ROW, RUN, summed_up, 0)
                        with pool.Else():
                            with pool.Fori(0, CH) as c:
                                pool.wait_ge(gen_idx, c + 1)
                                pool.wait_ge(gen_free, c + 1)
                                pool.sem_inc(pool_go, 1)
                                gather_chunk(pool, 0, att_rows, ROW)

                    @block.vector
                    def _(dve):
                        wide = dve.value_load(wide_int[0:1, 0:1], min_val=0, max_val=1)
                        nc.vector.memset(slopes[:, 0:1], 1.0)
                        nc.vector.memset(slopes[:, 1:2], -0.8).then_inc(slopes_set, 1)
                        nc.vector.memset(flat[:, 0:NT * P], 0.0).then_inc(sums_cleared, 1)
                        dve.wait_ge(sums_cleared, 1)

                        def col(arr, c):
                            return arr[:, bass.ds(c, 1), :].rearrange("p c j -> p (c j)")

                        def own_parts(c, q, u, rel, base, landed, serial=False):
                            d = u % 2
                            if not serial:
                                after(dve, scored, q - 1)
                            nc.vector.tensor_tensor(
                                tgt_win[:, d, :].rearrange("k (h n) -> k h n", n=WIN),
                                bcast(tgt_score[:, bass.ds(base, WIN)], 1, HEADS),
                                bcast(ident[0:HEADS, 0:HEADS], 2, WIN), ALU.mult)
                            nc.vector.tensor_tensor(far[:, d], bcast(iota_win, 1, J), bcast(rel, 2, WIN),
                                                    ALU.not_equal)
                            dve.wait_ge(rows_landed[u], landed)
                            nc.vector.tensor_tensor(z[:, d, :].rearrange("p (j h) -> p j h", h=HEADS),
                                                    rows[:, u, :, P:ROW],
                                                    edge_score[:, bass.ds(c, 1), :].rearrange("p c (j h) -> p (c j) h", h=HEADS),
                                                    ALU.add).then_inc(z_done, 1)

                        def mask(q, u):
                            d = u % 2
                            dve.wait_ge(z_done, q + 1)
                            nc.vector.tensor_tensor(
                                masked[:, d, :].rearrange("p (j h n) -> p j h n", h=HEADS, n=WIN),
                                bcast(far[:, d], 2, HEADS),
                                bcast(z[:, d, :].rearrange("p (j h) -> p j h", h=HEADS), 3, WIN),
                                ALU.subtract).then_inc(prepped, 1)

                        def maximum(q, u):
                            d = u % 2
                            dve.wait_ge(lrelued, q + 1)
                            dve.sem_inc(max_go, 1)
                            nc.vector.tensor_tensor_reduce(out=score[:, d, :], in0=score[:, d, :], in1=rise[:, d, :],
                                                           scale=1.0, scalar=0.0, op0=ALU.add, op1=ALU.max,
                                                           accum_out=top[:, d, 1:2]).then_inc(maxed, 1)

                        def negate(q, u):
                            d = u % 2
                            dve.wait_ge(maxed, q + 1)
                            nc.vector.tensor_scalar(top[:, d, 2:3], top[:, d, 1:2], -1.0, None, ALU.mult).then_inc(topped, 1)

                        def diagonals(q, u, serial=False):
                            d = u % 2
                            dve.wait_ge(exped, q + 1)
                            if not serial:
                                after(dve, spread, q - 1)
                            nc.vector.tensor_tensor(diag[:, d], bcast(node_sel[:, :], 1, 2), bcast(top[:, d, 0:2], 2, WIN),
                                                    ALU.mult).then_inc(diagonal, 1)

                        def chunk_top(u):
                            return bank[4 + u % 2][:, TOP_COL:TOP_COL + WIN]

                        def compare_tops(q, u, base, serial=False):
                            dve.wait_ge(spread, q + 1)
                            if not serial:
                                after(dve, differed, q)
                            nc.vector.tensor_tensor(fall[:, :], mid[:, bass.ds(base, WIN)], chunk_top(u),
                                                    ALU.subtract).then_inc(fell, 1)

                        def raise_top(q, u, base, serial=False):
                            d = u % 2
                            dve.wait_ge(fell, q + 1)
                            if not serial:
                                after(dve, factored, q - 1)
                            nc.vector.tensor_scalar(diff[:, d, 0, :], fall[:, :], 0.0, None, ALU.min)
                            nc.vector.tensor_scalar(diff[:, d, 1, :], fall[:, :], -1.0, 0.0, ALU.mult, ALU.min)
                            run = mid[:, bass.ds(base, WIN)]
                            nc.vector.tensor_tensor(run, run, chunk_top(u), ALU.max).then_inc(differed, 1)

                        def scale_parts(q, u, base, serial=False):
                            d = u % 2
                            dve.wait_ge(factored, q + 1)
                            dve.wait_ge(summed_up, q + 1 if serial else q + (SLOTS + 1))
                            if not serial:
                                after(dve, merged, q)
                            nc.vector.tensor_tensor(old_part[:, :, :], acc[:, :, bass.ds(base, WIN)],
                                                    bcast(fac[:, d, 0, :], 1, 2), ALU.mult)
                            for h in range(HEADS):
                                mine = slice(h * HD, (h + 1) * HD)
                                nc.vector.tensor_tensor(new_part[mine, 0, :], bank[4 + d][mine, h * WIN:(h + 1) * WIN],
                                                        fac[mine, d, 1, :], ALU.mult)
                            nc.vector.tensor_tensor(new_part[:, 1, :], bank[4 + d][:, S_COL:S_COL + WIN], fac[:, d, 1, :],
                                                    ALU.mult).then_inc(parts, 1)

                        def merge(q, base):
                            dve.wait_ge(parts, q + 1)
                            nc.vector.tensor_tensor(acc[:, :, bass.ds(base, WIN)], old_part[:, :, :], new_part[:, :, :],
                                                    ALU.add).then_inc(merged, 1)

                        with dve.If(wide < 1):
                            chunks(dve, [
                                (lambda c, u, t, base: compare_tops(c, u, base), 3),
                                (lambda c, u, t, base: negate(c, u), 2),
                                (lambda c, u, t, base: scale_parts(c, u, base), 4),
                                (lambda c, u, t, base: raise_top(c, u, base), 3),
                                (lambda c, u, t, base: merge(c, base), 4),
                                (lambda c, u, t, base: own_parts(c, c, u, col(dst_rel, c), base, landed_at(RUN, u, t)), 0),
                                (lambda c, u, t, base: diagonals(c, u), 2),
                                (lambda c, u, t, base: mask(c, u), 0),
                                (lambda c, u, t, base: maximum(c, u), 1)], load_bases)
                        with dve.Else():
                            dve.sem_inc(gen_free, 1)
                            with dve.Fori(0, CH) as c:
                                with dve.Fori(0, NWIN) as k:
                                    q = c * NWIN + k
                                    nc.vector.tensor_scalar(att_rel[:, :], col(dst_col, c), win_start[:, bass.ds(k, 1)],
                                                            None, ALU.subtract).then_inc(gen_rel_ready, 1)
                                    dve.wait_ge(gen_rel_ready, q + 1)
                                    own_parts(c, q, 0, att_rel[:, :], k * WIN, c * LAND + LAND * (RUN * CH + 1), serial=True)
                                    mask(q, 0)
                                    maximum(q, 0)
                                    negate(q, 0)
                                    diagonals(q, 0, serial=True)
                                    compare_tops(q, 0, k * WIN, serial=True)
                                    raise_top(q, 0, k * WIN, serial=True)
                                    scale_parts(q, 0, k * WIN, serial=True)
                                    merge(q, k * WIN)
                                    dve.wait_ge(merged, q + 1)
                                dve.sem_inc(gen_free, 1)

                    @block.scalar
                    def _(act):
                        wide = act.value_load(wide_int[0:1, 0:1], min_val=0, max_val=1)

                        def leaky(q, u, serial=False):
                            d = u % 2
                            act.wait_ge(scored, q + 1)
                            nc.scalar.copy(tgt_part[:, d, :], bank[6 + d][:, 0:2]).then_inc(tgt_copied, 1)
                            if not serial:
                                after(act, maxed, q - 1)
                                after(act, exped, q - 1)
                            act.wait_ge(tgt_copied, q + 1)
                            nc.scalar.activation(score[:, d, :], bank[d][:, :], ACT.Identity, bias=tgt_part[:, d, 0:1],
                                                 scale=-MASK)
                            nc.scalar.activation(rise[:, d, :], bank[d][:, :], ACT.Relu, bias=tgt_part[:, d, 1:2],
                                                 scale=0.8 * MASK).then_inc(lrelued, 1)

                        def exp(q, u, serial=False):
                            d = u % 2
                            act.wait_ge(topped, q + 1)
                            if not serial:
                                after(act, turned, q - 1)
                                after(act, diagonal, q - 1)
                            nc.scalar.activation(prob[:, d, :], score[:, d, :], ACT.Exp, bias=top[:, d, 2:3],
                                                 accum_out=top[:, d, 0:1]).then_inc(exped, 1)

                        def save(q, u, serial=False):
                            d = u % 2
                            act.wait_ge(turned, q + 1)
                            if not serial:
                                after(act, summed_up, q + (SLOTS - 1))
                            nc.scalar.copy(prob_turned[:, d, :], bank[2 + d][:, :]).then_inc(saved, 1)

                        def factors(q, u, serial=False):
                            d = u % 2
                            act.wait_ge(differed, q + 1)
                            if not serial:
                                after(act, merged, q - 1)
                            nc.scalar.activation(fac[:, d].rearrange("p k n -> p (k n)"),
                                                 diff[:, d].rearrange("p k n -> p (k n)"), ACT.Exp).then_inc(factored, 1)

                        with act.If(wide < 1):
                            chunks(act, [
                                (lambda c, u, t: save(c, u), 3),
                                (lambda c, u, t: exp(c, u), 2),
                                (lambda c, u, t: leaky(c, u), 1),
                                (lambda c, u, t: factors(c, u), 3),
                                (copy_idx(act, RUN), 0)])
                        with act.Else():
                            act.wait_ge(rows_landed[0], LAND * RUN * CH)
                            with act.Fori(0, CH) as c:
                                act.wait_ge(rows_landed[0], c * LAND + LAND * RUN * CH)
                                nc.scalar.copy(idx[:, 0, :], src_col[:, bass.ds(c, 1), :].rearrange("p c j -> p (c j)")
                                               ).then_inc(gen_idx, 1)
                                with act.Fori(0, NWIN) as k:
                                    q = c * NWIN + k
                                    leaky(q, 0, serial=True)
                                    exp(q, 0, serial=True)
                                    save(q, 0, serial=True)
                                    factors(q, 0, serial=True)

                    @block.tensor
                    def _(pe):
                        wide = pe.value_load(wide_int[0:1, 0:1], min_val=0, max_val=1)
                        pe.wait_ge(slopes_set, 1)

                        def turn_scores(q, u, serial=False):
                            d = u % 2
                            pe.wait_ge(prepped, q + 1)
                            if not serial:
                                after(pe, lrelued, q - 1)
                            nc.tensor.matmul(bank[6 + d][:, 0:2], tgt_win[:, d, :], slopes[:, :], start=True, stop=True)
                            for j in range(J):
                                ins = nc.tensor.transpose(bank[d][:, j * P:(j + 1) * P], masked[:, d, j * P:(j + 1) * P],
                                                          ident[:, :])
                            ins.then_inc(scored, 1)

                        def turn_probs(q, u, serial=False):
                            d = u % 2
                            pe.wait_ge(exped, q + 1)
                            if not serial:
                                after(pe, saved, q - 1)
                            for j in range(J):
                                ins = nc.tensor.transpose(bank[2 + d][:, j * P:(j + 1) * P], prob[:, d, j * P:(j + 1) * P],
                                                          ident[:, :])
                            ins.then_inc(turned, 1)

                        def spread_sums(q, u, serial=False):
                            d = u % 2
                            pe.wait_ge(diagonal, q + 1)
                            if not serial:
                                after(pe, merged, q - 1)
                            nc.tensor.matmul(bank[4 + d][:, S_COL:S_COL + 2 * WIN], head_blk[:, :],
                                             diag[:, d].rearrange("p k n -> p (k n)"), start=True, stop=True
                                             ).then_inc(spread, 1)

                        def sum_up(q, u, serial=False):
                            d = u % 2
                            pe.wait_ge(saved, q + 1)
                            pe.wait_ge(differed, q + 1)
                            for j in range(J):
                                ins = nc.tensor.matmul(bank[4 + d][:, 0:P], rows[:, u, j, 0:P],
                                                       prob_turned[:, d, j * P:(j + 1) * P], start=(j == 0), stop=(j == J - 1))
                            ins.then_inc(summed_up, 1)

                        with pe.If(wide < 1):
                            pe.sem_inc(summed_up, SLOTS)
                            chunks(pe, [(lambda c, u, t: sum_up(c, u), 3),
                                        (lambda c, u, t: turn_probs(c, u), 2),
                                        (lambda c, u, t: spread_sums(c, u), 2),
                                        (lambda c, u, t: turn_scores(c, u), 0)])
                        with pe.Else():
                            with pe.Fori(0, CH * NWIN) as q:
                                turn_scores(q, 0, serial=True)
                                turn_probs(q, 0, serial=True)
                                spread_sums(q, 0, serial=True)
                                sum_up(q, 0, serial=True)

        def attention_rows():
            slot_heads = cut(3900, BS, BLK)
            heads = cut(5150, 2 * BS, 2 * HEADS)
            rest = cut(5230, 2 * BS, HEADS)
            xn = edge_score[:, :, :].rearrange("p c k -> p (c k)")[:, 0:2 * BS * P].rearrange("p (t d) -> p t d", d=P)
            pick = diag[:, :, :, :].rearrange("p a b n -> p (a b n)")[:, 0:4 * HEADS].rearrange("p (k h) -> p k h", k=2)
            T = slice(0, TILE)
            H = 2 * P
            LINKS = 13
            with phase() as new:
                picks_set, picked, heads_saved, turned, added = (
                    new(n) for n in "picks_set picked heads_saved turned added".split())
                res_landed, chain, heads_in, exp_done, var_ready, std_ready = (
                    new("res_landed", BS), *(new(n) for n in "chain heads_in exp_done var_ready std_ready".split()))
                normed, stored, save_go, copy_go = new("normed"), new("stored", BS), new("save_go"), new("copy_go")
                with nc.Block() as block:
                    @block.sync
                    def _(sp):
                        def load(i):
                            for s in range(BS):
                                sp.wait_ge(added, i * BS + s + 1)
                                sp.dma_start(slot_x[T, s], node_rows(x1_rows)[:, bass.ds(2 * (i * BS + s), 2), :]
                                             ).then_inc(res_landed[s], 16)

                        def store(i):
                            for s in range(BS):
                                sp.wait_ge(normed, i * BS + (BS + s + 1))
                                sp.dma_start(node_rows(out)[:, bass.ds(2 * (i * BS + s), 2), :], slot_n[T, s, :, 0:P]
                                             ).then_inc(stored[s], 16)
                        for s in range(BS):
                            sp.sem_inc(stored[s], 16)
                        load(0)
                        with sp.Fori(0, BITERS - 1) as i:
                            load(i + 1)
                            store(i)
                        store(BITERS - 1)
                        for s in range(BS):
                            sp.wait_ge(stored[s], 16 * (BITERS + 1))

                    @block.tensor
                    def _(pe):
                        pe.sem_inc(turned, BS)
                        pe.wait_ge(picks_set, 2)

                        def pick_heads(b, s):
                            pe.wait_ge(heads_saved, b + 1)
                            for k, arr in enumerate((acc[:, 1, :], mid)):
                                ins = nc.tensor.matmul(bank[5 + s % 3][0:2 * HEADS, 0:BLK], pick[:, k, :], fblk(arr, b),
                                                       start=(k == 0), stop=(k == 1))
                            ins.then_inc(picked, 1)

                        def turn(b, s):
                            pe.wait_ge(heads_saved, b + 3)
                            pe.wait_ge(added, b + 1)
                            for t in range(2):
                                nodes = slice(t * TILE, (t + 1) * TILE)
                                nc.tensor.transpose(bank[s][T, t * P:(t + 1) * P], slot_f[:, s, nodes], ident[:, :])
                                ins = nc.tensor.transpose(bank[s][T, H + t * 2 * HEADS:H + (t + 1) * 2 * HEADS],
                                                          slot_heads[0:2 * HEADS, s, nodes],
                                                          ident[0:2 * HEADS, 0:2 * HEADS])
                            ins.then_inc(turned, 1)
                        with pe.Fori(0, BITERS) as i:
                            for s in range(BS):
                                pick_heads(i * BS + s, s)
                            for s in range(BS):
                                turn(i * BS + s, s)

                    @block.scalar
                    def _(act):
                        act.sem_inc(heads_saved, 2)

                        def save(b, s):
                            act.wait_ge(turned, b + 1)
                            act.sem_inc(save_go, 1)
                            nc.scalar.copy(slot_f[:, s, :], fblk(acc[:, 0, :], b))
                            act.wait_ge(picked, b + 1)
                            nc.scalar.copy(slot_heads[0:2 * HEADS, s, :], bank[5 + s % 3][0:2 * HEADS, 0:BLK]
                                           ).then_inc(heads_saved, 1)

                        def exp(i):
                            act.wait_ge(heads_in, i + 1)
                            nc.scalar.activation(rest[T], heads[T, :, HEADS:], ACT.Exp, scale=-1.0).then_inc(exp_done, 1)

                        def root(i):
                            act.wait_ge(var_ready, i + 1)
                            nc.scalar.activation(rstd[T, 0:2 * BS], ln_tmp[T, 0:2 * BS], ACT.Sqrt).then_inc(std_ready, 1)
                        for s in range(BS):
                            save(s, s)
                        with act.Fori(0, BITERS - 1) as i:
                            exp(i)
                            for s in range(BS):
                                save((i + 1) * BS + s, s)
                            root(i)
                        exp(BITERS - 1)
                        root(BITERS - 1)

                    @block.vector
                    def _(dve):
                        nc.vector.memset(pick[:, :, :], 0.0).then_inc(picks_set, 1)
                        dve.wait_ge(picks_set, 1)
                        nc.vector.tensor_copy(pick[:, 0, 0:HEADS], ident[:, 0:P:HD])
                        nc.vector.tensor_copy(pick[:, 1, HEADS:], ident[:, 0:P:HD]).then_inc(picks_set, 1)
                        dve.wait_ge(deg_landed, 16)
                        nc.vector.tensor_scalar(deg_tile[T, :], deg_tile[T, :], -1.0, float(E), ALU.mult,
                                                ALU.add).then_inc(picks_set, 1)
                        dve.wait_ge(picks_set, 3)
                        dve.sem_inc(added, BS)
                        dve.sem_inc(normed, BS)
                        with dve.Fori(0, BITERS) as i:
                            n = [0]

                            def link(ins):
                                n[0] += 1
                                ins.then_inc(chain, 1)
                                dve.wait_ge(chain, i * LINKS + n[0])
                            for s in range(BS):
                                dve.wait_ge(turned, i * BS + (BS + s + 1))
                                dve.sem_inc(copy_go, 1)
                                ins = nc.vector.tensor_copy(heads[T, 2 * s:2 * s + 2, :],
                                                            bank[s][T, H:H + 4 * HEADS].rearrange("p (t k) -> p t k", t=2))
                            ins.then_inc(heads_in, 1)
                            dve.wait_ge(heads_in, i + 1)
                            dve.wait_ge(exp_done, i + 1)
                            link(nc.vector.tensor_tensor(rest[T], rest[T], bcast(
                                deg_tile[T, bass.ds(i * 2 * BS, 2 * BS)], 2, HEADS), ALU.mult))
                            link(nc.vector.tensor_tensor(rest[T], rest[T], heads[T, :, 0:HEADS], ALU.add))
                            link(nc.vector.reciprocal(rest[T], rest[T]))

                            def mine(s):
                                return xn[T, 2 * s:2 * s + 2, :]
                            for s in range(BS):
                                ins = nc.vector.tensor_tensor(
                                    mine(s).rearrange("p t (h k) -> p (t h) k", k=HD),
                                    bank[s][T, 0:2 * P].rearrange("p (q k) -> p q k", k=HD),
                                    bcast(rest[T, 2 * s:2 * s + 2, :].rearrange("p t h -> p (t h)"), 2, HD), ALU.mult)
                            link(ins)
                            for s in range(BS):
                                dve.wait_ge(res_landed[s], i * 16 + 16)
                                nc.vector.tensor_tensor(mine(s), mine(s), slot_x[T, s], ALU.add).then_inc(added, 1)
                            dve.wait_ge(added, i * BS + 2 * BS)
                            for t in range(2 * BS):
                                ins = nc.vector.bn_stats(stats[T, t, :], xn[T, t, :])
                            link(ins)
                            norm_factors(link, 2 * BS, var_ready)
                            dve.wait_ge(std_ready, i + 1)
                            link(nc.vector.reciprocal(rstd[T, 0:2 * BS], rstd[T, 0:2 * BS]))
                            assert n[0] == LINKS
                            for s in range(BS):
                                dve.wait_ge(stored[s], i * 16 + 16)
                                for t in range(2):
                                    k = 2 * s + t
                                    ins = nc.vector.tensor_scalar(slot_n[T, s, t, 0:P], xn[T, k, :], mean[T, k, :],
                                                                  rstd[T, k, :], ALU.subtract, ALU.mult)
                                ins.then_inc(normed, 1)
                            dve.wait_ge(normed, i * BS + 2 * BS)

        for layer in range(LAYERS):
            messages(layer)
            first_product(layer)
            second_product(layer)
            second_norm(layer)
            if layer < LAYERS - 1:
                third_norm(layer)
        xn = flat[:, 0:NT * P].rearrange("p (t d) -> p t d", d=P)
        to_rows(xn)
        layer_norm(xn)
        attention()
        attention_rows()


_INS = ["x", "src", "dst", "edge_attr_64", "edge_weight", "L0_gnn_W0s", "L0_gnn_W1s", "L0_gnn_bn1_g",
        "L0_gnn_bn1_b", "L0_gnn_bn2_g", "L0_gnn_bn2_b", "L0_gnn_bn3_g", "L0_gnn_bn3_b", "L1_gnn_W_node",
        "L1_gnn_W_edge", "L1_gnn_a"]


def kernel(**inputs):
    import concourse.bacc as _bacc
    from concourse.bass_utils import run_bass_kernel_spmd as _run

    nc = _bacc.Bacc("TRN2", target_bir_lowering=False, num_devices=1)
    arrays, args = {}, []
    for name in _INS:
        v = np.ascontiguousarray(inputs[name])
        arrays[f"in_{name}"] = v
        args.append(nc.dram_tensor(f"in_{name}", v.shape, mybir.dt.from_np(v.dtype), kind="ExternalInput").ap())
    out = nc.dram_tensor("out_0", inputs["x"].shape, F32, kind="ExternalOutput").ap()
    gnn_program(nc, *args[:7], args[7:13], *args[13:], out)
    return _run(nc, [arrays], core_ids=[0]).results[0]["out_0"]
```
